# Optimizing a Trainium2 kernel written in Bass

```python
import numpy as np
import jax
import jax.numpy as jnp

def _softmax(x, axis=-1):
    return jax.nn.softmax(x, axis=axis)

def _gelu(x):
    return jax.nn.gelu(x, approximate=True)

def _silu(x):
    return jax.nn.silu(x)

def _sigmoid(x):
    return jax.nn.sigmoid(x)

def _layernorm(x, axis=-1, eps=1e-05):
    m = jnp.mean(x, axis=axis, keepdims=True)
    v = jnp.var(x, axis=axis, keepdims=True)
    return (x - m) / jnp.sqrt(v + eps)

def _scatter_add(tgt, idx, src, axis=0):
    return tgt.at[idx].add(src)

def _segment_sum(src, seg, n):
    return jax.ops.segment_sum(src, seg, n)
kernel_name = 'mk_conv_attn_hybrid_d2_conv_nhwc512_r2_d53e91'

def setup_inputs(seed: int=0):
    np.random.seed(seed)
    _w = jnp.asarray

    def _rec_inputs():
        import jax
        import jax.numpy as jnp
        _gk = jax.random.key(seed)
        x = 7.22e-05 + 1 * jax.random.normal(jax.random.fold_in(_gk, 1), (4, 32, 32, 256), jnp.float32)
        return x
    x = _rec_inputs()

    def _L0_conv_setup():
        import jax, jax.numpy as jnp
        import numpy as np
        B, H, W, C = (4, 32, 32, 256)
        F = C // 8
        key = jax.random.key(seed)
        ks = jax.random.split(key, 9)
        s = 0.05
        return {'x': jax.random.normal(ks[0], (B, H, W, C), dtype=jnp.float32), 'W_theta': jax.random.normal(ks[1], (C, F), dtype=jnp.float32) * s, 'b_theta': jnp.zeros((F,), dtype=jnp.float32), 'W_phi': jax.random.normal(ks[2], (C, F), dtype=jnp.float32) * s, 'b_phi': jnp.zeros((F,), dtype=jnp.float32), 'W_g': jax.random.normal(ks[3], (C, F), dtype=jnp.float32) * s, 'b_g': jnp.zeros((F,), dtype=jnp.float32), 'W_out': jax.random.normal(ks[4], (F, C), dtype=jnp.float32) * s, 'b_out': jnp.zeros((C,), dtype=jnp.float32)}
    _L0_conv_all = _L0_conv_setup()
    _L0_conv_in = {k: v for k, v in _L0_conv_all.items() if k in ('W_theta', 'b_theta', 'W_phi', 'b_phi', 'W_g', 'b_g', 'W_out', 'b_out')}
    del _L0_conv_all

    def _L1_attn_setup():
        import jax, jax.numpy as jnp
        import numpy as np
        DIM = 256
        H = 8
        M = 128
        HD = DIM // H
        ITERS = 6
        SCALE = HD ** (-0.5)

        def _iterative_pinv(A, iters=ITERS):
            m = A.shape[-1]
            I = jnp.eye(m, dtype=A.dtype)
            absA = jnp.abs(A)
            n1 = jnp.max(jnp.sum(absA, axis=-2), axis=-1)[..., None, None]
            ninf = jnp.max(jnp.sum(absA, axis=-1), axis=-1)[..., None, None]
            Ak = jnp.swapaxes(A, -2, -1) / (n1 * ninf)
            for _ in range(iters):
                Ak = Ak @ (2.0 * I - A @ Ak)
            return Ak
        key = jax.random.key(seed)
        k0, k1, k2 = jax.random.split(key, 3)
        x = jax.random.normal(k0, (2, 4096, DIM), jnp.float32)
        w_qkv = jax.random.normal(k1, (3 * DIM, DIM), jnp.float32) * 0.02
        w_out = jax.random.normal(k2, (DIM, DIM), jnp.float32) * 0.02
        b_out = jnp.zeros((DIM,), jnp.float32)
        return {'x': x, 'w_qkv': w_qkv, 'w_out': w_out, 'b_out': b_out}
    _L1_attn_all = _L1_attn_setup()
    _L1_attn_in = {k: v for k, v in _L1_attn_all.items() if k in ('w_qkv', 'w_out', 'b_out')}
    del _L1_attn_all

    def _L1_ffn_setup():
        import jax, jax.numpy as jnp
        import numpy as np
        K = 2
        key = jax.random.key(seed)
        k1, k2, k3, k4 = jax.random.split(key, 4)
        B, L, D, H, E = (8, 512, 256, 512, 16)
        x = jax.random.normal(k1, (B, L, D), dtype=jnp.float32)
        W_gate = jax.random.normal(k2, (D, E), dtype=jnp.float32) * 0.02
        W1 = jax.random.normal(k3, (E, D, H), dtype=jnp.float32) * 0.02
        W2 = jax.random.normal(k4, (E, H, D), dtype=jnp.float32) * 0.02
        return {'x': x, 'W_gate': W_gate, 'W1': W1, 'W2': W2}
    _L1_ffn_all = _L1_ffn_setup()
    _L1_ffn_in = {k: v for k, v in _L1_ffn_all.items() if k in ('W_gate', 'W1', 'W2')}
    del _L1_ffn_all
    return {'x': x, 'L0_conv_W_theta': _L0_conv_in['W_theta'], 'L0_conv_b_theta': _L0_conv_in['b_theta'], 'L0_conv_W_phi': _L0_conv_in['W_phi'], 'L0_conv_b_phi': _L0_conv_in['b_phi'], 'L0_conv_W_g': _L0_conv_in['W_g'], 'L0_conv_b_g': _L0_conv_in['b_g'], 'L0_conv_W_out': _L0_conv_in['W_out'], 'L0_conv_b_out': _L0_conv_in['b_out'], 'L1_attn_w_qkv': _L1_attn_in['w_qkv'], 'L1_attn_w_out': _L1_attn_in['w_out'], 'L1_attn_b_out': _L1_attn_in['b_out'], 'L1_ffn_W_gate': _L1_ffn_in['W_gate'], 'L1_ffn_W1': _L1_ffn_in['W1'], 'L1_ffn_W2': _L1_ffn_in['W2']}

def reference(x, L0_conv_W_theta, L0_conv_b_theta, L0_conv_W_phi, L0_conv_b_phi, L0_conv_W_g, L0_conv_b_g, L0_conv_W_out, L0_conv_b_out, L1_attn_w_qkv, L1_attn_w_out, L1_attn_b_out, L1_ffn_W_gate, L1_ffn_W1, L1_ffn_W2):
    import jax
    import jax.numpy as jnp

    def _L0_conv_ref(x, W_theta, b_theta, W_phi, b_phi, W_g, b_g, W_out, b_out):
        import jax, jax.numpy as jnp
        import numpy as np
        B, H, W, C = (4, 32, 32, 256)
        F = C // 8
        b, h, w, c = x.shape
        n = h * w
        xf = x.reshape(b, n, c)
        theta = xf @ W_theta + b_theta
        phi = xf @ W_phi + b_phi
        g = xf @ W_g + b_g
        scores = jnp.einsum('bnf,bmf->bnm', theta, phi)
        attn = jax.nn.softmax(scores, axis=-1)
        attn_out = jnp.einsum('bnm,bmf->bnf', attn, g)
        out = attn_out @ W_out + b_out
        return x + out.reshape(b, h, w, c)

    def _L1_attn_ref(x, w_qkv, w_out, b_out):
        import jax, jax.numpy as jnp
        import numpy as np
        DIM = 256
        H = 8
        M = 128
        HD = DIM // H
        ITERS = 6
        SCALE = HD ** (-0.5)

        def _iterative_pinv(A, iters=ITERS):
            m = A.shape[-1]
            I = jnp.eye(m, dtype=A.dtype)
            absA = jnp.abs(A)
            n1 = jnp.max(jnp.sum(absA, axis=-2), axis=-1)[..., None, None]
            ninf = jnp.max(jnp.sum(absA, axis=-1), axis=-1)[..., None, None]
            Ak = jnp.swapaxes(A, -2, -1) / (n1 * ninf)
            for _ in range(iters):
                Ak = Ak @ (2.0 * I - A @ Ak)
            return Ak
        B, N, _ = x.shape
        m = min(M, N)
        qkv = x @ w_qkv.T
        q, k, v = jnp.split(qkv, 3, axis=-1)

        def heads(t):
            return t.reshape(B, N, H, HD).transpose(0, 2, 1, 3)
        q = heads(q) * SCALE
        k = heads(k)
        v = heads(v)
        q_l = q.reshape(B, H, m, N // m, HD).mean(axis=3)
        k_l = k.reshape(B, H, m, N // m, HD).mean(axis=3)
        kernel_1 = jax.nn.softmax(jnp.einsum('bhnd,bhmd->bhnm', q, k_l), axis=-1)
        kernel_2 = jax.nn.softmax(jnp.einsum('bhmd,bhld->bhml', q_l, k_l), axis=-1)
        kernel_3 = jax.nn.softmax(jnp.einsum('bhmd,bhnd->bhmn', q_l, k), axis=-1)
        pinv = _iterative_pinv(kernel_2)
        attn = kernel_1 @ (pinv @ (kernel_3 @ v))
        attn = attn.transpose(0, 2, 1, 3).reshape(B, N, H * HD)
        return attn @ w_out.T + b_out

    def _L1_ffn_ref(x, W_gate, W1, W2):
        import jax, jax.numpy as jnp
        import numpy as np
        K = 2
        B, L, D = x.shape
        E = W_gate.shape[1]
        xf = x.reshape(-1, D)
        T = xf.shape[0]
        probs = jax.nn.softmax(xf @ W_gate, axis=-1)
        top_g, top_i = jax.lax.top_k(probs, K)
        gates = jnp.zeros((T, E), dtype=x.dtype).at[jnp.arange(T)[:, None], top_i].set(top_g)

        def step(y, params):
            W1e, W2e, ge = params
            h = jax.nn.gelu(xf @ W1e, approximate=False)
            return (y + ge[:, None] * (h @ W2e), None)
        y0 = jnp.zeros((T, D), dtype=x.dtype)
        y, _ = jax.lax.scan(step, y0, (W1, W2, gates.T))
        return y.reshape(B, L, D)

    def _gn(v, G=32, eps=1e-05):
        B_, H_, W_, C_ = v.shape
        g = v.reshape(B_, H_, W_, G, C_ // G)
        m = jnp.mean(g, axis=(1, 2, 4), keepdims=True)
        s = jnp.var(g, axis=(1, 2, 4), keepdims=True)
        return ((g - m) / jnp.sqrt(s + eps)).reshape(v.shape)

    def _ln_c(v, eps=1e-06):
        m = jnp.mean(v, axis=-1, keepdims=True)
        s = jnp.var(v, axis=-1, keepdims=True)
        return (v - m) / jnp.sqrt(s + eps)

    def _ln_t(v, eps=1e-05):
        m = jnp.mean(v, axis=-1, keepdims=True)
        s = jnp.var(v, axis=-1, keepdims=True)
        return (v - m) / jnp.sqrt(s + eps)

    def _to_tokens(v):
        B_, H_, W_, C_ = v.shape
        return v.reshape(B_, H_ * W_, C_)

    def _from_tokens(t, like):
        return t.reshape(like.shape)
    x = _L0_conv_ref(x, L0_conv_W_theta, L0_conv_b_theta, L0_conv_W_phi, L0_conv_b_phi, L0_conv_W_g, L0_conv_b_g, L0_conv_W_out, L0_conv_b_out)
    t = _to_tokens(x)
    t = t + _L1_attn_ref(_ln_t(t), L1_attn_w_qkv, L1_attn_w_out, L1_attn_b_out)
    t = t + _L1_ffn_ref(_ln_t(t), L1_ffn_W_gate, L1_ffn_W1, L1_ffn_W2)
    x = _from_tokens(t, x)
    return x

_drawn_inputs = setup_inputs


def setup_inputs(seed=0):
    import zlib

    import numpy as np

    out = dict(_drawn_inputs(seed))
    spreads = {'L0_conv_b_theta': (0.0, 0.299),
     'L0_conv_b_phi': (0.0, 0.8),
     'L0_conv_b_g': (0.0, 0.276),
     'L0_conv_b_out': (0.0, 0.1),
     'L1_attn_b_out': (0.0, 0.1)}
    factors = {'L1_attn_w_qkv': 4.739,
     'L1_attn_w_out': 4.992,
     'L1_ffn_W_gate': 5.542,
     'L1_ffn_W1': 5.34,
     'L1_ffn_W2': 5.21}
    for name, (base, spread) in spreads.items():
        noise = np.random.default_rng([zlib.crc32(name.encode()), seed]).standard_normal(out[name].shape)
        drawn = base * np.exp(spread * noise) if base else spread * noise
        out[name] = jnp.asarray(drawn.astype(out[name].dtype))
    for name, factor in factors.items():
        out[name] = (out[name] * factor).astype(out[name].dtype)
    return out
```

```python
from contextlib import ExitStack

import concourse.bass as bass
from concourse import mybir

P = 128
ALU = mybir.AluOpType
ACT = mybir.ActivationFunctionType
AX = mybir.AxisListType
F32 = mybir.dt.float32
BF16 = mybir.dt.bfloat16
I32 = mybir.dt.int32
U32 = mybir.dt.uint32

HEADS = 8
PINV_ITERS = 6
EPS_LN = 1e-5
QUADS = 4


class Chain:

    def __init__(self, sem, per_pass=0):
        self.sem, self.per_pass, self.n = sem, per_pass, 0

    def link(self, eng, ins, i=None):
        self.n += 1
        ins.then_inc(self.sem, 1)
        eng.wait_ge(self.sem, self.n if i is None else i * self.per_pass + self.n)

    def close(self):
        assert self.n == self.per_pass, ("steps of a pass", self.n)


def conv_attn_nystrom_moe_kernel(
    nc, x, w_theta, b_theta, w_phi, b_phi, w_g, b_g, w_out0, b_out0, w_qkv, w_out1, b_out1, w_gate, w1, w2, out,
):
    B, HH, WW, D = x.shape
    N = HH * WW
    T = B * N
    NT = N // P
    TT = T // P
    KC = D // P
    F = w_theta.shape[1]
    HD = D // HEADS
    M = P
    RUN = N // M
    GH = P // HD
    NG = HEADS // GH
    E, _, H = w1.shape
    HC = H // P
    BLOCKS = 2 * T // P + E
    SLOT_ROWS = 2 * T
    HALF = N // 2
    assert F == HD == 32 and GH == NG * 2 == QUADS and HALF == 512 and NT == 8 and KC == 2

    x_rows = x.rearrange("b h w d -> (b h w) d")
    x_dram = x_rows.rearrange("(t p) d -> p t d", p=P)
    out_dram = out.rearrange("b h w d -> (b h w) d").rearrange("(t p) d -> p t d", p=P)
    xn2_dram = nc.dram_tensor("xn2_scratch", (T, D), F32, kind="Internal").ap()
    y_dram = nc.dram_tensor("y_scratch", (SLOT_ROWS, D), F32, kind="Internal").ap()

    with ExitStack() as ctx:
        def sb(name, shape, dt=F32):
            return ctx.enter_context(nc.sbuf_tensor(name, shape, dt))

        def sem(name):
            return ctx.enter_context(nc.semaphore(name))

        PS = ctx.enter_context(nc.psum_tensor("PS", [P, 8, 512], F32))

        ident = sb("ident", [P, P])
        stacked_ident = sb("stacked_ident", [P, HD])
        ones = sb("ones", [P, P])
        lower = sb("lower", [P, P])
        low = sb("low", [P, 5632])
        wT_qkv = low[:, 0:1536].rearrange("p (c n) -> p c n", c=KC)
        wT_out1 = low[:, 1536:2048].rearrange("p (c n) -> p c n", c=KC)
        wt_sb = low[:, 2048:2304].rearrange("p (c n) -> p c n", c=KC)
        wp_sb = low[:, 2304:2560].rearrange("p (c n) -> p c n", c=KC)
        wg_sb = sb("wg_sb", [P, KC, F])
        wo0_sb = low[:, 2560:2816]
        bias_cols = sb("bias_cols", [P, 3])
        bo0 = low[:, 2816:3072]
        bo1 = low[:, 3072:3328]
        wgate_sb = sb("wgate_sb", [P, KC, E])
        t2_all = sb("t2_all", [P, TT, D])
        logits = sb("logits", [P, TT, E])

        arena = sb("arena", [P, 32 * 1024])
        xs = arena[:, 0:2048].rearrange("p (t d) -> p t d", d=D)
        xb = arena[:, 2048:4096].rearrange("p (t d) -> p t d", d=D)
        x1 = arena[:, 4096:6144].rearrange("p (t d) -> p t d", d=D)
        xn = arena[:, 6144:8192].rearrange("p (t d) -> p t d", d=D)
        xT = arena[:, 8192:10240].rearrange("p (c n) -> p c n", c=KC)
        thT = arena[:, 10240:11264]
        phT = arena[:, 11264:12288]
        gT = arena[:, 12288:13312]
        Pm = arena[:, 13312:15360].rearrange("p (b n) -> p b n", b=2)
        PT = arena[:, 15360:17408].rearrange("p (b n) -> p b n", b=2)
        qT = arena[:, 17408:19456].rearrange("p (c n) -> p c n", c=KC)
        kT = arena[:, 19456:21504].rearrange("p (c n) -> p c n", c=KC)
        v = arena[:, 21504:23552].rearrange("p (t d) -> p t d", d=D)
        RM = arena[:, 23552:25600].rearrange("p (g h r m) -> p g h r m", g=NG, h=GH, r=2)
        A = arena[:, 25600:26624].rearrange("p (g n) -> p g n", g=NG)
        AT = arena[:, 26624:27648].rearrange("p (g n) -> p g n", g=NG)
        kl_bd = arena[:, 27648:28672].rearrange("p (g n) -> p g n", g=NG)
        ql_bd = arena[:, 28672:29696].rearrange("p (g n) -> p g n", g=NG)
        misc = low[:, 3328:4352].rearrange("p (a n) -> p a n", a=4)
        g_sb = misc[:, 0, :].rearrange("p (t f) -> p t f", f=F)
        W_sb = misc[:, 1, :].rearrange("p (h d) -> p h d", d=HD)
        U_sb = misc[:, 2, :].rearrange("p (h d) -> p h d", d=HD)
        Y_sb = misc[:, 3, :].rearrange("p (h d) -> p h d", d=HD)
        k_sum = low[:, 4352:4608].rearrange("p (g m) -> p g m", g=NG)
        q_lm = low[:, 4608:4864].rearrange("p (g m) -> p g m", g=NG)
        OT = low[:, 4864:5376].rearrange("p (b n) -> p b n", b=2)
        rs_sb = low[:, 5376:5632]
        neg_max = sb("neg_max", [P, 2, NT])
        row_sum = sb("row_sum", [P, NT])
        row_inv = sb("row_inv", [P, NT])
        small = sb("small", [P, 64])
        stats = sb("stats", [P, 8])
        minus_half = sb("minus_half", [P, 1])
        aggr = sb("aggr", [P, NT, 4])

        BW = BLOCKS + 4
        iota_i = sb("iota_i", [P, 256], I32)
        iota_e = sb("iota_e", [P, E])
        iota_blk = sb("iota_blk", [P, BW])
        iota_lo = sb("iota_lo", [P, P], BF16)
        iota_hi = sb("iota_hi", [P, BLOCKS], BF16)
        row_no = sb("row_no", [P, 2])
        tile_no = sb("tile_no", [P, TT])
        probs = sb("probs", [P, TT, E])
        top = sb("top", [P, TT, 8])
        top_i = sb("top_i", [P, TT, 8], U32)
        pick = sb("pick", [P, 2, TT])
        oh = sb("oh", [P, 2, TT, E])
        route = sb("route", [P, 2, TT * E])
        col_e = sb("col_e", [P, 6, E])
        col_ei = sb("col_ei", [P, E], I32)
        pos = sb("pos", [P, 2, TT])
        pos_i = sb("pos_i", [P, 3, 2, TT], I32)
        pos_lo = sb("pos_lo", [P, 2, TT])
        pos_hi = sb("pos_hi", [P, 2, TT])
        hot_lo = sb("hot_lo", [P, 2, 2, P], BF16)
        hot_hi = sb("hot_hi", [P, 2, 2, 2, BLOCKS], BF16)
        slot = sb("slot", [P, 4, BW])
        slot_i = sb("slot_i", [P, BW], I32)
        token_of = sb("token_of", [P, BW], I32)
        row_of = sb("row_of", [P, BW], I32)
        expert_of = sb("expert_of", [P, BW], I32)
        w1_sb = arena[:, 0:E * KC * H]
        w2_sb = arena[:, E * KC * H:E * (KC * H + HC * D)]
        gather_ix = sb("gather_ix", [P, 4], I32)
        scatter_ix = sb("scatter_ix", [P, 4], I32)
        xg = low[:, 0:1024].rearrange("p (b d) -> p b d", b=4)
        xgT = low[:, 1024:1536].rearrange("p (b c n) -> p b c n", b=2, c=KC)
        hb = low[:, 1536:2560].rearrange("p (b n) -> p b n", b=2)
        hT = low[:, 2560:3584].rearrange("p (b c n) -> p b c n", b=2, c=HC)
        y_sb = low[:, 3584:4608].rearrange("p (b d) -> p b d", b=4)
        y_in = arena[:, 0:2 * TT * D].rearrange("p (c t k d) -> p c t k d", c=8, k=2, d=D)

        consts_ready = sem("consts_ready")
        weights_loaded = sem("weights_loaded")
        raw_w_loaded = sem("raw_w_loaded")
        prep_mm = sem("prep_mm")
        prep_copied = sem("prep_copied")
        padded = sem("padded")
        pool_chain = Chain(sem("pool_chain"))
        dve_chain0 = Chain(sem("dve_chain0"))
        dve_steps = Chain(sem("dve_steps"), 65)
        dve_chain2 = Chain(sem("dve_chain2"))
        x_loaded = sem("x_loaded")
        xb_ready = sem("xb_ready")
        x1b_ready = sem("x1b_ready")
        x1_done = sem("x1_done")
        bulk_mm = sem("bulk_mm")
        bulk_dve = sem("bulk_dve")
        bulk_act = sem("bulk_act")
        gt_mm = sem("gt_mm")
        g_ready = sem("g_ready")
        s_mm = sem("s_mm")
        s_max = sem("s_max")
        s_exp = sem("s_exp")
        t_mm = sem("t_mm")
        t_dve = sem("t_dve")
        t_act = sem("t_act")
        pv_mm = sem("pv_mm")
        ot_ready = sem("ot_ready")
        pr_mm = sem("pr_mm")
        pr_used = sem("pr_used")
        lm_ready = sem("lm_ready")
        pinv_mm = sem("pinv_mm")
        pinv_ev = sem("pinv_ev")
        pinv_in = sem("pinv_in")
        pinv_exp = sem("pinv_exp")
        uy_mm = sem("uy_mm")
        uy_ready = sem("uy_ready")
        gate_mm = sem("gate_mm")
        gate_ready = sem("gate_ready")
        xn_ready = sem("xn_ready")
        x2_done = sem("x2_done")
        xn2_ready = sem("xn2_ready")
        xn2_stored = sem("xn2_stored")
        sample_done = sem("sample_done")

        probs_in = sem("probs_in")
        probs_exp = sem("probs_exp")
        hot_ready = sem("hot_ready")
        rank_mm = sem("rank_mm")
        sel_ready = sem("sel_ready")
        sel_used = sem("sel_used")
        table_mm = sem("table_mm")
        tables_ready = sem("tables_ready")
        experts_loaded = sem("experts_loaded")
        gix = sem("gix")
        six = sem("six")
        xg_loaded = [sem(f"xg_loaded{u}") for u in range(4)]
        y_stored = [sem(f"y_stored{u}") for u in range(4)]
        xt_mm = sem("xt_mm")
        xgT_ready = sem("xgT_ready")
        h_mm = sem("h_mm")
        gelu_done = sem("gelu_done")
        ht_mm = sem("ht_mm")
        hT_ready = sem("hT_ready")
        y_mm = sem("y_mm")
        y_copied = sem("y_copied")
        y_back = [sem(f"y_back{c}") for c in range(8)]
        rows_ready = sem("rows_ready")
        out_stored = sem("out_stored")

        block = ctx.enter_context(nc.Block())

        pieces = [(p, g) for p in ("scores", "transpose", "norms", "start", 0, 1, 2, 3, 4, 5) for g in range(NG)]
        slot_pieces = {h: pieces[3 * h:3 * h + 3] for h in range(7)}
        n_pieces = len(pieces)
        piece_no = {pg: n + 1 for n, pg in enumerate(pieces)}
        BULK = 30
        UNITS = 3 * NT
        S_BANK = (4, 6)
        RAW = 13312

        def s_banks(u):
            return S_BANK[0] if NT <= u < 2 * NT else S_BANK[u % 2]

        passed = {e: sem(f"passed_{e}") for e in ("pool", "pe", "dve", "sp")}

        def apart(eng, name):
            eng.sem_inc(passed[name], 1)

        @block.gpsimd
        def _(pool):
            link = lambda ins: pool_chain.link(pool, ins)
            link(pool.memset(ident[:], 0.0))
            link(pool.affine_select(out=ident[:], in_=ident[:], compare_op=ALU.not_equal, fill=1.0, base=0,
                                    pattern=[[-1, P]], channel_multiplier=1))
            link(pool.memset(stacked_ident[:], 0.0))
            for j in range(QUADS):
                link(pool.affine_select(out=stacked_ident[:], in_=stacked_ident[:], compare_op=ALU.not_equal,
                                        fill=1.0, base=-HD * j, pattern=[[-1, HD]], channel_multiplier=1))
            link(pool.memset(lower[:], 1.0))
            link(pool.affine_select(out=lower[:], in_=lower[:], compare_op=ALU.is_gt, fill=0.0, base=0,
                                    pattern=[[1, P]], channel_multiplier=-1))
            pool.memset(ones[:], 1.0).then_inc(consts_ready, 1)
            link(pool.memset(minus_half[:], -0.5))
            link(pool.iota(iota_i[:, 0:255], pattern=[[1, 255]], base=0, channel_multiplier=0))
            pool.iota(iota_i[:, 255:256], pattern=[[1, 1]], base=0, channel_multiplier=1).then_inc(consts_ready, 1)
            pool.wait_ge(weights_loaded, 16 * 13)
            pool_steps = Chain(sem("pool_steps"), 5 * NT)

            def norm(t, i):
                pool_steps.link(pool, pool.tensor_scalar(aggr[:, t, 2:3], aggr[:, t, 1:2], EPS_LN, None, ALU.add), i)
                pool_steps.link(pool, pool.tensor_tensor(aggr[:, t, 3:4], aggr[:, t, 2:3], minus_half[:], ALU.pow), i)
                apart(pool, "pool")
                return pool.tensor_scalar(xn[:, t, :], x1[:, t, :], aggr[:, t, 0:1], aggr[:, t, 3:4], ALU.subtract, ALU.mult)

            with pool.Fori(0, B) as i:
                pool.wait_ge(x_loaded, (i + 1) * 16)
                pool.tensor_tensor(xb, xs, bo0.unsqueeze(1).broadcast_to([P, NT, D]), ALU.add).then_inc(xb_ready, 1)
                for t in range(NT):
                    pool.wait_ge(x1_done, i * NT + t + 1)
                    apart(pool, "pool")
                    norm(t, i).then_inc(xn_ready, 1)
                    pool.wait_ge(xn_ready, i * NT + t + 1)
                    pool.tensor_tensor(x1[:, t, :], x1[:, t, :], bo1, ALU.add).then_inc(x1b_ready, 1)
                for t in range(NT):
                    pool.wait_ge(x2_done, i * NT + t + 1)
                    apart(pool, "pool")
                    norm(t, i).then_inc(xn2_ready, 1)
                    pool_steps.link(pool, pool.tensor_copy(t2_all[:, bass.ds(i * NT + t, 1), :].rearrange("p o d -> p (o d)"), x1[:, t, :]), i)
                pool_steps.close()
                pool.wait_ge(xn2_ready, (i + 1) * NT)
                pool.dma_start(xn2_dram.rearrange("(b t p) d -> b p t d", p=P, t=NT)[i], xn).then_inc(xn2_stored, 16)
                pool.wait_ge(sample_done, i + 1)
                apart(pool, "pool")

            def gather(n, b):
                pool.tensor_copy(gather_ix[:, b:b + 1], token_of[:, bass.ds(n, 1)]).then_inc(gix, 1)
                pool.wait_ge(gix, n + 1)
                apart(pool, "pool")
                pool.indirect_dma_start(xg[:, b, :], None, xn2_dram,
                                        bass.IndirectOffsetOnAxis(ap=gather_ix[:, b:b + 1], axis=0)).then_inc(xg_loaded[b], 16)

            pool.wait_ge(tables_ready, 1)
            for n in range(3):
                gather(n, n)
            with pool.Fori(0, BLOCKS // 4) as i:
                for u in range(4):
                    pool.wait_ge(xt_mm, i * 4 + u + 1)
                    gather(i * 4 + u + 3, (u + 3) % 4)
                    pool.tensor_copy(scatter_ix[:, u:u + 1], row_of[:, bass.ds(i * 4 + u, 1)]).then_inc(six, 1)
                    pool.wait_ge(six, i * 4 + u + 1)
                    pool.wait_ge(y_copied, i * 4 + u + 3)
                    apart(pool, "pool")
                    pool.indirect_dma_start(y_dram, bass.IndirectOffsetOnAxis(ap=scatter_ix[:, u:u + 1], axis=0),
                                            y_sb[:, u, :], None, bounds_check=SLOT_ROWS - 1,
                                            oob_is_err=False).then_inc(y_stored[u], 16)
            for b in range(3):
                pool.wait_ge(xg_loaded[b], 16 * (BLOCKS // 4 + 1))

        @block.sync
        def _(sp):
            sp.wait_ge(padded, 1)
            c = lambda ap: ap.rearrange("(f o) -> f o", o=1)
            for dst, src in (
                (wt_sb[:, :, 0:F], w_theta.rearrange("(c p) f -> p c f", p=P)),
                (wp_sb[:, :, 0:F], w_phi.rearrange("(c p) f -> p c f", p=P)),
                (wg_sb[:], w_g.rearrange("(c p) f -> p c f", p=P)),
                (bias_cols[0:F, 0:1], c(b_theta)), (bias_cols[0:F, 1:2], c(b_phi)), (bias_cols[0:F, 2:3], c(b_g)),
                *[(wo0_sb[F * j:F * j + F, :], w_out0) for j in range(QUADS)],
                (bo0, b_out0.partition_broadcast(P)), (bo1, b_out1.partition_broadcast(P)),
                (wgate_sb[:], w_gate.rearrange("(c p) e -> p c e", p=P)),
            ):
                sp.dma_start(dst, src).then_inc(weights_loaded, 16)
            sp.dma_start(arena[:, RAW:RAW + 6 * D].rearrange("p (r d) -> p r d", d=D),
                         w_qkv.rearrange("(r p) d -> p r d", p=P)).then_inc(raw_w_loaded, 16)
            sp.dma_start(arena[:, RAW + 6 * D:RAW + 8 * D].rearrange("p (r d) -> p r d", d=D),
                         w_out1.rearrange("(r p) d -> p r d", p=P)).then_inc(raw_w_loaded, 16)
            with sp.Fori(0, B) as i:
                sp.dma_start(xs, x_dram.rearrange("p (b t) d -> b p t d", t=NT)[i]).then_inc(x_loaded, 16)
                sp.wait_ge(x_loaded, (i + 1) * 16)
                sp.wait_ge(bulk_mm, i * BULK + 4)
                sp.wait_ge(xb_ready, i + 1)
                apart(sp, "sp")
            sp.wait_ge(sample_done, B)
            for q in range(4):
                es = slice(q * E // 4, (q + 1) * E // 4)
                sp.dma_start(w1_sb.rearrange("p (e c h) -> p e c h", e=E, c=KC)[:, es],
                             w1.rearrange("e (c p) h -> p e c h", p=P)[:, es]).then_inc(experts_loaded, 16)
                sp.dma_start(w2_sb.rearrange("p (e c d) -> p e c d", e=E, c=HC)[:, es],
                             w2.rearrange("e (c p) d -> p e c d", p=P)[:, es]).then_inc(experts_loaded, 16)
            for u in range(4):
                sp.wait_ge(y_stored[u], 16 * (BLOCKS // 4))
            for c in range(8):
                sp.dma_start(y_in[:, c], y_dram.rearrange("(c t p k) d -> c p t k d", c=8, t=4, k=2)[c]).then_inc(y_back[c], 16)
            for c in range(8):
                sp.wait_ge(rows_ready, c + 1)
                sp.dma_start(out_dram[:, 4 * c:4 * c + 4, :], t2_all[:, 4 * c:4 * c + 4, :]).then_inc(out_stored, 16)
            sp.wait_ge(out_stored, 16 * 8)

        def transposes(pe, dst_bank, srcs):
            for n, s in enumerate(srcs):
                mm = pe.transpose(PS[0:s.shape[1], dst_bank, n * P:n * P + s.shape[0]], s, ident[0:s.shape[0], 0:s.shape[0]])
            return mm

        @block.tensor
        def _(pe):
            pe.wait_ge(consts_ready, 1)
            pe.wait_ge(raw_w_loaded, 32)
            raw = arena[:, RAW:RAW + 8 * D].rearrange("p (r d) -> p r d", d=D)
            for n in range(4):
                srcs = [raw[:, r, c * P:(c + 1) * P] for r in (2 * n, 2 * n + 1) for c in range(KC)]
                transposes(pe, n, srcs).then_inc(prep_mm, 1)
            pe.wait_ge(prep_copied, 4)
            pe.wait_ge(weights_loaded, 16 * 13)

            with pe.Fori(0, B) as i:
                def bulk_free(n):
                    if n >= 8:
                        if (n - 8) % 2 == 0:
                            pe.wait_ge(bulk_dve, i * (BULK // 2) + (n - 8) // 2 + 1)
                        else:
                            pe.wait_ge(bulk_act, i * (BULK // 2) + (n - 8) // 2 + 1)

                def bulk_done(n):
                    pe.wait_ge(bulk_dve, i * (BULK // 2) + n // 2 + 1)
                    pe.wait_ge(bulk_act, i * (BULK // 2) + (n + 1) // 2)

                def turn(n0, src):
                    for u in range(4):
                        bulk_free(n0 + u)
                        srcs = [src[:, 4 * (u // 2) + t, (u % 2) * P:(u % 2 + 1) * P] for t in range(4)]
                        mm = transposes(pe, (n0 + u) % 8, srcs).then_inc(bulk_mm, 1)
                    return mm

                def project(n, w, m, half):
                    bulk_free(n)
                    for c in range(KC):
                        mm = pe.matmul(PS[0:m, n % 8, :], w[c], xT[:, c, half * 512:half * 512 + 512],
                                       start=c == 0, stop=c == KC - 1)
                    mm.then_inc(bulk_mm, 1)

                pe.wait_ge(x_loaded, (i + 1) * 16)
                turn(0, xs)
                bulk_done(3)
                n = 4
                for w, m in ((wt_sb, P), (wp_sb, P), (wg_sb, F)):
                    for half in range(2):
                        project(n, [w[:, c, :] for c in range(KC)], m, half)
                        n += 1
                bulk_done(9)

                def scores(u):
                    b = s_banks(u)
                    last = u - 1 if NT <= u <= 2 * NT else u - 2
                    if last >= 0:
                        pe.wait_ge(s_exp, i * UNITS + last + 1)
                    for k in range(2):
                        if u < NT:
                            ops = thT[:, u * P:(u + 1) * P], phT[:, k * 512:(k + 1) * 512]
                        elif u < 2 * NT:
                            h = u - NT
                            ops = (ql_bd[:, h // GH, (h % GH) * M:(h % GH + 1) * M],
                                   kT[:, h // GH, k * 512:(k + 1) * 512])
                        else:
                            t = u - 2 * NT
                            ops = qT[:, k, t * P:(t + 1) * P], kl_bd[:, k, :]
                        mm = pe.matmul(PS[:, b + k, :], ops[0], ops[1], start=True, stop=True)
                    mm.then_inc(s_mm, 1)

                def turn_probs(u):
                    pe.wait_ge(s_exp, i * UNITS + u + 1)
                    if u >= 1:
                        pe.wait_ge(t_dve, i * UNITS + u)
                        pe.wait_ge(t_act, i * UNITS + u)
                    for k in range(2):
                        mm = transposes(pe, 2 + k, [Pm[:, u % 2, (4 * k + n) * P:(4 * k + n + 1) * P] for n in range(4)])
                    mm.then_inc(t_mm, 1)

                def values(u):
                    pe.wait_ge(t_dve, i * UNITS + u + 1)
                    pe.wait_ge(t_act, i * UNITS + u + 1)
                    if u >= 1:
                        pe.wait_ge(ot_ready, i * UNITS + u)
                    pt = lambda n: PT[:, u % 2, n * P:(n + 1) * P]
                    if u < 2 * NT:
                        for r in range(2):
                            for j in range(QUADS):
                                n = 2 * j + r
                                vals = g_sb[:, n, :] if u < NT else v[:, n, (u - NT) * HD:(u - NT + 1) * HD]
                                mm = pe.matmul(PS[HD * j:HD * j + HD, 0, 0:P], vals, pt(n), start=r == 0, stop=r == 1,
                                               tile_position=(0, HD * j))
                    else:
                        for g in range(NG):
                            for j in range(QUADS):
                                pe.matmul(PS[HD * j:HD * j + HD, 0, g * P:(g + 1) * P], Y_sb[:, g * GH + j, :],
                                          pt(g * GH + j), start=True, stop=True, tile_position=(0, HD * j))
                            for j in range(QUADS):
                                mm = pe.matmul(PS[HD * j:HD * j + HD, 0, 256 + g * P:256 + (g + 1) * P], ones[:, 0:HD],
                                               pt(g * GH + j), start=True, stop=True, tile_position=(0, HD * j))
                    mm.then_inc(pv_mm, 1)

                def finish(u):
                    pe.wait_ge(ot_ready, i * UNITS + u + 1)
                    if u >= 1:
                        pe.wait_ge(pr_used, i * UNITS + u)
                    if u < NT:
                        mm = pe.matmul(PS[:, 1, 0:D], OT[:, u % 2, 0:P], wo0_sb, start=True, stop=True)
                    elif u < 2 * NT:
                        mm = pe.matmul(PS[:, 1, 0:HD], OT[:, u % 2, 0:P], stacked_ident[:], start=True, stop=True)
                    else:
                        for c in range(KC):
                            mm = pe.matmul(PS[:, 1, 0:D], OT[:, u % 2, c * P:(c + 1) * P], wT_out1[:, c, :],
                                           start=c == 0, stop=c == KC - 1)
                    mm.then_inc(pr_mm, 1)

                apart(pe, "pe")
                for t in range(NT):
                    mm = pe.transpose(PS[:, 0, t * F:(t + 1) * F], gT[0:F, t * P:(t + 1) * P], ident[0:F, 0:F])
                mm.then_inc(gt_mm, 1)
                scores(0)
                pe.wait_ge(g_ready, i + 1)
                for s in range(NT + 2):
                    if s + 1 < NT:
                        scores(s + 1)
                    if s < NT:
                        turn_probs(s)
                    if 1 <= s <= NT:
                        values(s - 1)
                    if s >= 2:
                        finish(s - 2)

                pe.wait_ge(xn_ready, (i + 1) * NT)
                turn(10, xn)
                bulk_done(13)
                n = 14
                for r in range(2 * KC):
                    for half in range(2):
                        project(n, [wT_qkv[:, c, r * P:(r + 1) * P] for c in range(KC)], P, half)
                        n += 1
                for n in range(22, 26):
                    bulk_free(n)
                    for t2 in range(2):
                        t = 2 * (n - 22) + t2
                        for c in range(KC):
                            mm = pe.matmul(PS[:, n % 8, t2 * D:(t2 + 1) * D], xT[:, c, t * P:(t + 1) * P],
                                           wT_qkv[:, c, 2 * D:3 * D], start=c == 0, stop=c == KC - 1)
                    mm.then_inc(bulk_mm, 1)
                bulk_done(25)

                def inverse_piece(p, g):
                    k = piece_no[(p, g)]
                    if k > 1:
                        pe.wait_ge(pinv_ev, i * n_pieces + k - 1)
                    if p == "scores":
                        mm = pe.matmul(PS[:, 6, :], q_lm[:, g, :], kl_bd[:, g, :], start=True, stop=True)
                    elif p == "transpose":
                        mm = transposes(pe, 6, [A[:, g, h * M:(h + 1) * M] for h in range(GH)])
                    elif p == "norms":
                        pe.matmul(PS[:, 6, :], ones[:], A[:, g, :], start=True, stop=True)
                        mm = pe.matmul(PS[:, 7, :], ones[:], AT[:, g, :], start=True, stop=True)
                    elif p == "start":
                        for h in range(GH):
                            at = AT[:, g, h * M:(h + 1) * M]
                            mm = pe.matmul(PS[:, 6, h * M:(h + 1) * M], at, at, start=True, stop=True)
                    else:
                        lo, hi = (0, 1) if p == 0 else (1, 2) if p == PINV_ITERS - 1 else (0, 2)
                        for h in range(GH):
                            o = (h % 2) * 2 * M
                            mm = pe.matmul(PS[:, 6 + h // 2, o + lo * M:o + hi * M], RM[:, g, h, 0, :],
                                           RM[:, g, h, lo:hi, :].rearrange("p r m -> p (r m)"), start=True, stop=True)
                    mm.then_inc(pinv_mm, 1)

                pe.wait_ge(lm_ready, i + 1)
                scores(NT)
                for s in range(NT + 2):
                    if s < NT:
                        turn_probs(NT + s)
                    if s + 1 < NT:
                        scores(NT + s + 1)
                    for p, g in slot_pieces.get(s, []):
                        inverse_piece(p, g)
                    if 1 <= s <= NT:
                        values(NT + s - 1)
                    if s >= 2:
                        finish(NT + s - 2)
                pe.wait_ge(pr_used, i * UNITS + 2 * NT)
                pe.wait_ge(pinv_ev, (i + 1) * n_pieces)
                scores(2 * NT)
                for h in range(HEADS):
                    mm = pe.matmul(PS[:, 0, h * HD:(h + 1) * HD], RM[:, h // GH, h % GH, 1, :], W_sb[:, h, :],
                                   start=True, stop=True)
                mm.then_inc(uy_mm, 1)
                pe.wait_ge(uy_ready, 2 * i + 1)
                for h in range(HEADS):
                    mm = pe.matmul(PS[:, 1, h * HD:(h + 1) * HD], A[:, h // GH, (h % GH) * M:(h % GH + 1) * M],
                                   U_sb[:, h, :], start=True, stop=True)
                mm.then_inc(uy_mm, 1)
                pe.wait_ge(uy_ready, 2 * i + 2)
                for s in range(NT + 2):
                    if s + 1 < NT:
                        scores(2 * NT + s + 1)
                    if s < NT:
                        turn_probs(2 * NT + s)
                    if 1 <= s <= NT:
                        values(2 * NT + s - 1)
                    if s >= 2:
                        finish(2 * NT + s - 2)
                pe.wait_ge(xn2_ready, (i + 1) * NT)
                turn(26, xn)
                bulk_done(29)
                for half in range(2):
                    for c in range(KC):
                        mm = pe.matmul(PS[0:E, half, :], wgate_sb[:, c, :], xT[:, c, half * 512:half * 512 + 512],
                                       start=c == 0, stop=c == KC - 1)
                    mm.then_inc(gate_mm, 1)
                pe.wait_ge(gate_ready, i + 1)
                apart(pe, "pe")
                for t in range(NT):
                    mm = pe.transpose(PS[:, 2, t * E:(t + 1) * E], gT[0:E, t * P:(t + 1) * P], ident[0:E, 0:E])
                mm.then_inc(gate_mm, 1)
                pe.wait_ge(sample_done, i + 1)

            pe.wait_ge(hot_ready, 1)
            both = route[:, 0, :]
            pe.matmul(PS[:, 0, :], lower[:], both, start=True, stop=True).then_inc(sel_used, 1)
            pe.matmul(PS[:, 1, :], ones[:], both, start=True, stop=True).then_inc(sel_used, 1)
            pe.matmul(PS[:, 3, 0:P], ident[:], ones[:], start=True, stop=True).then_inc(rank_mm, 1)
            def place(s, b, first):
                pe.wait_ge(sel_ready, s + 1)
                for k in range(2):
                    mm = pe.matmul(PS[:, 2, 0:2 * BLOCKS], hot_lo[:, b, k, :], hot_hi[:, b, k, :, :].rearrange("p a n -> p (a n)"),
                                   start=first and k == 0, stop=False, skip_group_check=True)
                return mm
            place(0, 0, True).then_inc(sel_used, 1)
            place(1, 1, False).then_inc(sel_used, 1)
            with pe.Fori(1, TT // 2) as i:
                for b in range(2):
                    place(2 * i + b, b, False).then_inc(sel_used, 1)
            pe.matmul(PS[:, 3, 0:P], ident[:], ones[:], start=True, stop=True).then_inc(table_mm, 1)

            pe.wait_ge(tables_ready, 1)
            pe.wait_ge(experts_loaded, 16 * 8)

            def turn_rows(b, r, p, m):
                pe.wait_ge(xg_loaded[b], 16 * (r + 1))
                transposes(pe, p, [xg[:, b, c * P:(c + 1) * P] for c in range(KC)]).then_inc(xt_mm, 1)

            def hidden(n, p, e):
                pe.wait_ge(xgT_ready, n + 1)
                for c in range(KC):
                    mm = pe.matmul(PS[:, 2 + p, :], xgT[:, p, c, :], w1_sb[:, bass.ds(e * (KC * H) + c * H, H)],
                                   start=c == 0, stop=c == KC - 1)
                mm.then_inc(h_mm, 1)

            expert = lambda n: pe.value_load(expert_of[0:1, bass.ds(n, 1)], min_val=0, max_val=E - 1)
            pe.transpose(PS[:, 4, 0:P], ident[:], ident[:]).then_inc(ht_mm, 1)
            turn_rows(0, 0, 0, 0)
            turn_rows(1, 0, 1, 1)
            hidden(0, 0, expert(0))
            with pe.Fori(0, BLOCKS // 4) as i:
                for u in range(4):
                    p = u % 2
                    n = i * 4 + u
                    hidden(n + 1, 1 - p, expert(n + 1))
                    pe.wait_ge(gelu_done, n + 1)
                    transposes(pe, 4 + p, [hb[:, p, c * P:(c + 1) * P] for c in range(HC)]).then_inc(ht_mm, 1)
                    turn_rows((u + 2) % 4, i + (u + 2) // 4, p, n + 2)
                    e = expert(n)
                    pe.wait_ge(hT_ready, n + 1)
                    pe.wait_ge(y_copied, n + 1)
                    for c in range(HC):
                        mm = pe.matmul(PS[:, 6 + p, 0:D], hT[:, p, c, :], w2_sb[:, bass.ds(e * (HC * D) + c * D, D)],
                                       start=c == 0, stop=c == HC - 1)
                    mm.then_inc(y_mm, 1)

        @block.scalar
        def _(act):
            act.wait_ge(weights_loaded, 16 * 13)
            with act.Fori(0, B) as i:
                def bulk(n, dst, m=P, bias=0.0, scale=1.0):
                    act.wait_ge(bulk_mm, i * BULK + n + 1)
                    act.activation(dst, PS[0:m, n % 8, :], ACT.Identity, bias=bias, scale=scale).then_inc(bulk_act, 1)

                def exponentials(u):
                    act.wait_ge(s_max, i * UNITS + u + 1)
                    if u >= 2:
                        act.wait_ge(t_mm, i * UNITS + u - 1)
                    src = PS[:, s_banks(u):s_banks(u) + 2, :].rearrange("p b n -> p (b n)")
                    if u < 2 * NT:
                        if u == NT:
                            act.wait_ge(pr_used, i * UNITS + NT)
                        act.activation(Pm[:, u % 2, :], src, ACT.Exp, bias=neg_max[:, u % 2, 0:1],
                                       accum_out=row_sum[:, u % NT:u % NT + 1]).then_inc(s_exp, 1)
                    else:
                        act.activation(Pm[:, u % 2, :], Pm[:, u % 2, :], ACT.Exp).then_inc(s_exp, 1)

                def turned(u):
                    act.wait_ge(t_mm, i * UNITS + u + 1)
                    if u >= 2:
                        act.wait_ge(pv_mm, i * UNITS + u - 1)
                    act.copy(PT[:, u % 2, 512:1024], PS[:, 3, :]).then_inc(t_act, 1)

                bulk(1, xT[:, 1, 0:512])
                bulk(3, xT[:, 1, 512:1024])
                bulk(5, thT[:, 512:1024], bias=bias_cols[:, 0:1])
                bulk(7, phT[:, 512:1024], bias=bias_cols[:, 1:2])
                bulk(9, gT[0:F, 512:1024], m=F, bias=bias_cols[0:F, 2:3])
                exponentials(0)
                for s in range(NT):
                    if s + 1 < NT:
                        exponentials(s + 1)
                    turned(s)
                bulk(11, xT[:, 1, 0:512])
                bulk(13, xT[:, 1, 512:1024])
                for r in range(2 * KC):
                    bulk(15 + 2 * r, (qT if r < KC else kT)[:, r % KC, 512:1024], scale=HD ** -0.5 if r < KC else 1.0)
                for n in (23, 25):
                    t = 2 * (n - 22)
                    bulk(n, v[:, t:t + 2, :].rearrange("p t d -> p (t d)"))
                exponentials(NT)
                for s in range(NT):
                    turned(NT + s)
                    if s + 1 < NT:
                        exponentials(NT + s + 1)
                    for p, g in slot_pieces.get(s, []):
                        if p == "scores":
                            act.wait_ge(pinv_in, i * NG + g + 1)
                            act.activation(A[:, g, :], A[:, g, :], ACT.Exp).then_inc(pinv_exp, 1)
                exponentials(2 * NT)
                for s in range(NT):
                    if s + 1 < NT:
                        exponentials(2 * NT + s + 1)
                    turned(2 * NT + s)
                bulk(27, xT[:, 1, 0:512])
                bulk(29, xT[:, 1, 512:1024])
                act.wait_ge(sample_done, i + 1)

            act.wait_ge(probs_in, 1)
            act.activation(probs[:], probs[:], ACT.Exp).then_inc(probs_exp, 1)
            act.wait_ge(h_mm, 1)
            act.activation(hb[:, 0, :], PS[:, 2, :], ACT.Gelu).then_inc(gelu_done, 1)
            with act.Fori(0, BLOCKS // 4) as i:
                for u in range(4):
                    n = i * 4 + u
                    act.wait_ge(h_mm, n + 2)
                    act.wait_ge(ht_mm, n + 1)
                    act.activation(hb[:, 1 - u % 2, :], PS[:, 3 - u % 2, :], ACT.Gelu).then_inc(gelu_done, 1)

        @block.vector
        def _(dve):
            dve.memset(wt_sb, 0.0)
            dve.memset(bias_cols[:], 0.0)
            dve.memset(wp_sb, 0.0)
            dve_chain0.link(dve, dve.memset(arena[:, 27648:29696], 0.0))
            dve.memset(small[:, 0:1], 0.0).then_inc(padded, 1)
            for n in range(4):
                dve.wait_ge(prep_mm, n + 1)
                for r in (2 * n, 2 * n + 1):
                    src = PS[:, n, (r % 2) * D:(r % 2 + 1) * D].rearrange("p (c m) -> p c m", c=KC)
                    dst = wT_qkv[:, :, r * P:(r + 1) * P] if r < 6 else wT_out1[:, :, (r - 6) * P:(r - 5) * P]
                    cp = dve.tensor_copy(dst, src)
                cp.then_inc(prep_copied, 1)
            dve.wait_ge(weights_loaded, 16 * 13)

            with dve.Fori(0, B) as i:
                link = lambda ins: dve_steps.link(dve, ins, i)

                def bulk(n, dst, m=P, bias=None, scale=None):
                    dve.wait_ge(bulk_mm, i * BULK + n + 1)
                    src = PS[0:m, n % 8, :]
                    if bias is not None:
                        cp = dve.tensor_scalar(dst, src, bias, None, ALU.add)
                    elif scale is not None:
                        cp = dve.tensor_scalar(dst, src, scale, None, ALU.mult)
                    else:
                        cp = dve.tensor_copy(dst, src)
                    cp.then_inc(bulk_dve, 1)

                def maxima(u):
                    dve.wait_ge(s_mm, i * UNITS + u + 1)
                    b = s_banks(u)
                    src = PS[:, b:b + 2, :].rearrange("p b n -> p (b n)")
                    if u < 2 * NT:
                        if u >= 2:
                            dve.wait_ge(s_exp, i * UNITS + u - 1)
                        dve.tensor_reduce(neg_max[:, u % 2, 0:1], src, AX.X, ALU.max, negate=True).then_inc(s_max, 1)
                    else:
                        src = src.rearrange("p (h m) -> p h m", m=M)
                        link(dve.tensor_reduce(neg_max[:, u % 2, :], src, AX.X, ALU.max, negate=True))
                        dve.wait_ge(t_mm, i * UNITS + u - 1)
                        dve.tensor_tensor(Pm[:, u % 2, :].rearrange("p (h m) -> p h m", m=M), src,
                                          neg_max[:, u % 2, :].unsqueeze(2).broadcast_to([P, NT, M]),
                                          ALU.add).then_inc(s_max, 1)

                def turned(u):
                    dve.wait_ge(t_mm, i * UNITS + u + 1)
                    if u >= 2:
                        dve.wait_ge(pv_mm, i * UNITS + u - 1)
                    dve.tensor_copy(PT[:, u % 2, 0:512], PS[:, 2, :]).then_inc(t_dve, 1)

                def out_t(u):
                    dve.wait_ge(pv_mm, i * UNITS + u + 1)
                    if u >= 2:
                        dve.wait_ge(pr_mm, i * UNITS + u - 1)
                    if u < 2 * NT:
                        dve.tensor_copy(OT[:, u % 2, 0:P], PS[:, 0, 0:P]).then_inc(ot_ready, 1)
                    else:
                        link(dve.reciprocal(rs_sb, PS[:, 0, 256:512]))
                        dve.tensor_tensor(OT[:, u % 2, :], PS[:, 0, 0:256], rs_sb, ALU.mult).then_inc(ot_ready, 1)

                def moments(t, done):
                    link(dve.bn_stats(stats[:, 0:6], x1[:, t, :]))
                    apart(dve, "dve")
                    dve.bn_aggr(aggr[:, t, 0:2], stats[:, 0:6]).then_inc(done, 1)

                def rows0(t):
                    u = t
                    link(dve.reciprocal(row_inv[:, t:t + 1], row_sum[:, t:t + 1]))
                    dve.wait_ge(pr_mm, i * UNITS + u + 1)
                    dve.scalar_tensor_tensor(x1[:, t, :], PS[:, 1, 0:D], row_inv[:, t:t + 1], xb[:, t, :],
                                             ALU.mult, ALU.add).then_inc(pr_used, 1)
                    dve.wait_ge(pr_used, i * UNITS + u + 1)
                    moments(t, x1_done)

                def rows1(t):
                    u = 2 * NT + t
                    dve.wait_ge(pr_mm, i * UNITS + u + 1)
                    dve.wait_ge(x1b_ready, i * NT + t + 1)
                    dve.tensor_tensor(x1[:, t, :], PS[:, 1, 0:D], x1[:, t, :], ALU.add).then_inc(pr_used, 1)
                    dve.wait_ge(pr_used, i * UNITS + u + 1)
                    moments(t, x2_done)

                bulk(0, xT[:, 0, 0:512])
                bulk(2, xT[:, 0, 512:1024])
                bulk(4, thT[:, 0:512], bias=bias_cols[:, 0:1])
                bulk(6, phT[:, 0:512], bias=bias_cols[:, 1:2])
                bulk(8, gT[0:F, 0:512], m=F, bias=bias_cols[0:F, 2:3])
                maxima(0)
                dve.wait_ge(gt_mm, i + 1)
                dve.tensor_copy(misc[:, 0, :], PS[:, 0, 0:NT * F]).then_inc(g_ready, 1)
                dve.wait_ge(xb_ready, i + 1)
                for s in range(NT + 2):
                    if s + 1 < NT:
                        maxima(s + 1)
                    if s < NT:
                        turned(s)
                    if 1 <= s <= NT:
                        out_t(s - 1)
                    if s >= 2:
                        rows0(s - 2)

                bulk(10, xT[:, 0, 0:512])
                bulk(12, xT[:, 0, 512:1024])
                for r in range(2 * KC):
                    bulk(14 + 2 * r, (qT if r < KC else kT)[:, r % KC, 0:512], scale=HD ** -0.5 if r < KC else None)
                for n in (22, 24):
                    t = 2 * (n - 22)
                    bulk(n, v[:, t:t + 2, :].rearrange("p t d -> p (t d)"))
                dve.wait_ge(bulk_act, i * (BULK // 2) + 11)
                dve.wait_ge(bulk_dve, i * (BULK // 2) + 11)
                for g in range(NG):
                    dve.tensor_reduce(q_lm[:, g, :], qT[:, g, :].rearrange("p (m r) -> p m r", r=RUN), AX.X, ALU.add)
                    red = dve.tensor_reduce(k_sum[:, g, :], kT[:, g, :].rearrange("p (m r) -> p m r", r=RUN), AX.X, ALU.add)
                link(red)
                for g in range(NG):
                    for j in range(GH):
                        rows = slice(HD * j, HD * j + HD)
                        dve.tensor_scalar(kl_bd[rows, g, j * M:(j + 1) * M], k_sum[rows, g, :], 1.0 / RUN, None, ALU.mult)
                        last = dve.tensor_scalar(ql_bd[rows, g, j * M:(j + 1) * M], q_lm[rows, g, :], 1.0 / RUN, None, ALU.mult)
                link(last)
                dve.tensor_scalar(q_lm, q_lm, 1.0 / RUN, None, ALU.mult).then_inc(lm_ready, 1)

                scale_c = small[:, 8:16]

                def inverse_piece(p, g):
                    k = piece_no[(p, g)]
                    dve.wait_ge(pinv_mm, i * n_pieces + k)
                    heads = lambda ap: ap.rearrange("p (h m) -> p h m", m=M)
                    spread = lambda ap: ap.unsqueeze(2).broadcast_to([P, GH, M])
                    done = lambda ins: ins.then_inc(pinv_ev, 1)
                    col = small[:, 16:20]
                    if p == "scores":
                        link(dve.tensor_reduce(col, heads(PS[:, 6, :]), AX.X, ALU.max, negate=True))
                        dve.tensor_tensor(heads(A[:, g, :]), heads(PS[:, 6, :]), spread(col), ALU.add).then_inc(pinv_in, 1)
                        dve.wait_ge(pinv_exp, i * NG + g + 1)
                        link(dve.tensor_reduce(small[:, 20:24], heads(A[:, g, :]), AX.X, ALU.add))
                        link(dve.reciprocal(small[:, 24:28], small[:, 20:24]))
                        done(dve.tensor_tensor(heads(A[:, g, :]), heads(A[:, g, :]), spread(small[:, 24:28]), ALU.mult))
                    elif p == "transpose":
                        done(dve.tensor_copy(AT[:, g, :], PS[:, 6, :]))
                    elif p == "norms":
                        dve.tensor_reduce(small[:, 28:32], heads(PS[:, 6, :]), AX.X, ALU.max)
                        link(dve.tensor_reduce(small[:, 32:36], heads(PS[:, 7, :]), AX.X, ALU.max))
                        link(dve.tensor_tensor(small[:, 36:40], small[:, 28:32], small[:, 32:36], ALU.mult))
                        done(dve.reciprocal(scale_c[:, g * GH:(g + 1) * GH], small[:, 36:40]))
                    elif p == "start":
                        link(dve.tensor_tensor(RM[:, g, :, 0, :], heads(PS[:, 6, :]), spread(scale_c[:, g * GH:(g + 1) * GH]), ALU.mult))
                        idb = ident[:].unsqueeze(1).broadcast_to([P, GH, M])
                        link(dve.tensor_tensor(RM[:, g, :, 0, :], idb, RM[:, g, :, 0, :], ALU.subtract))
                        done(dve.tensor_tensor(RM[:, g, :, 1, :], idb, RM[:, g, :, 0, :], ALU.add))
                    else:
                        src = PS[:, 6:8, :].rearrange("p b (h r m) -> p (b h) r m", r=2, m=M)
                        if p == PINV_ITERS - 1:
                            done(dve.tensor_tensor(RM[:, g, :, 1, :], src[:, :, 1, :], RM[:, g, :, 1, :], ALU.add))
                        elif p == 0:
                            done(dve.tensor_copy(RM[:, g, :, 0, :], src[:, :, 0, :]))
                        else:
                            dve.tensor_copy(RM[:, g, :, 0, :], src[:, :, 0, :])
                            done(dve.tensor_tensor(RM[:, g, :, 1, :], src[:, :, 1, :], RM[:, g, :, 1, :], ALU.add))

                maxima(NT)
                for s in range(NT + 2):
                    if s < NT:
                        turned(NT + s)
                    if s + 1 < NT:
                        maxima(NT + s + 1)
                    for p, g in slot_pieces.get(s, []):
                        inverse_piece(p, g)
                    if 1 <= s <= NT:
                        out_t(NT + s - 1)
                    if s >= 2:
                        h = s - 2
                        link(dve.reciprocal(row_inv[:, h:h + 1], row_sum[:, h:h + 1]))
                        dve.wait_ge(pr_mm, i * UNITS + NT + h + 1)
                        dve.tensor_scalar(W_sb[:, h, :], PS[:, 1, 0:HD], row_inv[:, h:h + 1], None, ALU.mult).then_inc(pr_used, 1)
                maxima(2 * NT)
                dve.wait_ge(uy_mm, 2 * i + 1)
                dve.tensor_copy(misc[:, 2, :], PS[:, 0, 0:D]).then_inc(uy_ready, 1)
                dve.wait_ge(uy_mm, 2 * i + 2)
                dve.tensor_tensor(Y_sb, PS[:, 1, 0:D].rearrange("p (h d) -> p h d", d=HD),
                                  scale_c.unsqueeze(2).broadcast_to([P, HEADS, HD]), ALU.mult).then_inc(uy_ready, 1)
                for s in range(NT + 2):
                    if s + 1 < NT:
                        maxima(2 * NT + s + 1)
                    if s < NT:
                        turned(2 * NT + s)
                    if 1 <= s <= NT:
                        out_t(2 * NT + s - 1)
                    if s >= 2:
                        rows1(s - 2)
                bulk(26, xT[:, 0, 0:512])
                bulk(28, xT[:, 0, 512:1024])
                dve.wait_ge(gate_mm, 3 * i + 2)
                dve.tensor_copy(gT[0:E, :], PS[0:E, 0:2, :].rearrange("p b n -> p (b n)")).then_inc(gate_ready, 1)
                dve.wait_ge(gate_mm, 3 * i + 3)
                link(dve.tensor_copy(logits[:, bass.ds(i * NT, NT), :].rearrange("p t e -> p (t e)"), PS[:, 2, 0:NT * E]))
                dve.wait_ge(xn2_stored, (i + 1) * 16)
                dve.memset(small[:, 4:5], 0.0).then_inc(sample_done, 1)
                dve_steps.close()

            link = lambda ins: dve_chain2.link(dve, ins)
            spread = lambda ap, n: ap.unsqueeze(2).broadcast_to([ap.shape[0], ap.shape[1], n])
            over_t = lambda ap: ap.unsqueeze(1).broadcast_to([P, TT, E])
            link(dve.tensor_reduce(pick[:, 0, :], logits[:], AX.X, ALU.max, negate=True))
            dve.tensor_tensor(probs[:], logits[:], spread(pick[:, 0, :], E), ALU.add).then_inc(probs_in, 1)
            dve.wait_ge(consts_ready, 2)
            link(dve.tensor_copy(iota_e[:], iota_i[:, 0:E]))
            dve.tensor_scalar(iota_blk[:], iota_i[:, 0:BW], float(P), None, ALU.mult)
            dve.tensor_copy(iota_lo[:], iota_i[:, 0:P])
            dve.tensor_copy(iota_hi[:], iota_i[:, 0:BLOCKS])
            dve.tensor_copy(tile_no[:], iota_i[:, 0:TT])
            for k in range(2):
                dve.tensor_scalar(row_no[:, k:k + 1], iota_i[:, 255:256], 2.0, float(k + 1), ALU.mult, ALU.add)
            dve.wait_ge(probs_exp, 1)
            link(dve.tensor_reduce(pos_lo[:, 0, :], probs[:], AX.X, ALU.add))
            link(dve.reciprocal(pos_lo[:, 1, :], pos_lo[:, 0, :]))
            link(dve.tensor_tensor(probs[:], probs[:], spread(pos_lo[:, 1, :], E), ALU.mult))
            for t in range(TT):
                ins = dve.max(out=top[:, t, :], in_=probs[:, t, :])
            link(ins)
            for t in range(TT):
                ins = dve.max_index(out=top_i[:, t, :], in_max=top[:, t, :], in_values=probs[:, t, :])
            link(ins)
            for k in range(2):
                ins = dve.tensor_copy(pick[:, k, :], top_i[:, :, k])
            link(ins)
            for k in range(2):
                ins = dve.tensor_tensor(oh[:, k], over_t(iota_e[:]), spread(pick[:, k, :], E), ALU.is_equal)
            link(ins)
            flat = lambda ap: ap.rearrange("p t e -> p (t e)")
            dve.tensor_tensor(route[:, 0, :], flat(oh[:, 0]), flat(oh[:, 1]), ALU.add).then_inc(hot_ready, 1)
            dve.wait_ge(rank_mm, 1)
            total, run = probs[:].rearrange("p t e -> p (t e)"), route[:, 1, :]
            by_e = lambda ap: ap.rearrange("p (e t) -> p e t", e=E)
            link(dve.tensor_copy(by_e(total), PS[:, 1, :].rearrange("p (t e) -> p e t", e=E)))
            dve.memset(route[:, 0, :], 0.0)
            link(dve.memset(col_e[:, 5, :], 0.0))
            link(dve.tensor_tensor_scan(run, total, route[:, 0, :], 0.0, ALU.add, ALU.add))
            link(dve.tensor_tensor(total, run, total, ALU.subtract))
            first, last = by_e(total)[:, :, 0], by_e(run)[:, :, TT - 1]
            link(dve.tensor_tensor(col_e[:, 0, :], last, first, ALU.subtract))
            link(dve.tensor_scalar(col_ei[:], col_e[:, 0, :], float(P - 1), None, ALU.add))
            link(dve.tensor_scalar(col_ei[:], col_ei[:], 7, 7, ALU.logical_shift_right, ALU.logical_shift_left))
            link(dve.tensor_copy(col_e[:, 1, :], col_ei[:]))
            link(dve.tensor_tensor_scan(col_e[:, 2, :], col_e[:, 1, :], col_e[:, 5, :], 0.0, ALU.add, ALU.add))
            link(dve.tensor_tensor(col_e[:, 3, :], col_e[:, 2, :], col_e[:, 1, :], ALU.subtract))
            link(dve.tensor_tensor(col_e[:, 4, :], col_e[:, 3, :], first, ALU.subtract))
            link(dve.tensor_tensor(by_e(total), by_e(total), spread(col_e[:, 4, :], TT), ALU.add))
            link(dve.tensor_tensor(run.rearrange("p (t e) -> p t e", e=E), PS[:, 0, :].rearrange("p (t e) -> p t e", e=E),
                                   by_e(total).rearrange("p e t -> p t e"), ALU.add))
            for k in range(2):
                ins = dve.tensor_tensor(flat(oh[:, k]), flat(oh[:, k]), run, ALU.mult)
            link(ins)
            link(dve.tensor_reduce(pos[:].rearrange("p k t -> p (k t)"), oh[:].rearrange("p k t e -> p (k t) e"), AX.X, ALU.add))
            link(dve.tensor_copy(pos_i[:, 0], pos[:]))
            dve.tensor_scalar(pos_i[:, 1], pos_i[:, 0], P - 1, None, ALU.bitwise_and)
            link(dve.tensor_scalar(pos_i[:, 2], pos_i[:, 0], 7, None, ALU.logical_shift_right))
            dve.tensor_copy(pos_lo[:], pos_i[:, 1])
            link(dve.tensor_copy(pos_hi[:], pos_i[:, 2]))
            ends = probs[:].rearrange("p t e -> p (t e)")

            def select(s, t, b):
                dve.wait_ge(sel_used, s + 1)
                for k in range(2):
                    lo, hi = pos_lo[:, k, bass.ds(t, 1)], pos_hi[:, k, bass.ds(t, 1)]
                    dve.tensor_scalar(hot_lo[:, b, k, :], iota_lo[:], lo, None, ALU.is_equal)
                    dve.tensor_scalar(hot_hi[:, b, k, 0, :], iota_hi[:], hi, row_no[:, k:k + 1], ALU.is_equal, ALU.mult)
                    ins = dve.tensor_scalar(hot_hi[:, b, k, 1, :], iota_hi[:], hi, tile_no[:, bass.ds(t, 1)], ALU.is_equal, ALU.mult)
                ins.then_inc(sel_ready, 1)
            with dve.Fori(0, TT // 2) as i:
                for b in range(2):
                    select(2 * i + b, 2 * i + b, b)
            link(dve.memset(slot[:, 2, :], 0.0))
            for e in range(E):
                link(dve.scalar_tensor_tensor(slot[:, 2, :], iota_blk[:], col_e[:, 2, e:e + 1], slot[:, 2, :], ALU.is_ge, ALU.add))
            dve.tensor_scalar(expert_of[:], slot[:, 2, :], float(E - 1), None, ALU.min)
            link(dve.memset(slot[:, 0, :], 0.0))
            dve.wait_ge(table_mm, 1)
            link(dve.tensor_copy(slot[:, 1, 0:BLOCKS], PS[:, 2, 0:BLOCKS]))
            link(dve.scalar_tensor_tensor(slot[:, 0, 0:BLOCKS], PS[:, 2, BLOCKS:2 * BLOCKS], 256.0, slot[:, 1, 0:BLOCKS], ALU.mult, ALU.add))
            link(dve.tensor_scalar(slot[:, 1, :], slot[:, 0, :], 0.0, float(4 * SLOT_ROWS), ALU.is_equal, ALU.mult))
            dve.scalar_tensor_tensor(row_of[:], slot[:, 0, :], -1.0, slot[:, 1, :], ALU.add, ALU.add)
            link(dve.tensor_scalar(slot_i[:], slot[:, 0, :], -1.0, 0.0, ALU.add, ALU.max))
            link(dve.tensor_scalar(token_of[:], slot_i[:], 1, None, ALU.logical_shift_right))
            for u in range(2):
                dve.memset(small[:, 44 + u:45 + u], 0.0).then_inc(y_copied, 1)
            dve.memset(small[:, 46:47], 0.0).then_inc(tables_ready, 1)

            def rows_turned(n, p):
                dve.wait_ge(xt_mm, n + 1)
                dve.tensor_copy(xgT[:, p].rearrange("p c n -> p (c n)"), PS[:, p, 0:D]).then_inc(xgT_ready, 1)
            rows_turned(0, 0)
            rows_turned(1, 1)

            def expert_copies(i, u, again):
                n, p = i * 4 + u, u % 2
                dve.wait_ge(ht_mm, n + 2)
                dve.tensor_copy(hT[:, p].rearrange("p c n -> p (c n)"), PS[:, 4 + p, :]).then_inc(hT_ready, 1)
                dve.wait_ge(h_mm, n + 1)
                rows_turned(n + 2, p)
                dve.wait_ge(y_mm, n + 1)
                if again:
                    dve.wait_ge(y_stored[u], i * 16)
                dve.tensor_copy(y_sb[:, u, :], PS[:, 6 + p, 0:D]).then_inc(y_copied, 1)

            for u in range(4):
                expert_copies(0, u, False)
            with dve.Fori(1, BLOCKS // 4) as i:
                for u in range(4):
                    expert_copies(i, u, True)
            for c in range(8):
                dve.wait_ge(y_back[c], 16)
                for k in range(2):
                    for t in range(4):
                        tt = 4 * c + t
                        ins = dve.scalar_tensor_tensor(t2_all[:, tt, :], y_in[:, c, t, k, :], top[:, tt, k:k + 1], t2_all[:, tt, :],
                                                       ALU.mult, ALU.add)
                    if k == 0:
                        link(ins)
                ins.then_inc(rows_ready, 1)


_INS = ['x', 'L0_conv_W_theta', 'L0_conv_b_theta', 'L0_conv_W_phi', 'L0_conv_b_phi', 'L0_conv_W_g', 'L0_conv_b_g',
        'L0_conv_W_out', 'L0_conv_b_out', 'L1_attn_w_qkv', 'L1_attn_w_out', 'L1_attn_b_out', 'L1_ffn_W_gate',
        'L1_ffn_W1', 'L1_ffn_W2']
_OUTS = [((4, 32, 32, 256), 'float32')]


def kernel(**inputs):
    import numpy as _np
    import concourse.bacc as _bacc
    from concourse import mybir as _mybir
    from concourse.bass_utils import run_bass_kernel_spmd as _run

    nc = _bacc.Bacc("TRN2", target_bir_lowering=False, num_devices=1)
    arrays, args = {}, []
    for name in _INS:
        a = _np.ascontiguousarray(inputs[name])
        arrays[f"in_{name}_dram"] = a
        args.append(nc.dram_tensor(f"in_{name}_dram", a.shape, _mybir.dt.from_np(a.dtype), kind="ExternalInput").ap())
    for i, (shape, dtype) in enumerate(_OUTS):
        dt = _mybir.dt.from_np(_np.dtype(dtype))
        args.append(nc.dram_tensor(f"out_{i}_dram", shape, dt, kind="ExternalOutput").ap())
    conv_attn_nystrom_moe_kernel(nc, *args)
    r = _run(nc, [arrays], core_ids=[0])
    return r.results[0]["out_0_dram"]
```

```python
from contextlib import ExitStack

import concourse.bass as bass
from concourse import mybir

P = 128
ALU = mybir.AluOpType
ACT = mybir.ActivationFunctionType
AX = mybir.AxisListType
F32 = mybir.dt.float32
BF16 = mybir.dt.bfloat16
I32 = mybir.dt.int32
U32 = mybir.dt.uint32

HEADS = 8
PINV_ITERS = 6
EPS_LN = 1e-5
QUADS = 4


class Chain:

    def __init__(self, sem, per_pass=0):
        self.sem, self.per_pass, self.n = sem, per_pass, 0

    def link(self, eng, ins, i=None):
        self.n += 1
        ins.then_inc(self.sem, 1)
        eng.wait_ge(self.sem, self.n if i is None else i * self.per_pass + self.n)

    def close(self):
        assert self.n == self.per_pass, ("steps of a pass", self.n)


def conv_attn_nystrom_moe_kernel(
    nc, x, w_theta, b_theta, w_phi, b_phi, w_g, b_g, w_out0, b_out0, w_qkv, w_out1, b_out1, w_gate, w1, w2, out,
):
    B, HH, WW, D = x.shape
    N = HH * WW
    T = B * N
    NT = N // P
    TT = T // P
    KC = D // P
    F = w_theta.shape[1]
    HD = D // HEADS
    M = P
    RUN = N // M
    GH = P // HD
    NG = HEADS // GH
    E, _, H = w1.shape
    HC = H // P
    BLOCKS = 2 * T // P + E
    SLOT_ROWS = 2 * T
    HALF = N // 2
    assert F == HD == 32 and GH == NG * 2 == QUADS and HALF == 512 and NT == 8 and KC == 2

    x_rows = x.rearrange("b h w d -> (b h w) d")
    x_dram = x_rows.rearrange("(t p) d -> p t d", p=P)
    out_dram = out.rearrange("b h w d -> (b h w) d").rearrange("(t p) d -> p t d", p=P)
    xn2_dram = nc.dram_tensor("xn2_scratch", (T, D), F32, kind="Internal").ap()
    y_dram = nc.dram_tensor("y_scratch", (SLOT_ROWS, D), F32, kind="Internal").ap()

    with ExitStack() as ctx:
        def sb(name, shape, dt=F32):
            return ctx.enter_context(nc.sbuf_tensor(name, shape, dt))

        def sem(name):
            return ctx.enter_context(nc.semaphore(name))

        PS = ctx.enter_context(nc.psum_tensor("PS", [P, 8, 512], F32))

        ident = sb("ident", [P, P])
        stacked_ident = sb("stacked_ident", [P, HD])
        ones = sb("ones", [P, P])
        lower = sb("lower", [P, P])
        low = sb("low", [P, 5632])
        wT_qkv = low[:, 0:1536].rearrange("p (c n) -> p c n", c=KC)
        wT_out1 = low[:, 1536:2048].rearrange("p (c n) -> p c n", c=KC)
        w_tpg = low[:, 2048:2240].rearrange("p (c n) -> p c n", c=KC)
        xm = low[:, 2304:2560].rearrange("p (c m) -> p c m", c=KC)
        wo0_sb = low[:, 2560:2816]
        bias_col = sb("bias_col", [P, 1])
        bo0 = low[:, 2816:3072]
        bo1 = low[:, 3072:3328]
        wgate_sb = sb("wgate_sb", [P, KC, E])
        t2_all = sb("t2_all", [P, TT, D])
        logits = sb("logits", [P, TT, E])

        arena = sb("arena", [P, 32 * 1024])
        xs = arena[:, 0:2048].rearrange("p (t d) -> p t d", d=D)
        xb = arena[:, 2048:4096].rearrange("p (t d) -> p t d", d=D)
        x1 = arena[:, 4096:6144].rearrange("p (t d) -> p t d", d=D)
        xn = arena[:, 6144:8192].rearrange("p (t d) -> p t d", d=D)
        xT = arena[:, 8192:10240].rearrange("p (c n) -> p c n", c=KC)
        thT = arena[:, 10240:11264]
        phT = arena[:, 11264:12288]
        gT = arena[:, 12288:13312]
        Pm = arena[:, 13312:15360].rearrange("p (b n) -> p b n", b=2)
        PT = arena[:, 15360:17408].rearrange("p (b n) -> p b n", b=2)
        qT = arena[:, 17408:19456].rearrange("p (c n) -> p c n", c=KC)
        kT = arena[:, 19456:21504].rearrange("p (c n) -> p c n", c=KC)
        v = arena[:, 21504:23552].rearrange("p (t d) -> p t d", d=D)
        RX = arena[:, 23552:25600].rearrange("p (g h r m) -> p g h r m", g=NG, h=GH, r=2)
        AT = arena[:, 26624:27648].rearrange("p (g n) -> p g n", g=NG)
        kl_bd = arena[:, 27648:28672].rearrange("p (g n) -> p g n", g=NG)
        ql_bd = arena[:, 28672:29696].rearrange("p (g n) -> p g n", g=NG)
        misc = low[:, 3328:4352].rearrange("p (a n) -> p a n", a=4)
        g_sb = misc[:, 0, :].rearrange("p (t f) -> p t f", f=F)
        W_sb = misc[:, 1, :].rearrange("p (h d) -> p h d", d=HD)
        U_sb = misc[:, 2, :].rearrange("p (h d) -> p h d", d=HD)
        Y_sb = misc[:, 3, :].rearrange("p (h d) -> p h d", d=HD)
        q_lm = low[:, 4608:4864].rearrange("p (g m) -> p g m", g=NG)
        OT = low[:, 4864:5376].rearrange("p (b n) -> p b n", b=2)
        inv_wide = arena[:, 29696:30208].rearrange("p (b d) -> p b d", b=2)
        inv_T = arena[:, 30208:30720].rearrange("p (b d) -> p b d", b=2)
        head_sum = sb("head_sum", [P, 2, HEADS])
        head_inv = sb("head_inv", [P, HEADS])
        neg_max = sb("neg_max", [P, 2, NT])
        row_sum = sb("row_sum", [P, NT])
        row_inv = sb("row_inv", [P, NT])
        small = sb("small", [P, 64])
        stats = sb("stats", [P, 8])
        minus_half = sb("minus_half", [P, 1])
        aggr = sb("aggr", [P, NT, 4])

        BW = BLOCKS + 4
        iota_i = sb("iota_i", [P, 256], I32)
        iota_e = sb("iota_e", [P, E])
        iota_blk = sb("iota_blk", [P, BW])
        iota_lo = sb("iota_lo", [P, P], BF16)
        iota_hi = sb("iota_hi", [P, BLOCKS], BF16)
        row_no = sb("row_no", [P, 2])
        tile_no = sb("tile_no", [P, TT])
        probs = low[:, 0:512].rearrange("p (t e) -> p t e", e=E)
        top = sb("top", [P, TT, 8])
        top_i = sb("top_i", [P, TT, 8], U32)
        pick = sb("pick", [P, 2, TT])
        oh = low[:, 512:1536].rearrange("p (k t e) -> p k t e", k=2, e=E)
        route = low[:, 1536:2560].rearrange("p (a n) -> p a n", a=2)
        col_e = sb("col_e", [P, 6, E])
        col_ei = sb("col_ei", [P, E], I32)
        pos = sb("pos", [P, 2, TT])
        pos_i = sb("pos_i", [P, 3, 2, TT], I32)
        pos_lo = sb("pos_lo", [P, 2, TT])
        pos_hi = sb("pos_hi", [P, 2, TT])
        hot_lo = sb("hot_lo", [P, 2, 2, P], BF16)
        hot_hi = sb("hot_hi", [P, 2, 2, 2, BLOCKS], BF16)
        slot = sb("slot", [P, 4, BW])
        slot_i = sb("slot_i", [P, BW], I32)
        token_of = sb("token_of", [P, BW], I32)
        row_of = sb("row_of", [P, BW], I32)
        expert_of = sb("expert_of", [P, BW], I32)
        w1_sb = arena[:, 0:E * KC * H]
        w2_sb = arena[:, E * KC * H:E * (KC * H + HC * D)]
        gather_ix = sb("gather_ix", [P, 4], I32)
        scatter_ix = sb("scatter_ix", [P, 4], I32)
        xg = low[:, 0:1024].rearrange("p (b d) -> p b d", b=4)
        xgT = low[:, 1024:1536].rearrange("p (b c n) -> p b c n", b=2, c=KC)
        hb = low[:, 1536:2560].rearrange("p (b n) -> p b n", b=2)
        hT = low[:, 2560:3584].rearrange("p (b c n) -> p b c n", b=2, c=HC)
        y_sb = low[:, 3584:4608].rearrange("p (b d) -> p b d", b=4)
        y_in = arena[:, 0:2 * TT * D].rearrange("p (c t k d) -> p c t k d", c=8, k=2, d=D)

        consts_ready = sem("consts_ready")
        weights_loaded = sem("weights_loaded")
        raw_w_loaded = sem("raw_w_loaded")
        prep_mm = sem("prep_mm")
        prep_copied = sem("prep_copied")
        padded = sem("padded")
        pool_chain = Chain(sem("pool_chain"))
        dve_chain0 = Chain(sem("dve_chain0"))
        dve_steps = Chain(sem("dve_steps"), 53)
        dve_chain2 = Chain(sem("dve_chain2"))
        x_loaded = sem("x_loaded")
        xb_ready = sem("xb_ready")
        x1b_ready = sem("x1b_ready")
        x1_done = sem("x1_done")
        bulk_mm = sem("bulk_mm")
        bulk_dve = sem("bulk_dve")
        bulk_act = sem("bulk_act")
        gt_mm = sem("gt_mm")
        g_ready = sem("g_ready")
        s_mm = sem("s_mm")
        s_max = sem("s_max")
        s_exp = sem("s_exp")
        t_mm = sem("t_mm")
        t_dve = sem("t_dve")
        t_act = sem("t_act")
        pv_mm = sem("pv_mm")
        ot_ready = sem("ot_ready")
        pr_mm = sem("pr_mm")
        pr_used = sem("pr_used")
        lm_ready = sem("lm_ready")
        pinv_mm = sem("pinv_mm")
        pinv_ev = sem("pinv_ev")
        pinv_in = sem("pinv_in")
        pinv_exp = sem("pinv_exp")
        xm_ready = sem("xm_ready")
        lm_mm = sem("lm_mm")
        inv_ready = sem("inv_ready")
        inv_mm = sem("inv_mm")
        inv_copied = sem("inv_copied")
        y_head_mm = sem("y_head_mm")
        y_head_ready = sem("y_head_ready")
        gate_mm = sem("gate_mm")
        gate_ready = sem("gate_ready")
        xn_ready = sem("xn_ready")
        x2_done = sem("x2_done")
        xn_free = sem("xn_free")
        dev_ready = sem("dev_ready")
        dev2_ready = sem("dev2_ready")
        xn2_ready = sem("xn2_ready")
        xn2_stored = sem("xn2_stored")
        sample_done = sem("sample_done")

        probs_in = sem("probs_in")
        probs_exp = sem("probs_exp")
        hot_ready = sem("hot_ready")
        rank_mm = sem("rank_mm")
        sel_ready = sem("sel_ready")
        sel_used = sem("sel_used")
        table_mm = sem("table_mm")
        tables_ready = sem("tables_ready")
        experts_loaded = sem("experts_loaded")
        gix = sem("gix")
        six = sem("six")
        xg_loaded = [sem(f"xg_loaded{u}") for u in range(4)]
        y_stored = [sem(f"y_stored{u}") for u in range(4)]
        xt_mm = sem("xt_mm")
        xgT_ready = sem("xgT_ready")
        h_mm = sem("h_mm")
        gelu_done = sem("gelu_done")
        ht_mm = sem("ht_mm")
        hT_ready = sem("hT_ready")
        y_mm = sem("y_mm")
        y_copied = sem("y_copied")
        y_back = [sem(f"y_back{c}") for c in range(8)]
        rows_ready = sem("rows_ready")
        out_stored = sem("out_stored")

        block = ctx.enter_context(nc.Block())

        pieces = [(p, g, None) for p in ("scores", "transpose", "norm 1", "norm inf", "start") for g in range(NG)]
        pieces += [(k, g, pair) for k in range(PINV_ITERS - 1) for g in range(NG) for pair in range(2)]
        pieces += [(PINV_ITERS - 1, g, None) for g in range(NG)]
        n_pieces = len(pieces)
        assert n_pieces == 4 * NT
        slot_pieces = {h: pieces[4 * h:4 * h + 4] for h in range(NT)}
        piece_no = {pg: n + 1 for n, pg in enumerate(pieces)}
        BULK = 26
        UNIT_BANK = [0, 1, 2, 3, 4, 5, 6, 7, 4, 5, 2, 3, 6, 7, 0, 1, 4, 5, 2, 3, 0, 1, 6, 7, 4, 5]
        UNIT_PREV = {12: 6, 13: 7, 16: 8, 17: 9, 18: 10, 19: 11, 20: 14, 21: 15}
        UNITS = 3 * NT
        S_BANK = (4, 6)
        RAW = 13312

        def s_banks(u):
            return S_BANK[u % 2]

        passed = {e: sem(f"passed_{e}") for e in ("pool", "pe", "dve", "sp")}

        def apart(eng, name):
            eng.sem_inc(passed[name], 1)

        @block.gpsimd
        def _(pool):
            link = lambda ins: pool_chain.link(pool, ins)
            link(pool.memset(ident[:], 0.0))
            link(pool.affine_select(out=ident[:], in_=ident[:], compare_op=ALU.not_equal, fill=1.0, base=0,
                                    pattern=[[-1, P]], channel_multiplier=1))
            link(pool.memset(stacked_ident[:], 0.0))
            for j in range(QUADS):
                link(pool.affine_select(out=stacked_ident[:], in_=stacked_ident[:], compare_op=ALU.not_equal,
                                        fill=1.0, base=-HD * j, pattern=[[-1, HD]], channel_multiplier=1))
            link(pool.memset(lower[:], 1.0))
            link(pool.affine_select(out=lower[:], in_=lower[:], compare_op=ALU.is_gt, fill=0.0, base=0,
                                    pattern=[[1, P]], channel_multiplier=-1))
            pool.memset(ones[:], 1.0).then_inc(consts_ready, 1)
            link(pool.memset(minus_half[:], -0.5))
            link(pool.iota(iota_i[:, 0:255], pattern=[[1, 255]], base=0, channel_multiplier=0))
            pool.iota(iota_i[:, 255:256], pattern=[[1, 1]], base=0, channel_multiplier=1).then_inc(consts_ready, 1)
            pool.wait_ge(weights_loaded, 16 * 13)
            pool.sem_inc(xn_free, 1)
            pool_steps = Chain(sem("pool_steps"), 2 * NT)

            def deviation(t, i):
                pool_steps.link(pool, pool.tensor_scalar(aggr[:, t, 2:3], aggr[:, t, 1:2], EPS_LN, None, ALU.add), i)
                return pool.tensor_tensor(aggr[:, t, 3:4], aggr[:, t, 2:3], minus_half[:], ALU.pow)

            with pool.Fori(0, B) as i:
                pool.wait_ge(x_loaded, (i + 1) * 16)
                pool.tensor_tensor(xb, xs, bo0.unsqueeze(1).broadcast_to([P, NT, D]), ALU.add).then_inc(xb_ready, 1)
                for t in range(NT + 1):
                    if t < NT:
                        pool.wait_ge(x1_done, i * NT + t + 1)
                        apart(pool, "pool")
                        deviation(t, i).then_inc(dev_ready, 1)
                    if t >= 1:
                        pool.wait_ge(xn_ready, i * NT + t)
                        pool.tensor_tensor(x1[:, t - 1, :], x1[:, t - 1, :], bo1, ALU.add).then_inc(x1b_ready, 1)
                for t in range(NT):
                    pool.wait_ge(x2_done, i * NT + t + 1)
                    apart(pool, "pool")
                    deviation(t, i).then_inc(dev2_ready, 1)
                pool_steps.close()
                pool.wait_ge(xn2_ready, (i + 1) * NT)
                pool.dma_start(xn2_dram.rearrange("(b t p) d -> b p t d", p=P, t=NT)[i], xn).then_inc(xn2_stored, 16)
                pool.wait_ge(xn2_stored, (i + 1) * 16)
                pool.sem_inc(xn_free, 1)

            def gather(n, b):
                pool.tensor_copy(gather_ix[:, b:b + 1], token_of[:, bass.ds(n, 1)]).then_inc(gix, 1)
                pool.wait_ge(gix, n + 1)
                apart(pool, "pool")
                pool.indirect_dma_start(xg[:, b, :], None, xn2_dram,
                                        bass.IndirectOffsetOnAxis(ap=gather_ix[:, b:b + 1], axis=0)).then_inc(xg_loaded[b], 16)

            pool.wait_ge(tables_ready, 1)
            for n in range(3):
                gather(n, n)
            with pool.Fori(0, BLOCKS // 4) as i:
                for u in range(4):
                    pool.wait_ge(xt_mm, i * 4 + u + 1)
                    gather(i * 4 + u + 3, (u + 3) % 4)
                    pool.tensor_copy(scatter_ix[:, u:u + 1], row_of[:, bass.ds(i * 4 + u, 1)]).then_inc(six, 1)
                    pool.wait_ge(six, i * 4 + u + 1)
                    pool.wait_ge(y_copied, i * 4 + u + 3)
                    apart(pool, "pool")
                    pool.indirect_dma_start(y_dram, bass.IndirectOffsetOnAxis(ap=scatter_ix[:, u:u + 1], axis=0),
                                            y_sb[:, u, :], None, bounds_check=SLOT_ROWS - 1,
                                            oob_is_err=False).then_inc(y_stored[u], 16)
            for b in range(3):
                pool.wait_ge(xg_loaded[b], 16 * (BLOCKS // 4 + 1))

        @block.sync
        def _(sp):
            sp.wait_ge(padded, 1)
            c = lambda ap: ap.rearrange("(f o) -> f o", o=1)
            for dst, src in (
                *[(w_tpg[:, :, F * k:F * k + F], w.rearrange("(c p) f -> p c f", p=P)) for k, w in enumerate((w_theta, w_phi, w_g))],
                *[(bias_col[F * k:F * k + F, :], c(b)) for k, b in enumerate((b_theta, b_phi, b_g))],
                *[(wo0_sb[F * j:F * j + F, :], w_out0) for j in range(QUADS)],
                (bo0, b_out0.partition_broadcast(P)), (bo1, b_out1.partition_broadcast(P)),
                (wgate_sb[:], w_gate.rearrange("(c p) e -> p c e", p=P)),
            ):
                sp.dma_start(dst, src).then_inc(weights_loaded, 16)
            sp.dma_start(arena[:, RAW:RAW + 6 * D].rearrange("p (r d) -> p r d", d=D),
                         w_qkv.rearrange("(r p) d -> p r d", p=P)).then_inc(raw_w_loaded, 16)
            sp.dma_start(arena[:, RAW + 6 * D:RAW + 8 * D].rearrange("p (r d) -> p r d", d=D),
                         w_out1.rearrange("(r p) d -> p r d", p=P)).then_inc(raw_w_loaded, 16)
            with sp.Fori(0, B) as i:
                sp.dma_start(xs, x_dram.rearrange("p (b t) d -> b p t d", t=NT)[i]).then_inc(x_loaded, 16)
                sp.wait_ge(x_loaded, (i + 1) * 16)
                sp.wait_ge(bulk_mm, i * BULK + 4)
                sp.wait_ge(xb_ready, i + 1)
                apart(sp, "sp")
            sp.wait_ge(sample_done, B)
            sp.wait_ge(xn2_stored, 16 * B)
            for e in range(E):
                sp.dma_start(w1_sb.rearrange("p (e c h) -> p e c h", e=E, c=KC)[:, e],
                             w1.rearrange("e (c p) h -> p e c h", p=P)[:, e]).then_inc(experts_loaded, 16)
                sp.dma_start(w2_sb.rearrange("p (e c d) -> p e c d", e=E, c=HC)[:, e],
                             w2.rearrange("e (c p) d -> p e c d", p=P)[:, e]).then_inc(experts_loaded, 16)
                sp.wait_ge(experts_loaded, 32 * (e + 1))
            for u in range(4):
                sp.wait_ge(y_stored[u], 16 * (BLOCKS // 4))
            for c in range(8):
                sp.dma_start(y_in[:, c], y_dram.rearrange("(c t p k) d -> c p t k d", c=8, t=4, k=2)[c]).then_inc(y_back[c], 16)
            for c in range(8):
                sp.wait_ge(rows_ready, c + 1)
                sp.dma_start(out_dram[:, 4 * c:4 * c + 4, :], t2_all[:, 4 * c:4 * c + 4, :]).then_inc(out_stored, 16)
            sp.wait_ge(out_stored, 16 * 8)

        def transposes(pe, dst_bank, srcs):
            for n, s in enumerate(srcs):
                mm = pe.transpose(PS[0:s.shape[1], dst_bank, n * P:n * P + s.shape[0]], s, ident[0:s.shape[0], 0:s.shape[0]])
            return mm

        @block.tensor
        def _(pe):
            pe.wait_ge(consts_ready, 1)
            pe.wait_ge(raw_w_loaded, 32)
            raw = arena[:, RAW:RAW + 8 * D].rearrange("p (r d) -> p r d", d=D)
            for n in range(4):
                srcs = [raw[:, r, c * P:(c + 1) * P] for r in (2 * n, 2 * n + 1) for c in range(KC)]
                transposes(pe, n, srcs).then_inc(prep_mm, 1)
            pe.wait_ge(prep_copied, 4)
            pe.wait_ge(weights_loaded, 16 * 13)

            with pe.Fori(0, B) as i:
                def bulk_free(n):
                    if n in UNIT_PREV:
                        last = UNIT_PREV[n]
                        pe.wait_ge(bulk_act if last % 2 else bulk_dve, i * (BULK // 2) + last // 2 + 1)

                def bulk_done(n):
                    pe.wait_ge(bulk_dve, i * (BULK // 2) + n // 2 + 1)
                    pe.wait_ge(bulk_act, i * (BULK // 2) + (n + 1) // 2)

                def turn(n, src, half):
                    for c in range(KC):
                        bulk_free(n + c)
                        srcs = [src[:, 4 * half + t, c * P:(c + 1) * P] for t in range(4)]
                        transposes(pe, UNIT_BANK[n + c], srcs).then_inc(bulk_mm, 1)

                def project(n, w, m, half):
                    bulk_free(n)
                    for c in range(KC):
                        mm = pe.matmul(PS[0:m, UNIT_BANK[n], :], w[c], xT[:, c, half * 512:half * 512 + 512],
                                       start=c == 0, stop=c == KC - 1)
                    mm.then_inc(bulk_mm, 1)

                pe.wait_ge(x_loaded, (i + 1) * 16)
                turn(0, xs, 0)
                turn(2, xs, 1)
                bulk_done(3)
                for half in range(2):
                    project(4 + half, [w_tpg[:, c, :] for c in range(KC)], 3 * F, half)
                bulk_done(5)

                def scores(u, k):
                    b = s_banks(u)
                    if k == 0 and u >= 2:
                        pe.wait_ge(s_exp, i * UNITS + u - 1)
                    if u < NT:
                        ops = thT[:, u * P:(u + 1) * P], phT[:, k * 512:(k + 1) * 512]
                    elif u < 2 * NT:
                        h = u - NT
                        ops = (ql_bd[:, h // GH, (h % GH) * M:(h % GH + 1) * M],
                               kT[:, h // GH, k * 512:(k + 1) * 512])
                    else:
                        t = u - 2 * NT
                        ops = qT[:, k, t * P:(t + 1) * P], kl_bd[:, k, :]
                    mm = pe.matmul(PS[:, b + k, :], ops[0], ops[1], start=True, stop=True)
                    if k == 1:
                        mm.then_inc(s_mm, 1)

                def copied(u):
                    pe.wait_ge(t_act, i * UNITS + u + 1)
                    if u >= 2 * NT:
                        pe.wait_ge(t_dve, i * NT + u - 2 * NT + 1)

                def turn_probs(u, k):
                    if k == 0:
                        pe.wait_ge(s_exp, i * UNITS + u + 1)
                        if u >= 1:
                            copied(u - 1)
                    mm = transposes(pe, 2 + k, [Pm[:, u % 2, (4 * k + n) * P:(4 * k + n + 1) * P] for n in range(4)])
                    if k == 1:
                        mm.then_inc(t_mm, 1)

                def turn_inverses(t):
                    pe.wait_ge(inv_ready, i * NT + t + 1)
                    if t >= 2:
                        pe.wait_ge(ot_ready, i * UNITS + 2 * NT + t - 1)
                    transposes(pe, 0, [inv_wide[:, t % 2, g * P:(g + 1) * P] for g in range(NG)]).then_inc(inv_mm, 1)

                def values(u):
                    copied(u)
                    if u >= 1:
                        pe.wait_ge(ot_ready, i * UNITS + u)
                    if u >= NT and u < 2 * NT and u - NT >= 1:
                        pe.wait_ge(pr_used, i * UNITS + u)
                    if u >= 2 * NT:
                        pe.wait_ge(inv_copied, i * NT + min(u - 2 * NT + 2, NT))
                    pt = lambda n: PT[:, u % 2, n * P:(n + 1) * P]
                    if u < 2 * NT:
                        for r in range(2):
                            for j in range(QUADS):
                                n = 2 * j + r
                                vals = g_sb[:, n, :] if u < NT else v[:, n, (u - NT) * HD:(u - NT + 1) * HD]
                                mm = pe.matmul(PS[HD * j:HD * j + HD, 0, 0:P], vals, pt(n), start=r == 0, stop=r == 1,
                                               tile_position=(0, HD * j))
                    else:
                        for g in range(NG):
                            for j in range(QUADS):
                                mm = pe.matmul(PS[HD * j:HD * j + HD, 0, 256 + g * P:256 + (g + 1) * P], Y_sb[:, g * GH + j, :],
                                               pt(g * GH + j), start=True, stop=True, tile_position=(0, HD * j))
                    mm.then_inc(pv_mm, 1)

                def finish(u):
                    pe.wait_ge(ot_ready, i * UNITS + u + 1)
                    if u >= 1:
                        pe.wait_ge(pr_used, i * UNITS + u)
                    if u < NT:
                        mm = pe.matmul(PS[:, 1, 0:D], OT[:, u % 2, 0:P], wo0_sb, start=True, stop=True)
                    elif u < 2 * NT:
                        mm = pe.matmul(PS[:, 0, 256:256 + HD], OT[:, u % 2, 0:P], stacked_ident[:], start=True, stop=True)
                    else:
                        for c in range(KC):
                            mm = pe.matmul(PS[:, 1, 0:D], OT[:, u % 2, c * P:(c + 1) * P], wT_out1[:, c, :],
                                           start=c == 0, stop=c == KC - 1)
                    mm.then_inc(pr_mm, 1)

                def qk(n, r, half):
                    project(n, [wT_qkv[:, c, r * P:(r + 1) * P] for c in range(KC)], P, half)

                apart(pe, "pe")
                for t in range(NT):
                    mm = pe.transpose(PS[:, 0, t * F:(t + 1) * F], gT[0:F, t * P:(t + 1) * P], ident[0:F, 0:F])
                mm.then_inc(gt_mm, 1)
                for u in range(2):
                    for k in range(2):
                        scores(u, k)
                pe.wait_ge(g_ready, i + 1)
                for s in range(NT + 2):
                    for k in range(2):
                        if s < NT:
                            turn_probs(s, k)
                    for k in range(2):
                        if s + 2 < NT:
                            scores(s + 2, k)
                    if 1 <= s <= NT:
                        values(s - 1)
                    if s >= 2:
                        finish(s - 2)
                    if s == NT - 1:
                        pe.wait_ge(xn_ready, i * NT + NT // 2)
                        turn(6, xn, 0)
                    if s == NT:
                        bulk_done(7)
                        for r in range(2):
                            qk(8 + r, r, 0)

                copied(NT - 1)
                for r in range(2, 2 * KC):
                    qk(8 + r, r, 0)
                pe.wait_ge(xn_ready, (i + 1) * NT)
                turn(12, xn, 1)
                bulk_done(13)
                pe.wait_ge(ot_ready, i * UNITS + NT)
                for r in range(2 * KC):
                    qk(14 + r, r, 1)
                pe.wait_ge(xm_ready, i + 1)
                for r in range(2 * KC):
                    for c in range(KC):
                        mm = pe.matmul(PS[:, 6, r * M:(r + 1) * M], wT_qkv[:, c, r * P:(r + 1) * P], xm[:, c, :],
                                       start=c == 0, stop=c == KC - 1)
                mm.then_inc(lm_mm, 1)

                def value_rows(n):
                    bulk_free(n)
                    for t2 in range(2):
                        t = 2 * (n - 18) + t2
                        for c in range(KC):
                            mm = pe.matmul(PS[:, UNIT_BANK[n], t2 * D:(t2 + 1) * D], xT[:, c, t * P:(t + 1) * P],
                                           wT_qkv[:, c, 2 * D:3 * D], start=c == 0, stop=c == KC - 1)
                    mm.then_inc(bulk_mm, 1)

                value_rows(18)
                value_rows(19)
                bulk_done(17)
                pe.wait_ge(lm_ready, i + 1)
                for u in range(2):
                    for k in range(2):
                        scores(NT + u, k)
                value_rows(20)
                value_rows(21)
                bulk_done(21)

                def inverse_piece(p, g, pair):
                    k = piece_no[(p, g, pair)]
                    if k > 1:
                        pe.wait_ge(pinv_ev, i * n_pieces + k - 1)
                    bank = PS[:, 1, :]
                    if p == "scores":
                        mm = pe.matmul(bank, q_lm[:, g, :], kl_bd[:, g, :], start=True, stop=True)
                    elif p == "transpose":
                        mm = transposes(pe, 1, [RX[:, g, h, 1, :] for h in range(GH)])
                    elif p == "norm 1":
                        mm = pe.matmul(bank, ones[:], RX[:, g, :, 1, :], start=True, stop=True)
                    elif p == "norm inf":
                        mm = pe.matmul(bank, ones[:], AT[:, g, :], start=True, stop=True)
                    elif p == "start":
                        for h in range(GH):
                            at = AT[:, g, h * M:(h + 1) * M]
                            mm = pe.matmul(bank[:, h * M:(h + 1) * M], at, at, start=True, stop=True)
                    elif p < PINV_ITERS - 1:
                        for h in (2 * pair, 2 * pair + 1):
                            o = (h % 2) * 2 * M
                            mm = pe.matmul(bank[:, o:o + 2 * M], RX[:, g, h, 0, :], RX[:, g, h].rearrange("p r m -> p (r m)"),
                                           start=True, stop=True)
                    else:
                        for h in range(GH):
                            mm = pe.matmul(bank[:, h * M:(h + 1) * M], RX[:, g, h, 0, :], RX[:, g, h, 1, :], start=True, stop=True)
                    mm.then_inc(pinv_mm, 1)

                for s in range(NT + 1):
                    mine = slot_pieces.get(s, [])
                    if s >= 2:
                        finish(NT + s - 2)
                    for k in range(2):
                        if s < NT:
                            turn_probs(NT + s, k)
                    for k in range(2):
                        if s < NT:
                            inverse_piece(*mine[k])
                            scores(NT + s + 2, k)
                    if s < NT:
                        inverse_piece(*mine[2])
                    if 1 <= s <= NT:
                        values(NT + s - 1)
                    if s < NT:
                        inverse_piece(*mine[3])
                def head_values(hs):
                    pe.wait_ge(pr_used, i * UNITS + NT + hs[-1] + 1)
                    for h in hs:
                        mm = pe.matmul(PS[:, 1, h * HD:(h + 1) * HD], RX[:, h // GH, h % GH, 1, :], W_sb[:, h, :],
                                       start=True, stop=True)
                    return mm
                pe.wait_ge(pinv_ev, (i + 1) * n_pieces)
                head_values(range(HEADS - 2))
                finish(2 * NT - 1)
                for s in range(NT + 2):
                    for k in range(2):
                        if s < NT:
                            turn_probs(2 * NT + s, k)
                    if s == 0:
                        head_values(range(HEADS - 2, HEADS)).then_inc(y_head_mm, 1)
                    for k in range(2):
                        if s + 2 < NT:
                            scores(2 * NT + s + 2, k)
                        if k == 0 and s < NT:
                            turn_inverses(s)
                    if s == 0:
                        pe.wait_ge(y_head_ready, i + 1)
                    if 1 <= s <= NT:
                        values(2 * NT + s - 1)
                    if s >= 2:
                        finish(2 * NT + s - 2)
                    if s == NT - 1:
                        pe.wait_ge(xn2_ready, i * NT + NT // 2)
                        turn(22, xn, 0)
                pe.wait_ge(xn2_ready, (i + 1) * NT)
                turn(24, xn, 1)
                bulk_done(25)
                for half in range(2):
                    for c in range(KC):
                        mm = pe.matmul(PS[0:E, 2 + half, :], wgate_sb[:, c, :], xT[:, c, half * 512:half * 512 + 512],
                                       start=c == 0, stop=c == KC - 1)
                    mm.then_inc(gate_mm, 1)
                pe.wait_ge(gate_ready, i + 1)
                apart(pe, "pe")
                for t in range(NT):
                    mm = pe.transpose(PS[:, 7, t * E:(t + 1) * E], gT[0:E, t * P:(t + 1) * P], ident[0:E, 0:E])
                mm.then_inc(gate_mm, 1)

            pe.wait_ge(hot_ready, 1)
            both = route[:, 0, :]
            pe.matmul(PS[:, 0, :], lower[:], both, start=True, stop=True).then_inc(sel_used, 1)
            pe.matmul(PS[:, 1, :], ones[:], both, start=True, stop=True).then_inc(sel_used, 1)
            pe.matmul(PS[:, 3, 0:P], ident[:], ones[:], start=True, stop=True).then_inc(rank_mm, 1)
            def place(s, b, first):
                pe.wait_ge(sel_ready, s + 1)
                for k in range(2):
                    mm = pe.matmul(PS[:, 2, 0:2 * BLOCKS], hot_lo[:, b, k, :], hot_hi[:, b, k, :, :].rearrange("p a n -> p (a n)"),
                                   start=first and k == 0, stop=False, skip_group_check=True)
                return mm
            place(0, 0, True).then_inc(sel_used, 1)
            place(1, 1, False).then_inc(sel_used, 1)
            with pe.Fori(1, TT // 2) as i:
                for b in range(2):
                    place(2 * i + b, b, False).then_inc(sel_used, 1)
            pe.matmul(PS[:, 3, 0:P], ident[:], ones[:], start=True, stop=True).then_inc(table_mm, 1)

            pe.wait_ge(tables_ready, 1)

            def turn_rows(b, r, p, m):
                pe.wait_ge(xg_loaded[b], 16 * (r + 1))
                transposes(pe, p, [xg[:, b, c * P:(c + 1) * P] for c in range(KC)]).then_inc(xt_mm, 1)

            def hidden(n, p, e):
                pe.wait_ge(xgT_ready, n + 1)
                pe.wait_ge(experts_loaded, e * 32 + 32)
                for c in range(KC):
                    mm = pe.matmul(PS[:, 2 + p, :], xgT[:, p, c, :], w1_sb[:, bass.ds(e * (KC * H) + c * H, H)],
                                   start=c == 0, stop=c == KC - 1)
                mm.then_inc(h_mm, 1)

            expert = lambda n: pe.value_load(expert_of[0:1, bass.ds(n, 1)], min_val=0, max_val=E - 1)
            pe.transpose(PS[:, 4, 0:P], ident[:], ident[:]).then_inc(ht_mm, 1)
            turn_rows(0, 0, 0, 0)
            turn_rows(1, 0, 1, 1)
            hidden(0, 0, expert(0))
            with pe.Fori(0, BLOCKS // 4) as i:
                for u in range(4):
                    p = u % 2
                    n = i * 4 + u
                    e_next = expert(n + 1)
                    pe.wait_ge(gelu_done, n + 1)
                    transposes(pe, 4 + p, [hb[:, p, c * P:(c + 1) * P] for c in range(HC)]).then_inc(ht_mm, 1)
                    hidden(n + 1, 1 - p, e_next)
                    turn_rows((u + 2) % 4, i + (u + 2) // 4, p, n + 2)
                    e = expert(n)
                    pe.wait_ge(hT_ready, n + 1)
                    pe.wait_ge(y_copied, n + 1)
                    for c in range(HC):
                        mm = pe.matmul(PS[:, 6 + p, 0:D], hT[:, p, c, :], w2_sb[:, bass.ds(e * (HC * D) + c * D, D)],
                                       start=c == 0, stop=c == HC - 1)
                    mm.then_inc(y_mm, 1)

        @block.scalar
        def _(act):
            act.wait_ge(weights_loaded, 16 * 13)
            with act.Fori(0, B) as i:
                def bulk(n, dst, scale=1.0):
                    act.wait_ge(bulk_mm, i * BULK + n + 1)
                    act.activation(dst, PS[:, UNIT_BANK[n], :], ACT.Identity, scale=scale).then_inc(bulk_act, 1)

                def exponentials(u):
                    act.wait_ge(s_max, i * UNITS + u + 1)
                    if u >= 2:
                        act.wait_ge(t_mm, i * UNITS + u - 1)
                    src = PS[:, s_banks(u):s_banks(u) + 2, :].rearrange("p b n -> p (b n)")
                    if u < 2 * NT:
                        if u == NT:
                            act.wait_ge(pr_used, i * UNITS + NT)
                        act.activation(Pm[:, u % 2, :], src, ACT.Exp, bias=neg_max[:, u % 2, 0:1],
                                       accum_out=row_sum[:, u % NT:u % NT + 1]).then_inc(s_exp, 1)
                    else:
                        for h in range(HEADS):
                            o = h * M
                            ins = act.activation(Pm[:, u % 2, o:o + M], src[:, o:o + M], ACT.Exp, bias=neg_max[:, u % 2, h:h + 1],
                                                 accum_out=head_sum[:, u % 2, h:h + 1])
                        ins.then_inc(s_exp, 1)

                def turned(u):
                    act.wait_ge(t_mm, i * UNITS + u + 1)
                    if u >= 2:
                        act.wait_ge(pv_mm, i * UNITS + u - 1)
                    if u < 2 * NT:
                        act.copy(PT[:, u % 2, :], PS[:, 2:4, :].rearrange("p b n -> p (b n)")).then_inc(t_act, 1)
                    else:
                        act.copy(PT[:, u % 2, 0:512], PS[:, 2, :]).then_inc(t_act, 1)

                bulk(1, xT[:, 1, 0:512])
                bulk(3, xT[:, 1, 512:1024])
                act.wait_ge(bulk_mm, i * BULK + 6)
                for k, dst in enumerate((thT, phT, gT)):
                    rows = slice(F * k, F * k + F)
                    ins = act.activation(dst[0:F, 512:1024], PS[rows, 5, :], ACT.Identity, bias=bias_col[rows, :])
                ins.then_inc(bulk_act, 1)
                exponentials(0)
                for s in range(NT):
                    if s + 1 < NT:
                        exponentials(s + 1)
                    turned(s)
                bulk(7, xT[:, 1, 0:512])
                bulk(9, qT[:, 1, 0:512], scale=HD ** -0.5)
                bulk(11, kT[:, 1, 0:512])
                bulk(13, xT[:, 1, 512:1024])
                bulk(15, qT[:, 1, 512:1024], scale=HD ** -0.5)
                bulk(17, kT[:, 1, 512:1024])
                bulk(19, v[:, 2:4, :].rearrange("p t d -> p (t d)"))
                exponentials(NT)
                bulk(21, v[:, 6:8, :].rearrange("p t d -> p (t d)"))
                for s in range(NT):
                    exponentials(NT + s + 1)
                    turned(NT + s)
                    for p, g, _pair in slot_pieces[s]:
                        if p == "scores":
                            act.wait_ge(pinv_in, i * NG + g + 1)
                            act.activation(RX[:, g, :, 1, :], RX[:, g, :, 1, :], ACT.Exp).then_inc(pinv_exp, 1)
                for s in range(NT):
                    if s + 1 < NT:
                        exponentials(2 * NT + s + 1)
                    turned(2 * NT + s)
                bulk(23, xT[:, 1, 0:512])
                bulk(25, xT[:, 1, 512:1024])
                act.wait_ge(gate_mm, 3 * i + 3)

            act.wait_ge(probs_in, 1)
            act.activation(probs, probs, ACT.Exp).then_inc(probs_exp, 1)
            act.wait_ge(h_mm, 1)
            act.activation(hb[:, 0, :], PS[:, 2, :], ACT.Gelu).then_inc(gelu_done, 1)
            with act.Fori(0, BLOCKS // 4) as i:
                for u in range(4):
                    n = i * 4 + u
                    act.wait_ge(h_mm, n + 2)
                    act.wait_ge(ht_mm, n + 1)
                    act.activation(hb[:, 1 - u % 2, :], PS[:, 3 - u % 2, :], ACT.Gelu).then_inc(gelu_done, 1)

        @block.vector
        def _(dve):
            dve.memset(arena[:, 10240:12288], 0.0)
            dve_chain0.link(dve, dve.memset(arena[:, 27648:29696], 0.0))
            dve.memset(small[:, 0:1], 0.0).then_inc(padded, 1)
            for n in range(4):
                dve.wait_ge(prep_mm, n + 1)
                for r in (2 * n, 2 * n + 1):
                    src = PS[:, n, (r % 2) * D:(r % 2 + 1) * D].rearrange("p (c m) -> p c m", c=KC)
                    dst = wT_qkv[:, :, r * P:(r + 1) * P] if r < 6 else wT_out1[:, :, (r - 6) * P:(r - 5) * P]
                    cp = dve.tensor_copy(dst, src)
                cp.then_inc(prep_copied, 1)
            dve.wait_ge(weights_loaded, 16 * 13)

            with dve.Fori(0, B) as i:
                link = lambda ins: dve_steps.link(dve, ins, i)

                def bulk(n, dst, scale=None):
                    dve.wait_ge(bulk_mm, i * BULK + n + 1)
                    src = PS[:, UNIT_BANK[n], :]
                    if scale is not None:
                        cp = dve.tensor_scalar(dst, src, scale, None, ALU.mult)
                    else:
                        cp = dve.tensor_copy(dst, src)
                    cp.then_inc(bulk_dve, 1)

                def maxima(u):
                    dve.wait_ge(s_mm, i * UNITS + u + 1)
                    if u >= 2:
                        dve.wait_ge(s_exp, i * UNITS + u - 1)
                    src = PS[:, s_banks(u):s_banks(u) + 2, :].rearrange("p b n -> p (b n)")
                    dst = neg_max[:, u % 2, 0:1]
                    if u >= 2 * NT:
                        src, dst = src.rearrange("p (h m) -> p h m", m=M), neg_max[:, u % 2, :]
                    dve.tensor_reduce(dst, src, AX.X, ALU.max, negate=True).then_inc(s_max, 1)

                def inverses(t):
                    u = 2 * NT + t
                    dve.wait_ge(s_exp, i * UNITS + u + 1)
                    link(dve.reciprocal(head_inv[:], head_sum[:, u % 2, :]))
                    if t >= 2:
                        dve.wait_ge(inv_mm, i * NT + t - 1)
                    dve.tensor_copy(inv_wide[:, t % 2, :].rearrange("p (h d) -> p h d", d=HD),
                                    head_inv[:].unsqueeze(2).broadcast_to([P, HEADS, HD])).then_inc(inv_ready, 1)

                def turned(t):
                    u = 2 * NT + t
                    dve.wait_ge(t_mm, i * UNITS + u + 1)
                    dve.wait_ge(pv_mm, i * UNITS + u - 1)
                    dve.tensor_copy(PT[:, u % 2, 512:1024], PS[:, 3, :]).then_inc(t_dve, 1)

                def out_t(u):
                    dve.wait_ge(pv_mm, i * UNITS + u + 1)
                    if u >= 2:
                        dve.wait_ge(pr_mm, i * UNITS + u - 1)
                    if u < 2 * NT:
                        dve.tensor_copy(OT[:, u % 2, 0:P], PS[:, 0, 0:P]).then_inc(ot_ready, 1)
                    else:
                        dve.wait_ge(inv_copied, i * NT + u - 2 * NT + 1)
                        dve.tensor_tensor(OT[:, u % 2, :], PS[:, 0, 256:512], inv_T[:, u % 2, :], ALU.mult).then_inc(ot_ready, 1)

                def moments(row, t, done):
                    link(dve.bn_stats(stats[:, 0:6], row))
                    apart(dve, "dve")
                    dve.bn_aggr(aggr[:, t, 0:2], stats[:, 0:6]).then_inc(done, 1)

                def norm(row, t):
                    return dve.tensor_scalar(xn[:, t, :], row, aggr[:, t, 0:1], aggr[:, t, 3:4], ALU.subtract, ALU.mult)

                def t2_row(t):
                    return t2_all[:, bass.ds(i * NT + t, 1), :].rearrange("p o d -> p (o d)")

                def norm0(t):
                    dve.wait_ge(dev_ready, i * NT + t + 1)
                    norm(x1[:, t, :], t).then_inc(xn_ready, 1)

                def norm1(t):
                    dve.wait_ge(dev2_ready, i * NT + t + 1)
                    norm(t2_row(t), t).then_inc(xn2_ready, 1)

                def rows0(t):
                    u = t
                    link(dve.reciprocal(row_inv[:, t:t + 1], row_sum[:, t:t + 1]))
                    dve.wait_ge(pr_mm, i * UNITS + u + 1)
                    dve.scalar_tensor_tensor(x1[:, t, :], PS[:, 1, 0:D], row_inv[:, t:t + 1], xb[:, t, :],
                                             ALU.mult, ALU.add).then_inc(pr_used, 1)
                    dve.wait_ge(pr_used, i * UNITS + u + 1)
                    moments(x1[:, t, :], t, x1_done)

                def rows1(t):
                    u = 2 * NT + t
                    dve.wait_ge(pr_mm, i * UNITS + u + 1)
                    dve.wait_ge(x1b_ready, i * NT + t + 1)
                    dve.tensor_tensor(t2_row(t), PS[:, 1, 0:D], x1[:, t, :], ALU.add).then_inc(pr_used, 1)
                    dve.wait_ge(pr_used, i * UNITS + u + 1)
                    apart(dve, "dve")
                    moments(t2_row(t), t, x2_done)

                bulk(0, xT[:, 0, 0:512])
                bulk(2, xT[:, 0, 512:1024])
                dve.wait_ge(bulk_mm, i * BULK + 5)
                for k, dst in enumerate((thT, phT, gT)):
                    rows = slice(F * k, F * k + F)
                    ins = dve.tensor_scalar(dst[0:F, 0:512], PS[rows, 4, :], bias_col[rows, :], None, ALU.add)
                ins.then_inc(bulk_dve, 1)
                for u in range(2):
                    maxima(u)
                dve.wait_ge(gt_mm, i + 1)
                dve.tensor_copy(misc[:, 0, :], PS[:, 0, 0:NT * F]).then_inc(g_ready, 1)
                dve.wait_ge(xb_ready, i + 1)
                for s in range(NT + 2):
                    if s + 2 < NT:
                        maxima(s + 2)
                    if 1 <= s <= NT:
                        out_t(s - 1)
                    if s >= 2:
                        rows0(s - 2)
                        if s == 3:
                            dve.wait_ge(xn_free, i + 1)
                        if s >= 3:
                            norm0(s - 3)
                    if s == NT - 1:
                        bulk(6, xT[:, 0, 0:512])
                    if s == NT:
                        bulk(8, qT[:, 0, 0:512], scale=HD ** -0.5)
                bulk(10, kT[:, 0, 0:512])
                norm0(NT - 1)

                bulk(12, xT[:, 0, 512:1024])
                dve.wait_ge(bulk_act, i * (BULK // 2) + 7)
                dve.wait_ge(bulk_dve, i * (BULK // 2) + 7)
                for c in range(KC):
                    ins = dve.tensor_reduce(xm[:, c, :], xT[:, c, :].rearrange("p (m r) -> p m r", r=RUN), AX.X, ALU.add)
                ins.then_inc(xm_ready, 1)
                bulk(14, qT[:, 0, 512:1024], scale=HD ** -0.5)
                bulk(16, kT[:, 0, 512:1024])
                dve.wait_ge(lm_mm, i + 1)
                for j in range(GH):
                    rows = slice(HD * j, HD * j + HD)
                    sums = PS[rows, 6, :].rearrange("p (a g m) -> p a g m", a=2, g=NG)
                    dve.tensor_scalar(ql_bd[rows, :, j * M:(j + 1) * M], sums[:, 0], HD ** -0.5 / RUN, None, ALU.mult)
                    dve.tensor_scalar(kl_bd[rows, :, j * M:(j + 1) * M], sums[:, 1], 1.0 / RUN, None, ALU.mult)
                dve.tensor_scalar(q_lm.rearrange("p g m -> p (g m)"), PS[:, 6, 0:NG * M], HD ** -0.5 / RUN, None, ALU.mult).then_inc(lm_ready, 1)
                bulk(18, v[:, 0:2, :].rearrange("p t d -> p (t d)"))
                for u in range(2):
                    maxima(NT + u)
                bulk(20, v[:, 4:6, :].rearrange("p t d -> p (t d)"))

                scale_c = small[:, 8:16]

                def inverse_piece(p, g, pair):
                    k = piece_no[(p, g, pair)]
                    dve.wait_ge(pinv_mm, i * n_pieces + k)
                    heads = lambda ap: ap.rearrange("p (h m) -> p h m", m=M)
                    spread = lambda ap: ap.unsqueeze(2).broadcast_to([P, GH, M])
                    done = lambda ins: ins.then_inc(pinv_ev, 1)
                    A, bank = RX[:, g, :, 1, :], PS[:, 1, :]
                    if p == "scores":
                        link(dve.tensor_reduce(small[:, 16:20], heads(bank), AX.X, ALU.max, negate=True))
                        dve.tensor_tensor(A, heads(bank), spread(small[:, 16:20]), ALU.add).then_inc(pinv_in, 1)
                        dve.wait_ge(pinv_exp, i * NG + g + 1)
                        link(dve.tensor_reduce(small[:, 20:24], A, AX.X, ALU.add))
                        link(dve.reciprocal(small[:, 24:28], small[:, 20:24]))
                        done(dve.tensor_tensor(A, A, spread(small[:, 24:28]), ALU.mult))
                    elif p == "transpose":
                        done(dve.tensor_copy(AT[:, g, :], bank))
                    elif p == "norm 1":
                        done(dve.tensor_reduce(small[:, 28 + 4 * g:32 + 4 * g], heads(bank), AX.X, ALU.max))
                    elif p == "norm inf":
                        link(dve.tensor_reduce(small[:, 36:40], heads(bank), AX.X, ALU.max))
                        link(dve.tensor_tensor(small[:, 40:44], small[:, 28 + 4 * g:32 + 4 * g], small[:, 36:40], ALU.mult))
                        link(dve.reciprocal(scale_c[:, g * GH:(g + 1) * GH], small[:, 40:44]))
                        done(dve.tensor_scalar(small[:, 48 + 4 * g:52 + 4 * g], scale_c[:, g * GH:(g + 1) * GH], -1.0, None, ALU.mult))
                    elif p == "start":
                        for h in range(GH):
                            ins = dve.scalar_tensor_tensor(RX[:, g, h, 0, :], bank[:, h * M:(h + 1) * M],
                                                           small[:, 48 + 4 * g + h:49 + 4 * g + h], ident[:], ALU.mult, ALU.add)
                        done(ins)
                    elif p < PINV_ITERS - 1:
                        src = bank.rearrange("p (h r m) -> p h r m", r=2, m=M)
                        mine = RX[:, g, 2 * pair:2 * pair + 2]
                        dve.tensor_copy(mine[:, :, 0, :], src[:, :, 0, :])
                        done(dve.tensor_tensor(mine[:, :, 1, :], src[:, :, 1, :], mine[:, :, 1, :], ALU.add))
                    else:
                        done(dve.tensor_tensor(A, heads(bank), A, ALU.add))

                for s in range(NT + 2):
                    if s >= 2:
                        h = s - 2
                        link(dve.reciprocal(row_inv[:, h:h + 1], row_sum[:, h:h + 1]))
                        dve.wait_ge(pr_mm, i * UNITS + NT + h + 1)
                        dve.tensor_scalar(W_sb[:, h, :], PS[:, 0, 256:256 + HD], row_inv[:, h:h + 1], None, ALU.mult).then_inc(pr_used, 1)
                    mine = slot_pieces.get(s, [])
                    for piece in mine[0:3]:
                        inverse_piece(*piece)
                    if 1 <= s <= NT:
                        out_t(NT + s - 1)
                    if s < NT:
                        maxima(NT + s + 2)
                    for piece in mine[3:]:
                        inverse_piece(*piece)
                for s in range(NT + 2):
                    if s < NT:
                        inverses(s)
                    if s == 0:
                        dve.wait_ge(y_head_mm, i + 1)
                        dve.tensor_tensor(Y_sb, PS[:, 1, 0:D].rearrange("p (h d) -> p h d", d=HD),
                                          scale_c.unsqueeze(2).broadcast_to([P, HEADS, HD]), ALU.mult).then_inc(y_head_ready, 1)
                    if s < NT:
                        turned(s)
                        u = 2 * NT + s
                        dve.wait_ge(inv_mm, i * NT + s + 1)
                        dve.tensor_copy(inv_T[:, s % 2, :], PS[:, 0, 0:D]).then_inc(inv_copied, 1)
                    if 1 <= s <= NT:
                        out_t(2 * NT + s - 1)
                    if s + 2 < NT:
                        maxima(2 * NT + s + 2)
                    if s >= 2:
                        rows1(s - 2)
                        if s >= 3:
                            norm1(s - 3)
                    if s == NT - 1:
                        bulk(22, xT[:, 0, 0:512])
                norm1(NT - 1)
                bulk(24, xT[:, 0, 512:1024])
                dve.wait_ge(gate_mm, 3 * i + 2)
                dve.tensor_copy(gT[0:E, :], PS[0:E, 2:4, :].rearrange("p b n -> p (b n)")).then_inc(gate_ready, 1)
                dve.wait_ge(gate_mm, 3 * i + 3)
                link(dve.tensor_copy(logits[:, bass.ds(i * NT, NT), :].rearrange("p t e -> p (t e)"), PS[:, 7, 0:NT * E]))
                dve.memset(small[:, 4:5], 0.0).then_inc(sample_done, 1)
                dve_steps.close()

            link = lambda ins: dve_chain2.link(dve, ins)
            spread = lambda ap, n: ap.unsqueeze(2).broadcast_to([ap.shape[0], ap.shape[1], n])
            over_t = lambda ap: ap.unsqueeze(1).broadcast_to([P, TT, E])
            link(dve.tensor_reduce(pick[:, 0, :], logits[:], AX.X, ALU.max, negate=True))
            dve.tensor_tensor(probs, logits[:], spread(pick[:, 0, :], E), ALU.add).then_inc(probs_in, 1)
            dve.wait_ge(consts_ready, 2)
            link(dve.tensor_copy(iota_e[:], iota_i[:, 0:E]))
            dve.tensor_scalar(iota_blk[:], iota_i[:, 0:BW], float(P), None, ALU.mult)
            dve.tensor_copy(iota_lo[:], iota_i[:, 0:P])
            dve.tensor_copy(iota_hi[:], iota_i[:, 0:BLOCKS])
            dve.tensor_copy(tile_no[:], iota_i[:, 0:TT])
            for k in range(2):
                dve.tensor_scalar(row_no[:, k:k + 1], iota_i[:, 255:256], 2.0, float(k + 1), ALU.mult, ALU.add)
            dve.wait_ge(probs_exp, 1)
            link(dve.tensor_reduce(pos_lo[:, 0, :], probs, AX.X, ALU.add))
            link(dve.reciprocal(pos_lo[:, 1, :], pos_lo[:, 0, :]))
            link(dve.tensor_tensor(probs, probs, spread(pos_lo[:, 1, :], E), ALU.mult))
            for t in range(TT):
                ins = dve.max(out=top[:, t, :], in_=probs[:, t, :])
            link(ins)
            for t in range(TT):
                ins = dve.max_index(out=top_i[:, t, :], in_max=top[:, t, :], in_values=probs[:, t, :])
            link(ins)
            for k in range(2):
                ins = dve.tensor_copy(pick[:, k, :], top_i[:, :, k])
            link(ins)
            for k in range(2):
                ins = dve.tensor_tensor(oh[:, k], over_t(iota_e[:]), spread(pick[:, k, :], E), ALU.is_equal)
            link(ins)
            flat = lambda ap: ap.rearrange("p t e -> p (t e)")
            dve.tensor_tensor(route[:, 0, :], flat(oh[:, 0]), flat(oh[:, 1]), ALU.add).then_inc(hot_ready, 1)
            dve.wait_ge(rank_mm, 1)
            total, run = probs.rearrange("p t e -> p (t e)"), route[:, 1, :]
            by_e = lambda ap: ap.rearrange("p (e t) -> p e t", e=E)
            link(dve.tensor_copy(by_e(total), PS[:, 1, :].rearrange("p (t e) -> p e t", e=E)))
            dve.memset(route[:, 0, :], 0.0)
            link(dve.memset(col_e[:, 5, :], 0.0))
            link(dve.tensor_tensor_scan(run, total, route[:, 0, :], 0.0, ALU.add, ALU.add))
            link(dve.tensor_tensor(total, run, total, ALU.subtract))
            first, last = by_e(total)[:, :, 0], by_e(run)[:, :, TT - 1]
            link(dve.tensor_tensor(col_e[:, 0, :], last, first, ALU.subtract))
            link(dve.tensor_scalar(col_ei[:], col_e[:, 0, :], float(P - 1), None, ALU.add))
            link(dve.tensor_scalar(col_ei[:], col_ei[:], 7, 7, ALU.logical_shift_right, ALU.logical_shift_left))
            link(dve.tensor_copy(col_e[:, 1, :], col_ei[:]))
            link(dve.tensor_tensor_scan(col_e[:, 2, :], col_e[:, 1, :], col_e[:, 5, :], 0.0, ALU.add, ALU.add))
            link(dve.tensor_tensor(col_e[:, 3, :], col_e[:, 2, :], col_e[:, 1, :], ALU.subtract))
            link(dve.tensor_tensor(col_e[:, 4, :], col_e[:, 3, :], first, ALU.subtract))
            link(dve.tensor_tensor(by_e(total), by_e(total), spread(col_e[:, 4, :], TT), ALU.add))
            link(dve.tensor_tensor(run.rearrange("p (t e) -> p t e", e=E), PS[:, 0, :].rearrange("p (t e) -> p t e", e=E),
                                   by_e(total).rearrange("p e t -> p t e"), ALU.add))
            for k in range(2):
                ins = dve.tensor_tensor(flat(oh[:, k]), flat(oh[:, k]), run, ALU.mult)
            link(ins)
            link(dve.tensor_reduce(pos[:].rearrange("p k t -> p (k t)"), oh.rearrange("p k t e -> p (k t) e"), AX.X, ALU.add))
            link(dve.tensor_copy(pos_i[:, 0], pos[:]))
            dve.tensor_scalar(pos_i[:, 1], pos_i[:, 0], P - 1, None, ALU.bitwise_and)
            link(dve.tensor_scalar(pos_i[:, 2], pos_i[:, 0], 7, None, ALU.logical_shift_right))
            dve.tensor_copy(pos_lo[:], pos_i[:, 1])
            link(dve.tensor_copy(pos_hi[:], pos_i[:, 2]))
            ends = probs.rearrange("p t e -> p (t e)")

            def select(s, t, b):
                dve.wait_ge(sel_used, s + 1)
                for k in range(2):
                    lo, hi = pos_lo[:, k, bass.ds(t, 1)], pos_hi[:, k, bass.ds(t, 1)]
                    dve.tensor_scalar(hot_lo[:, b, k, :], iota_lo[:], lo, None, ALU.is_equal)
                    dve.tensor_scalar(hot_hi[:, b, k, 0, :], iota_hi[:], hi, row_no[:, k:k + 1], ALU.is_equal, ALU.mult)
                    ins = dve.tensor_scalar(hot_hi[:, b, k, 1, :], iota_hi[:], hi, tile_no[:, bass.ds(t, 1)], ALU.is_equal, ALU.mult)
                ins.then_inc(sel_ready, 1)
            with dve.Fori(0, TT // 2) as i:
                for b in range(2):
                    select(2 * i + b, 2 * i + b, b)
            link(dve.memset(slot[:, 2, :], 0.0))
            for e in range(E):
                link(dve.scalar_tensor_tensor(slot[:, 2, :], iota_blk[:], col_e[:, 2, e:e + 1], slot[:, 2, :], ALU.is_ge, ALU.add))
            dve.tensor_scalar(expert_of[:], slot[:, 2, :], float(E - 1), None, ALU.min)
            link(dve.memset(slot[:, 0, :], 0.0))
            dve.wait_ge(table_mm, 1)
            link(dve.tensor_copy(slot[:, 1, 0:BLOCKS], PS[:, 2, 0:BLOCKS]))
            link(dve.scalar_tensor_tensor(slot[:, 0, 0:BLOCKS], PS[:, 2, BLOCKS:2 * BLOCKS], 256.0, slot[:, 1, 0:BLOCKS], ALU.mult, ALU.add))
            link(dve.tensor_scalar(slot[:, 1, :], slot[:, 0, :], 0.0, float(4 * SLOT_ROWS), ALU.is_equal, ALU.mult))
            dve.scalar_tensor_tensor(row_of[:], slot[:, 0, :], -1.0, slot[:, 1, :], ALU.add, ALU.add)
            link(dve.tensor_scalar(slot_i[:], slot[:, 0, :], -1.0, 0.0, ALU.add, ALU.max))
            link(dve.tensor_scalar(token_of[:], slot_i[:], 1, None, ALU.logical_shift_right))
            for u in range(2):
                dve.memset(small[:, 44 + u:45 + u], 0.0).then_inc(y_copied, 1)
            dve.memset(small[:, 46:47], 0.0).then_inc(tables_ready, 1)

            def rows_turned(n, p):
                dve.wait_ge(xt_mm, n + 1)
                dve.tensor_copy(xgT[:, p].rearrange("p c n -> p (c n)"), PS[:, p, 0:D]).then_inc(xgT_ready, 1)
            rows_turned(0, 0)
            rows_turned(1, 1)

            def expert_copies(i, u, again):
                n, p = i * 4 + u, u % 2
                dve.wait_ge(ht_mm, n + 2)
                dve.tensor_copy(hT[:, p].rearrange("p c n -> p (c n)"), PS[:, 4 + p, :]).then_inc(hT_ready, 1)
                dve.wait_ge(h_mm, n + 1)
                rows_turned(n + 2, p)
                dve.wait_ge(y_mm, n + 1)
                if again:
                    dve.wait_ge(y_stored[u], i * 16)
                dve.tensor_copy(y_sb[:, u, :], PS[:, 6 + p, 0:D]).then_inc(y_copied, 1)

            for u in range(4):
                expert_copies(0, u, False)
            with dve.Fori(1, BLOCKS // 4) as i:
                for u in range(4):
                    expert_copies(i, u, True)
            for c in range(8):
                dve.wait_ge(y_back[c], 16)
                for k in range(2):
                    for t in range(4):
                        tt = 4 * c + t
                        ins = dve.scalar_tensor_tensor(t2_all[:, tt, :], y_in[:, c, t, k, :], top[:, tt, k:k + 1], t2_all[:, tt, :],
                                                       ALU.mult, ALU.add)
                    if k == 0:
                        link(ins)
                ins.then_inc(rows_ready, 1)


_INS = ['x', 'L0_conv_W_theta', 'L0_conv_b_theta', 'L0_conv_W_phi', 'L0_conv_b_phi', 'L0_conv_W_g', 'L0_conv_b_g',
        'L0_conv_W_out', 'L0_conv_b_out', 'L1_attn_w_qkv', 'L1_attn_w_out', 'L1_attn_b_out', 'L1_ffn_W_gate',
        'L1_ffn_W1', 'L1_ffn_W2']
_OUTS = [((4, 32, 32, 256), 'float32')]


def kernel(**inputs):
    import numpy as _np
    import concourse.bacc as _bacc
    from concourse import mybir as _mybir
    from concourse.bass_utils import run_bass_kernel_spmd as _run

    nc = _bacc.Bacc("TRN2", target_bir_lowering=False, num_devices=1)
    arrays, args = {}, []
    for name in _INS:
        a = _np.ascontiguousarray(inputs[name])
        arrays[f"in_{name}_dram"] = a
        args.append(nc.dram_tensor(f"in_{name}_dram", a.shape, _mybir.dt.from_np(a.dtype), kind="ExternalInput").ap())
    for i, (shape, dtype) in enumerate(_OUTS):
        dt = _mybir.dt.from_np(_np.dtype(dtype))
        args.append(nc.dram_tensor(f"out_{i}_dram", shape, dt, kind="ExternalOutput").ap())
    conv_attn_nystrom_moe_kernel(nc, *args)
    r = _run(nc, [arrays], core_ids=[0])
    return r.results[0]["out_0_dram"]
```

```python
from contextlib import ExitStack

import concourse.bass as bass
from concourse import mybir

P = 128
ALU = mybir.AluOpType
ACT = mybir.ActivationFunctionType
AX = mybir.AxisListType
F32 = mybir.dt.float32
BF16 = mybir.dt.bfloat16
F32R = mybir.dt.float32r
I32 = mybir.dt.int32
U32 = mybir.dt.uint32

HEADS = 8
PINV_ITERS = 6
EPS_LN = 1e-5
HIGH_BITS = -4096
QUADS = 4


class Chain:

    def __init__(self, sem, per_pass=0):
        self.sem, self.per_pass, self.n = sem, per_pass, 0

    def link(self, eng, ins, i=None):
        self.n += 1
        ins.then_inc(self.sem, 1)
        eng.wait_ge(self.sem, self.n if i is None else i * self.per_pass + self.n)

    def close(self):
        assert self.n == self.per_pass, ("steps of a pass", self.n)
        self.n = 0


def conv_attn_nystrom_moe_kernel(
    nc, x, w_theta, b_theta, w_phi, b_phi, w_g, b_g, w_out0, b_out0, w_qkv, w_out1, b_out1, w_gate, w1, w2, out,
):
    B, HH, WW, D = x.shape
    N = HH * WW
    T = B * N
    NT = N // P
    TT = T // P
    KC = D // P
    F = w_theta.shape[1]
    HD = D // HEADS
    M = P
    RUN = N // M
    GH = P // HD
    NG = HEADS // GH
    E, _, H = w1.shape
    HC = H // P
    BLOCKS = 2 * T // P + E - 1
    COLS = BLOCKS + 1
    ROUNDS = BLOCKS // 4
    LAST = range(4 * ROUNDS, BLOCKS)
    NO_ROW = 4 * T
    HALF = N // 2
    assert F == HD == 32 and GH == NG * 2 == QUADS and HALF == 512 and NT == 8 and KC == 2

    x_rows = x.rearrange("b h w d -> (b h w) d")
    x_dram = x_rows.rearrange("(t p) d -> p t d", p=P)
    out_rows = out.rearrange("b h w d -> (b h w) d")
    rows_dram = nc.dram_tensor("rows_scratch", (T, D + 2), F32, kind="Internal").ap()

    with ExitStack() as ctx:
        def sb(name, shape, dt=F32):
            return ctx.enter_context(nc.sbuf_tensor(name, shape, dt))

        def sem(name):
            return ctx.enter_context(nc.semaphore(name))

        PS = ctx.enter_context(nc.psum_tensor("PS", [P, 8, 512], F32))

        ident = sb("ident", [P, P])
        stacked_ident = sb("stacked_ident", [P, HD])
        ones = sb("ones", [P, P])
        lower = sb("lower", [P, P])
        low = sb("low", [P, 5632])
        wT_qkv = low[:, 0:1536].rearrange("p (c n) -> p c n", c=KC)
        wT_out1 = low[:, 1536:2048].rearrange("p (c n) -> p c n", c=KC)
        w_tpg = low[:, 2048:2240].rearrange("p (c n) -> p c n", c=KC)
        xm = low[:, 2304:2560].rearrange("p (c m) -> p c m", c=KC)
        wo0_sb = low[:, 2560:2816]
        bias_col = sb("bias_col", [P, 1])
        bo0 = low[:, 2816:3072]
        bo1 = low[:, 3072:3328]
        wgate_sb = sb("wgate_sb", [P, KC, E])
        t2 = sb("t2", [P, NT, D])
        logits = sb("logits", [P, TT, E])

        arena = sb("arena", [P, 32 * 1024])
        xs = arena[:, 0:2048].rearrange("p (t d) -> p t d", d=D)
        xb = arena[:, 2048:4096].rearrange("p (t d) -> p t d", d=D)
        x1 = arena[:, 4096:6144].rearrange("p (t d) -> p t d", d=D)
        xn = arena[:, 6144:8192].rearrange("p (t d) -> p t d", d=D)
        xT = arena[:, 8192:10240].rearrange("p (c n) -> p c n", c=KC)
        theta_parts = sb("theta_parts", [P, N], F32R)
        phi_parts = sb("phi_parts", [P, N], F32R)
        uppers = arena[:, 10240:11264]
        tpgT = arena[:, 12288:13312]
        Pm = arena[:, 13312:15360].rearrange("p (b n) -> p b n", b=2)
        PT = arena[:, 15360:17408].rearrange("p (b n) -> p b n", b=2)
        qT = arena[:, 17408:19456].rearrange("p (c n) -> p c n", c=KC)
        kT = arena[:, 19456:21504].rearrange("p (c n) -> p c n", c=KC)
        x0T = arena[:, 30720:32768].rearrange("p (c n) -> p c n", c=KC)
        gateT = arena[:, 25600:26624]
        v = arena[:, 21504:23552].rearrange("p (t d) -> p t d", d=D)
        RX = arena[:, 23552:25600].rearrange("p (g h r m) -> p g h r m", g=NG, h=GH, r=2)
        AT = arena[:, 26624:27648].rearrange("p (g n) -> p g n", g=NG)
        kl_bd = arena[:, 27648:28672].rearrange("p (g n) -> p g n", g=NG)
        ql_bd = arena[:, 28672:29696].rearrange("p (g n) -> p g n", g=NG)
        misc = low[:, 3328:4352].rearrange("p (a n) -> p a n", a=4)
        g_sb = misc[:, 0, :].rearrange("p (t f) -> p t f", f=F)
        W_sb = misc[:, 1, :].rearrange("p (h d) -> p h d", d=HD)
        Y_sb = misc[:, 3, :].rearrange("p (h d) -> p h d", d=HD)
        q_lm = low[:, 4608:4864].rearrange("p (g m) -> p g m", g=NG)
        OT = low[:, 4864:5376].rearrange("p (b n) -> p b n", b=2)
        inv_T = arena[:, 30208:30720].rearrange("p (b d) -> p b d", b=2)
        head_sum = sb("head_sum", [P, 2, HEADS])
        head_inv = sb("head_inv", [P, 2, HEADS])
        neg_max = sb("neg_max", [P, 2, NT])
        row_sum = sb("row_sum", [P, NT])
        row_inv = sb("row_inv", [P, NT])
        small = sb("small", [P, 64])
        stats = sb("stats", [P, 8])
        minus_half = sb("minus_half", [P, 1])
        aggr = sb("aggr", [P, NT, 4])

        BW = COLS
        iota_i = sb("iota_i", [P, 256], I32)
        iota_e = sb("iota_e", [P, E])
        iota_blk = sb("iota_blk", [P, BW])
        iota_lo = sb("iota_lo", [P, P], BF16)
        iota_hi = sb("iota_hi", [P, COLS], BF16)
        row_no = sb("row_no", [P, 2])
        tile_no = sb("tile_no", [P, TT, 2], BF16)
        zero_col = sb("zero_col", [P, 1])
        lower_h = sb("lower_h", [P, P], BF16)
        ones_h = sb("ones_h", [P, P], BF16)
        top = sb("top", [P, TT, 8])
        top_i = sb("top_i", [P, TT, 8], U32)
        pick = sb("pick", [P, TT, 2])
        gates = sb("gates", [P, TT, 2])
        prob_sum = sb("prob_sum", [P, 2, TT])
        pos = sb("pos", [P, TT * 2])
        pos_i = sb("pos_i", [P, 3, TT * 2], I32)
        pos_lo = sb("pos_lo", [P, TT * 2], BF16)
        pos_hi = sb("pos_hi", [P, TT * 2], BF16)
        col_e = sb("col_e", [P, 6, E])
        col_ei = sb("col_ei", [P, E], I32)
        total = low[:, 0:512]
        run = low[:, 512:1024]
        ended = low[:, 0:BW * E].rearrange("p (n e) -> p n e", e=E)
        oh = low[:, 1024:1536].bitcast(BF16).rearrange("p (t k e) -> p t k e", k=2, e=E)
        both = low[:, 1536:1792].bitcast(BF16)
        weighed = low[:, 1536:2560].rearrange("p (t k e) -> p t k e", k=2, e=E)
        probs = low[:, 2560:3072].rearrange("p (t e) -> p t e", e=E)
        ST = 4
        hot_lo = low[:, 2560:3584].bitcast(BF16).rearrange("p (b j n) -> p b j n", b=2, j=2 * ST)
        hot_hi = low[:, 3584:4224].bitcast(BF16).rearrange("p (b j n) -> p b j n", b=2, j=2 * ST)
        hot_val = low[:, 4224:5504].bitcast(BF16).rearrange("p (b a j n) -> p b a j n", b=2, a=2, j=2 * ST)
        slot = sb("slot", [P, 4, BW])
        slot_i = sb("slot_i", [P, BW], I32)
        pick_i = sb("pick_i", [P, BW], I32)
        token_of = sb("token_of", [P, BW], I32)
        row_of = sb("row_of", [P, BW], I32)
        expert_of = sb("expert_of", [P, BW], I32)
        w1_sb = arena[:, 0:E * KC * H]
        w2_sb = arena[:, E * KC * H:E * (KC * H + HC * D)]
        gather_ix = sb("gather_ix", [P, 4], I32)
        scatter_ix = sb("scatter_ix", [P, 4], I32)
        xg = low[:, 0:4 * (D + 2)].rearrange("p (b d) -> p b d", b=4)
        xgT = low[:, 1040:1552].rearrange("p (b c n) -> p b c n", b=2, c=KC)
        hb = low[:, 1552:2576].rearrange("p (b n) -> p b n", b=2)
        hT = low[:, 2576:3600].rearrange("p (b c n) -> p b c n", b=2, c=HC)
        y_sb = low[:, 3600:4624].rearrange("p (b d) -> p b d", b=4)
        pick_of = sb("pick_of", [P, BW, 2])
        gate_parts = sb("gate_parts", [P, 4, 2])
        slot_gate = sb("slot_gate", [P, 4])

        consts_ready = sem("consts_ready")
        tpg_loaded = sem("tpg_loaded")
        weights_loaded = sem("weights_loaded")
        raw_w_loaded = sem("raw_w_loaded")
        prep_mm = sem("prep_mm")
        prep_copied = sem("prep_copied")
        padded = sem("padded")
        pool_chain = Chain(sem("pool_chain"))
        dve_chain0 = Chain(sem("dve_chain0"))
        dve_steps = Chain(sem("dve_steps"), 45)
        dve_chain2 = Chain(sem("dve_chain2"))
        x_loaded = sem("x_loaded")
        xb_ready = sem("xb_ready")
        x1b_ready = sem("x1b_ready")
        x1_done = sem("x1_done")
        bulk_mm = sem("bulk_mm")
        bulk_dve = sem("bulk_dve")
        bulk_act = sem("bulk_act")
        tpg_mm = sem("tpg_mm")
        tpg_ready = sem("tpg_ready")
        uppers_ready = sem("uppers_ready")
        parts_dve = sem("parts_dve")
        parts_act = sem("parts_act")
        gt_mm = sem("gt_mm")
        g_ready = sem("g_ready")
        s_mm = sem("s_mm")
        s_max = sem("s_max")
        s_exp = sem("s_exp")
        t_mm = sem("t_mm")
        t_act = sem("t_act")
        t_dve = sem("t_dve")
        pv_mm = sem("pv_mm")
        ot_ready = sem("ot_ready")
        pr_mm = sem("pr_mm")
        pr_used = sem("pr_used")
        lm_ready = sem("lm_ready")
        pinv_mm = sem("pinv_mm")
        pinv_ev = sem("pinv_ev")
        pinv_in = sem("pinv_in")
        pinv_exp = sem("pinv_exp")
        xm_ready = sem("xm_ready")
        lm_mm = sem("lm_mm")
        inv_ready = sem("inv_ready")
        inv_mm = sem("inv_mm")
        inv_copied = sem("inv_copied")
        y_head_mm = sem("y_head_mm")
        y_head_ready = sem("y_head_ready")
        gate_mm = sem("gate_mm")
        gate_ready = sem("gate_ready")
        xn_ready = sem("xn_ready")
        x2_done = sem("x2_done")
        xn_free = sem("xn_free")
        dev_ready = sem("dev_ready")
        dev2_ready = sem("dev2_ready")
        xn2_ready = sem("xn2_ready")
        xn2_stored = sem("xn2_stored")
        sample_done = sem("sample_done")

        probs_in = sem("probs_in")
        probs_exp = sem("probs_exp")
        hot_ready = sem("hot_ready")
        rank_mm = sem("rank_mm")
        hi_ready = sem("hi_ready")
        rows_scaled = sem("rows_scaled")
        tiles_scaled = sem("tiles_scaled")
        tokens_ready = sem("tokens_ready")
        sel_ready = sem("sel_ready")
        sel_used = sem("sel_used")
        tables_ready = sem("tables_ready")
        expert_dma = [sem(f"expert_dma{k}") for k in range(2)]
        experts_loaded = sem("experts_loaded")
        gix = sem("gix")
        six = sem("six")
        xg_loaded = [sem(f"xg_loaded{u}") for u in range(4)]
        y_stored = [sem(f"y_stored{u}") for u in range(4)]
        xt_mm = sem("xt_mm")
        xgT_ready = sem("xgT_ready")
        h_mm = sem("h_mm")
        gelu_done = sem("gelu_done")
        ht_mm = sem("ht_mm")
        hT_ready = sem("hT_ready")
        y_mm = sem("y_mm")
        y_copied = sem("y_copied")
        gate_chain = Chain(sem("gate_chain"), 8)
        gates_made = sem("gates_made")
        gates_stored = sem("gates_stored")
        out_stored = sem("out_stored")

        block = ctx.enter_context(nc.Block())

        def ahead(i, u, k):
            return not isinstance(i, int) or 4 * i + u + k < BLOCKS

        pieces = [(p, g, None) for p in ("scores", "transpose", "norm 1", "norm inf", "start") for g in range(NG)]
        pieces += [(k, g, pair) for k in range(PINV_ITERS - 1) for g in range(NG) for pair in range(2)]
        pieces += [(PINV_ITERS - 1, g, None) for g in range(NG)]
        n_pieces = len(pieces)
        assert n_pieces == 4 * NT
        slot_pieces = {h: pieces[NG + 4 * h:NG + 4 * h + 4] for h in range(NT)}
        PIECE_BANK = {n + 1: (7, 1)[n] if n < NG else (1, 6)[n % 2] for n in range(n_pieces)}
        piece_no = {pg: n + 1 for n, pg in enumerate(pieces)}
        BULK = 24
        FIRST = 4
        UNIT_BANK = dict(enumerate([6, 7, 4, 5, 2, 3, 6, 7, 0, 1, 4, 5, 2, 3, 0, 1, 4, 5, 6, 7, 4, 5, 4, 5]))
        UNIT_BANK.update({-4: 4, -3: 5, -2: 6, -1: 7})
        UNIT_PREV = {6: 0, 7: 1, 10: 2, 11: 3, 12: 4, 13: 5, 14: 8, 15: 9, 20: 16, 21: 17, 22: 20, 23: 21}
        mm_count = lambda i, n: i * BULK + (FIRST + n + 1)
        dve_count = lambda i, n: i * (BULK // 2) + (FIRST // 2 + n // 2 + 1)
        act_count = lambda i, n: i * (BULK // 2) + (FIRST // 2 + (n + 1) // 2)
        UNITS = 3 * NT
        RAW = 13312

        def s_banks(u):
            return 4 if NT <= u < 2 * NT else (4, 6)[u % 2]

        passed = {e: sem(f"passed_{e}") for e in ("pool", "pe", "dve", "sp")}

        def apart(eng, name):
            eng.sem_inc(passed[name], 1)


        @block.gpsimd
        def _(pool):
            link = lambda ins: pool_chain.link(pool, ins)
            link(pool.memset(ident[:], 0.0))
            link(pool.affine_select(out=ident[:], in_=ident[:], compare_op=ALU.not_equal, fill=1.0, base=0,
                                    pattern=[[-1, P]], channel_multiplier=1))
            link(pool.memset(stacked_ident[:], 0.0))
            for j in range(QUADS):
                link(pool.affine_select(out=stacked_ident[:], in_=stacked_ident[:], compare_op=ALU.not_equal,
                                        fill=1.0, base=-HD * j, pattern=[[-1, HD]], channel_multiplier=1))
            link(pool.memset(lower[:], 1.0))
            link(pool.affine_select(out=lower[:], in_=lower[:], compare_op=ALU.is_gt, fill=0.0, base=0,
                                    pattern=[[1, P]], channel_multiplier=-1))
            pool.memset(ones[:], 1.0).then_inc(consts_ready, 1)
            link(pool.memset(minus_half[:], -0.5))
            link(pool.iota(iota_i[:, 0:255], pattern=[[1, 255]], base=0, channel_multiplier=0))
            pool.iota(iota_i[:, 255:256], pattern=[[1, 1]], base=0, channel_multiplier=1).then_inc(consts_ready, 1)
            pool.wait_ge(weights_loaded, 16 * 7)
            pool.sem_inc(xn_free, 1)
            pool_steps = Chain(sem("pool_steps"), 2 * NT)

            def deviation(t, i):
                pool_steps.link(pool, pool.tensor_scalar(aggr[:, t, 2:3], aggr[:, t, 1:2], EPS_LN, None, ALU.add), i)
                return pool.tensor_tensor(aggr[:, t, 3:4], aggr[:, t, 2:3], minus_half[:], ALU.pow)

            def add_bias(j):
                pool.wait_ge(x_loaded, (j + 1) * 16)
                pool.tensor_tensor(xb, xs, bo0.unsqueeze(1).broadcast_to([P, NT, D]), ALU.add).then_inc(xb_ready, 1)

            add_bias(0)
            with pool.Fori(0, B) as i:
                for t in range(NT + 1):
                    if t < NT:
                        pool.wait_ge(x1_done, i * NT + t + 1)
                        apart(pool, "pool")
                        deviation(t, i).then_inc(dev_ready, 1)
                    if t >= 1:
                        pool.wait_ge(xn_ready, i * NT + t)
                        pool.tensor_tensor(x1[:, t - 1, :], x1[:, t - 1, :], bo1, ALU.add).then_inc(x1b_ready, 1)
                add_bias(i + 1)
                for t in range(NT):
                    pool.wait_ge(x2_done, i * NT + t + 1)
                    apart(pool, "pool")
                    deviation(t, i).then_inc(dev2_ready, 1)
                pool_steps.close()
                pool.wait_ge(xn2_ready, (i + 1) * NT)
                of_sample = lambda rows: rows.rearrange("(b t p) d -> b p t d", p=P, t=NT)[i]
                pool.dma_start(of_sample(rows_dram)[:, :, 0:D], xn).then_inc(xn2_stored, 16)
                pool.dma_start(of_sample(out_rows), t2[:]).then_inc(out_stored, 16)
                pool.wait_ge(xn2_stored, (i + 1) * 16)
                pool.wait_ge(out_stored, (i + 1) * 16)
                pool.sem_inc(xn_free, 1)

            def gather(n, b):
                pool.tensor_copy(gather_ix[:, b:b + 1], token_of[:, bass.ds(n, 1)]).then_inc(gix, 1)
                pool.wait_ge(gix, n + 1)
                apart(pool, "pool")
                pool.indirect_dma_start(xg[:, b, :], None, rows_dram,
                                        bass.IndirectOffsetOnAxis(ap=gather_ix[:, b:b + 1], axis=0)).then_inc(xg_loaded[b], 16)

            def add_rows(i, u, again):
                if ahead(i, u, 3):
                    pool.wait_ge(xt_mm, i * 4 + u + 1)
                    gather(i * 4 + u + 3, (u + 3) % 4)
                pool.tensor_copy(scatter_ix[:, u:u + 1], row_of[:, bass.ds(i * 4 + u, 1)]).then_inc(six, 1)
                pool.wait_ge(six, i * 4 + u + 1)
                pool.wait_ge(y_copied, i * 4 + u + 3)
                if u >= 1:
                    pool.wait_ge(y_stored[u - 1], (i + 1) * 16)
                elif again:
                    pool.wait_ge(y_stored[3], i * 16)
                apart(pool, "pool")
                pool.indirect_dma_start(out_rows, bass.IndirectOffsetOnAxis(ap=scatter_ix[:, u:u + 1], axis=0),
                                        y_sb[:, u, :], None, bounds_check=T - 1, oob_is_err=False,
                                        compute_op=ALU.add).then_inc(y_stored[u], 16)

            def scale_tiles(s, b, again):
                pool.wait_ge(hi_ready, s + 1)
                if again:
                    pool.wait_ge(sel_used, s - 1)
                apart(pool, "pool")
                tiles = tile_no[:].rearrange("p t k -> p (t k)")[:, bass.ds(s * (2 * ST), 2 * ST)]
                pool.tensor_tensor(hot_val[:, b, 1], hot_hi[:, b], tiles.unsqueeze(2).broadcast_to([P, 2 * ST, COLS]),
                                   ALU.mult).then_inc(tiles_scaled, 1)

            for b in range(2):
                scale_tiles(b, b, False)
            with pool.Fori(1, TT // ST // 2) as i:
                for b in range(2):
                    scale_tiles(2 * i + b, b, True)
            pool.wait_ge(tokens_ready, 1)
            pool.wait_ge(gates_stored, 16)
            for n in range(3):
                gather(n, n)
            pool.wait_ge(tables_ready, 1)
            for u in range(4):
                add_rows(0, u, False)
            with pool.Fori(1, ROUNDS) as i:
                for u in range(4):
                    add_rows(i, u, True)
            for u in range(len(LAST)):
                add_rows(ROUNDS, u, True)

        @block.sync
        def _(sp):
            load_x = lambda j: sp.dma_start(xs, x_dram.rearrange("p (b t) d -> b p t d", t=NT)[j]).then_inc(x_loaded, 16)
            load_x(0)
            c = lambda ap: ap.rearrange("(f o) -> f o", o=1)
            for k, (w, b) in enumerate(((w_theta, b_theta), (w_phi, b_phi), (w_g, b_g))):
                sp.dma_start(w_tpg[:, :, F * k:F * k + F], w.rearrange("(c p) f -> p c f", p=P)).then_inc(tpg_loaded, 16)
                sp.dma_start(bias_col[F * k:F * k + F, :], c(b)).then_inc(tpg_loaded, 16)
            sp.dma_start(arena[:, RAW:RAW + 6 * D].rearrange("p (r d) -> p r d", d=D),
                         w_qkv.rearrange("(r p) d -> p r d", p=P)).then_inc(raw_w_loaded, 16)
            sp.dma_start(arena[:, RAW + 6 * D:RAW + 8 * D].rearrange("p (r d) -> p r d", d=D),
                         w_out1.rearrange("(r p) d -> p r d", p=P)).then_inc(raw_w_loaded, 16)
            for dst, src in (
                *[(wo0_sb[F * j:F * j + F, :], w_out0) for j in range(QUADS)],
                (bo0, b_out0.partition_broadcast(P)), (bo1, b_out1.partition_broadcast(P)),
                (wgate_sb[:], w_gate.rearrange("(c p) e -> p c e", p=P)),
            ):
                sp.dma_start(dst, src).then_inc(weights_loaded, 16)
            with sp.Fori(0, B - 1) as i:
                sp.wait_ge(x_loaded, (i + 1) * 16)
                sp.wait_ge(bulk_mm, i * BULK + FIRST)
                sp.wait_ge(xb_ready, i + 1)
                apart(sp, "sp")
                load_x(i + 1)
            sp.wait_ge(x_loaded, B * 16)
            sp.sem_inc(x_loaded, 16)
            sp.wait_ge(sample_done, B)
            sp.wait_ge(xn2_stored, 16 * B)
            def weights_in(e):
                sp.wait_ge(expert_dma[e % len(expert_dma)], 32 * (e // len(expert_dma) + 1))
                sp.sem_inc(experts_loaded, 1)

            for e in range(E):
                if e == 4:
                    sp.wait_ge(gates_made, 1)
                    sp.dma_start(rows_dram.rearrange("(t p) d -> p t d", p=P)[:, :, D:D + 2], gates[:]).then_inc(gates_stored, 16)
                loaded = expert_dma[e % len(expert_dma)]
                sp.dma_start(w1_sb.rearrange("p (e c h) -> p e c h", e=E, c=KC)[:, e],
                             w1.rearrange("e (c p) h -> p e c h", p=P)[:, e]).then_inc(loaded, 16)
                sp.dma_start(w2_sb.rearrange("p (e c d) -> p e c d", e=E, c=HC)[:, e],
                             w2.rearrange("e (c p) d -> p e c d", p=P)[:, e]).then_inc(loaded, 16)
                if e >= len(expert_dma) - 1:
                    weights_in(e - len(expert_dma) + 1)
            for e in range(E - len(expert_dma) + 1, E):
                weights_in(e)
            for u in range(4):
                sp.wait_ge(y_stored[u], 16 * (ROUNDS + (u < len(LAST))))

        def transposes(pe, dst_bank, srcs):
            for n, s in enumerate(srcs):
                mm = pe.transpose(PS[0:s.shape[1], dst_bank, n * P:n * P + s.shape[0]], s, ident[0:s.shape[0], 0:s.shape[0]])
            return mm

        @block.tensor
        def _(pe):
            pe.wait_ge(consts_ready, 1)
            i = 0

            def bulk_free(n):
                if n in UNIT_PREV:
                    last = UNIT_PREV[n]
                    pe.wait_ge(bulk_act if last % 2 else bulk_dve, (act_count if last % 2 else dve_count)(i, last))

            def bulk_done(n):
                pe.wait_ge(bulk_dve, dve_count(i, n))
                pe.wait_ge(bulk_act, act_count(i, n))

            def turn(n, src, half):
                for c in range(KC):
                    bulk_free(n + c)
                    srcs = [src[:, 4 * half + t, c * P:(c + 1) * P] for t in range(4)]
                    transposes(pe, UNIT_BANK[n + c], srcs).then_inc(bulk_mm, 1)

            def project(bank, w, m, half, src):
                for c in range(KC):
                    mm = pe.matmul(PS[0:m, bank, :], w[c], src[:, c, half * 512:half * 512 + 512],
                                   start=c == 0, stop=c == KC - 1)
                return mm

            def project_tpg(half):
                project(6 + half, [w_tpg[:, c, :] for c in range(KC)], 3 * F, half, x0T).then_inc(tpg_mm, 1)

            def turn_g(j):
                pe.wait_ge(tpg_ready, j * 2 + 2)
                apart(pe, "pe")
                for t in range(NT):
                    mm = pe.transpose(PS[:, 0, t * F:(t + 1) * F], tpgT[2 * F:3 * F, t * P:(t + 1) * P], ident[2 * F:3 * F, 2 * F:3 * F])
                mm.then_inc(gt_mm, 1)

            def parts_ready(j):
                pe.wait_ge(parts_dve, j * 2 + 2)
                pe.wait_ge(parts_act, j * 2 + 2)

            def scores(u, k):
                b = s_banks(u)
                if k == 0 and u == 2 * NT + 1:
                    pe.wait_ge(pinv_ev, (i + 1) * n_pieces)
                elif k == 0 and NT < u <= 2 * NT:
                    pe.wait_ge(s_exp, i * UNITS + u)
                elif k == 0 and u >= 2:
                    pe.wait_ge(s_exp, i * UNITS + u - 1)
                if u < NT:
                    ops = theta_parts[:, u * P:(u + 1) * P], phi_parts[:, k * 512:(k + 1) * 512]
                elif u < 2 * NT:
                    h = u - NT
                    ops = (ql_bd[:, h // GH, (h % GH) * M:(h % GH + 1) * M],
                           kT[:, h // GH, k * 512:(k + 1) * 512])
                else:
                    t = u - 2 * NT
                    ops = qT[:, k, t * P:(t + 1) * P], kl_bd[:, k, :]
                mm = pe.matmul(PS[:, b + k, :], ops[0], ops[1], start=True, stop=True)
                if k == 1:
                    mm.then_inc(s_mm, 1)

            pe.wait_ge(x_loaded, 16)
            turn(-4, xs, 0)
            turn(-2, xs, 1)
            bulk_done(-1)
            pe.wait_ge(tpg_loaded, 16 * 6)
            for half in range(2):
                project_tpg(half)
            pe.wait_ge(raw_w_loaded, 32)
            raw = arena[:, RAW:RAW + 8 * D].rearrange("p (r d) -> p r d", d=D)
            for n in range(4):
                srcs = [raw[:, r, c * P:(c + 1) * P] for r in (2 * n, 2 * n + 1) for c in range(KC)]
                transposes(pe, n, srcs).then_inc(prep_mm, 1)
            pe.wait_ge(padded, 1)
            parts_ready(0)
            for k in range(2):
                scores(0, k)
            pe.wait_ge(prep_copied, 4)
            turn_g(0)
            pe.wait_ge(weights_loaded, 16 * 7)

            with pe.Fori(0, B) as i:
                def copied(u):
                    pe.wait_ge(t_act, i * UNITS + u + 1)
                    if u >= 2 * NT:
                        pe.wait_ge(t_dve, i * NT + u - 2 * NT + 1)

                def turn_probs(u, k):
                    if k == 0:
                        pe.wait_ge(s_exp, i * UNITS + u + 1)
                        if u >= 1:
                            copied(u - 1)
                    mm = transposes(pe, 2 + k, [Pm[:, u % 2, (4 * k + n) * P:(4 * k + n + 1) * P] for n in range(4)])
                    if k == 1:
                        mm.then_inc(t_mm, 1)

                def turn_inverses(t):
                    pe.wait_ge(inv_ready, i * NT + t + 1)
                    if t == 0:
                        pe.wait_ge(pr_used, i * UNITS + 2 * NT)
                    if t >= 2:
                        pe.wait_ge(ot_ready, i * UNITS + 2 * NT + t - 1)
                    for g in range(NG):
                        for j in range(QUADS):
                            h = g * GH + j
                            mm = pe.matmul(PS[HD * j:HD * j + HD, 0, g * P:(g + 1) * P], head_inv[:, t % 2, h:h + 1].broadcast_to([P, HD]),
                                           ident[:], start=True, stop=True, tile_position=(0, HD * j))
                    mm.then_inc(inv_mm, 1)

                def values(u):
                    copied(u)
                    if u >= 1:
                        pe.wait_ge(ot_ready, i * UNITS + u)
                    if u >= NT and u < 2 * NT and u - NT >= 1:
                        pe.wait_ge(pr_used, i * UNITS + u)
                    if u >= 2 * NT:
                        pe.wait_ge(inv_copied, i * NT + min(u - 2 * NT + 2, NT))
                    pt = lambda n: PT[:, u % 2, n * P:(n + 1) * P]
                    if u < 2 * NT:
                        for r in range(2):
                            for j in range(QUADS):
                                n = 2 * j + r
                                vals = g_sb[:, n, :] if u < NT else v[:, n, (u - NT) * HD:(u - NT + 1) * HD]
                                mm = pe.matmul(PS[HD * j:HD * j + HD, 0, 0:P], vals, pt(n), start=r == 0, stop=r == 1,
                                               tile_position=(0, HD * j))
                    else:
                        for g in range(NG):
                            for j in range(QUADS):
                                mm = pe.matmul(PS[HD * j:HD * j + HD, 0, 256 + g * P:256 + (g + 1) * P], Y_sb[:, g * GH + j, :],
                                               pt(g * GH + j), start=True, stop=True, tile_position=(0, HD * j))
                    mm.then_inc(pv_mm, 1)

                def finish(u):
                    pe.wait_ge(ot_ready, i * UNITS + u + 1)
                    if u >= 1:
                        pe.wait_ge(pr_used, i * UNITS + u)
                    if u < NT:
                        mm = pe.matmul(PS[:, 1, 0:D], OT[:, u % 2, 0:P], wo0_sb, start=True, stop=True)
                    elif u < 2 * NT:
                        mm = pe.matmul(PS[:, 0, 256:256 + HD], OT[:, u % 2, 0:P], stacked_ident[:], start=True, stop=True)
                    else:
                        for c in range(KC):
                            mm = pe.matmul(PS[:, 1, 0:D], OT[:, u % 2, c * P:(c + 1) * P], wT_out1[:, c, :],
                                           start=c == 0, stop=c == KC - 1)
                    mm.then_inc(pr_mm, 1)

                def qk(n, r, half):
                    bulk_free(n)
                    project(UNIT_BANK[n], [wT_qkv[:, c, r * P:(r + 1) * P] for c in range(KC)], P, half, xT).then_inc(bulk_mm, 1)

                for k in range(2):
                    scores(1, k)
                pe.wait_ge(g_ready, i + 1)
                for s in range(NT + 2):
                    for k in range(2):
                        if s < NT:
                            turn_probs(s, k)
                    for k in range(2):
                        if s + 2 < NT:
                            scores(s + 2, k)
                    if 1 <= s <= NT:
                        values(s - 1)
                    if s >= 2:
                        finish(s - 2)
                    if s == NT - 1:
                        pe.wait_ge(xn_ready, i * NT + NT // 2)
                        turn(0, xn, 0)
                    if s == NT:
                        bulk_done(1)
                        for r in range(2):
                            qk(2 + r, r, 0)

                copied(NT - 1)
                for r in range(2, 2 * KC):
                    qk(2 + r, r, 0)
                pe.wait_ge(xn_ready, (i + 1) * NT)
                turn(6, xn, 1)
                bulk_done(7)
                pe.wait_ge(ot_ready, i * UNITS + NT)
                for r in range(2 * KC):
                    qk(8 + r, r, 1)
                pe.wait_ge(xm_ready, i + 1)
                for r in range(2 * KC):
                    for c in range(KC):
                        mm = pe.matmul(PS[:, 6, r * M:(r + 1) * M], wT_qkv[:, c, r * P:(r + 1) * P], xm[:, c, :],
                                       start=c == 0, stop=c == KC - 1)
                mm.then_inc(lm_mm, 1)

                def value_rows(n):
                    bulk_free(n)
                    for t2 in range(2):
                        t = 2 * (n - 12) + t2
                        for c in range(KC):
                            mm = pe.matmul(PS[:, UNIT_BANK[n], t2 * D:(t2 + 1) * D], xT[:, c, t * P:(t + 1) * P],
                                           wT_qkv[:, c, 2 * D:3 * D], start=c == 0, stop=c == KC - 1)
                    mm.then_inc(bulk_mm, 1)

                value_rows(12)
                value_rows(13)
                bulk_done(11)
                pe.wait_ge(lm_ready, i + 1)
                for g in range(NG):
                    pe.matmul(PS[:, PIECE_BANK[g + 1], :], q_lm[:, g, :], kl_bd[:, g, :], start=True, stop=True).then_inc(pinv_mm, 1)
                for k in range(2):
                    scores(NT, k)
                value_rows(14)
                pe.wait_ge(pinv_in, i * NG + 2)
                value_rows(15)
                bulk_done(13)

                def inverse_piece(p, g, pair):
                    k = piece_no[(p, g, pair)]
                    pe.wait_ge(pinv_ev, i * n_pieces + k - 2)
                    bank = PS[:, PIECE_BANK[k], :]
                    if p == "transpose":
                        mm = transposes(pe, PIECE_BANK[k], [RX[:, g, h, 1, :] for h in range(GH)])
                    elif p == "norm 1":
                        mm = pe.matmul(bank, ones[:], RX[:, g, :, 1, :], start=True, stop=True)
                    elif p == "norm inf":
                        mm = pe.matmul(bank, ones[:], AT[:, g, :], start=True, stop=True)
                    elif p == "start":
                        for h in range(GH):
                            at = AT[:, g, h * M:(h + 1) * M]
                            mm = pe.matmul(bank[:, h * M:(h + 1) * M], at, at, start=True, stop=True)
                    elif p < PINV_ITERS - 1:
                        for h in (2 * pair, 2 * pair + 1):
                            o = (h % 2) * 2 * M
                            mm = pe.matmul(bank[:, o:o + 2 * M], RX[:, g, h, 0, :], RX[:, g, h].rearrange("p r m -> p (r m)"),
                                           start=True, stop=True)
                    else:
                        for h in range(GH):
                            mm = pe.matmul(bank[:, h * M:(h + 1) * M], RX[:, g, h, 0, :], RX[:, g, h, 1, :], start=True, stop=True)
                    mm.then_inc(pinv_mm, 1)

                for s in range(NT + 1):
                    mine = slot_pieces.get(s, [])
                    if s >= 2:
                        finish(NT + s - 2)
                    for k in range(2):
                        if s < NT:
                            turn_probs(NT + s, k)
                    if s == 0:
                        bulk_done(15)
                    for k in range(2):
                        if s < NT:
                            scores(NT + s + 1, k)
                        for piece in mine[k:k + 1]:
                            inverse_piece(*piece)
                    if 1 <= s <= NT:
                        values(NT + s - 1)
                    for piece in mine[2:]:
                        inverse_piece(*piece)
                def head_values(hs):
                    pe.wait_ge(pr_used, i * UNITS + NT + hs[-1] + 1)
                    for h in hs:
                        mm = pe.matmul(PS[:, 1, h * HD:(h + 1) * HD], RX[:, h // GH, h % GH, 1, :], W_sb[:, h, :],
                                       start=True, stop=True)
                    return mm
                for k in range(2):
                    scores(2 * NT + 1, k)
                finish(2 * NT - 1)
                head_values(range(HEADS - 2))
                for s in range(NT + 2):
                    if s < NT:
                        turn_inverses(s)
                        for k in range(2):
                            turn_probs(2 * NT + s, k)
                    if s == 0:
                        head_values(range(HEADS - 2, HEADS)).then_inc(y_head_mm, 1)
                    for k in range(2):
                        if s + 2 < NT:
                            scores(2 * NT + s + 2, k)
                    if s == 0:
                        pe.wait_ge(y_head_ready, i + 1)
                    if 1 <= s <= NT:
                        values(2 * NT + s - 1)
                    if s >= 2:
                        finish(2 * NT + s - 2)
                    if s == NT - 2:
                        pe.wait_ge(x_loaded, (i + 2) * 16)
                        turn(16, xs, 0)
                    if s == NT - 1:
                        pe.wait_ge(xn2_ready, i * NT + NT // 2)
                        turn(18, xn, 0)
                        turn(20, xs, 1)
                    if s == NT:
                        bulk_done(21)
                        project_tpg(0)
                    if s == NT + 1:
                        project_tpg(1)

                def gate(half):
                    for c in range(KC):
                        mm = pe.matmul(PS[0:E, 2 + half, :], wgate_sb[:, c, :], xT[:, c, half * 512:half * 512 + 512],
                                       start=c == 0, stop=c == KC - 1)
                    mm.then_inc(gate_mm, 1)

                gate(0)
                pe.wait_ge(xn2_ready, (i + 1) * NT)
                turn(22, xn, 1)
                turn_g(i + 1)
                bulk_done(23)
                gate(1)
                parts_ready(i + 1)
                for k in range(2):
                    scores(0, k)
                pe.wait_ge(gate_ready, i * 2 + 2)
                apart(pe, "pe")
                for t in range(NT):
                    mm = pe.transpose(PS[:, 1, t * E:(t + 1) * E], gateT[0:E, t * P:(t + 1) * P], ident[0:E, 0:E])
                mm.then_inc(gate_mm, 1)

            pe.wait_ge(hot_ready, 1)
            pe.matmul(PS[:, 0, :], lower_h[:], both, start=True, stop=True)
            pe.matmul(PS[:, 1, :], ones_h[:], both, start=True, stop=True).then_inc(rank_mm, 1)

            def place(s, b, first=False):
                pe.wait_ge(sel_ready, s + 1)
                pe.wait_ge(rows_scaled, s + 1)
                pe.wait_ge(tiles_scaled, s + 1)
                for j in range(2 * ST):
                    mm = pe.matmul(PS[:, 2, 0:2 * COLS], hot_lo[:, b, j, :], hot_val[:, b, :, j, :],
                                   start=first and j == 0, stop=False, skip_group_check=True)
                mm.then_inc(sel_used, 1)

            for b in range(2):
                place(b, b, first=b == 0)
            with pe.Fori(1, TT // ST // 2) as i:
                for b in range(2):
                    place(2 * i + b, b)

            pe.wait_ge(tables_ready, 1)

            def turn_rows(b, r, p, m):
                pe.wait_ge(xg_loaded[b], 16 * (r + 1))
                transposes(pe, p, [xg[:, b, c * P:(c + 1) * P] for c in range(KC)]).then_inc(xt_mm, 1)

            def hidden(n, p, e):
                pe.wait_ge(xgT_ready, n + 1)
                pe.wait_ge(experts_loaded, e + 1)
                for c in range(KC):
                    mm = pe.matmul(PS[:, 2 + p, :], xgT[:, p, c, :], w1_sb[:, bass.ds(e * (KC * H) + c * H, H)],
                                   start=c == 0, stop=c == KC - 1)
                mm.then_inc(h_mm, 1)

            expert = lambda n: pe.value_load(expert_of[0:1, bass.ds(n, 1)], min_val=0, max_val=E - 1)
            pe.transpose(PS[:, 4, 0:P], ident[:], ident[:]).then_inc(ht_mm, 1)
            turn_rows(0, 0, 0, 0)
            turn_rows(1, 0, 1, 1)
            hidden(0, 0, expert(0))

            def expert_block(i, u):
                p = u % 2
                n = i * 4 + u
                if ahead(i, u, 1):
                    e_next = expert(n + 1)
                pe.wait_ge(gelu_done, n + 1)
                transposes(pe, 4 + p, [hb[:, p, c * P:(c + 1) * P] for c in range(HC)]).then_inc(ht_mm, 1)
                if ahead(i, u, 1):
                    hidden(n + 1, 1 - p, e_next)
                if ahead(i, u, 2):
                    turn_rows((u + 2) % 4, i + (u + 2) // 4, p, n + 2)
                e = expert(n)
                pe.wait_ge(hT_ready, n + 1)
                pe.wait_ge(y_copied, n + 1)
                for c in range(HC):
                    mm = pe.matmul(PS[:, 6 + p, 0:D], hT[:, p, c, :], w2_sb[:, bass.ds(e * (HC * D) + c * D, D)],
                                   start=c == 0, stop=c == HC - 1)
                mm.then_inc(y_mm, 1)

            with pe.Fori(0, ROUNDS) as i:
                for u in range(4):
                    expert_block(i, u)
            for u in range(len(LAST)):
                expert_block(ROUNDS, u)

        @block.scalar
        def _(act):
            act.wait_ge(padded, 1)
            act.wait_ge(tpg_loaded, 16 * 6)
            i = 0

            def bulk(n, dst, scale=1.0):
                act.wait_ge(bulk_mm, mm_count(i, n))
                act.activation(dst, PS[:, UNIT_BANK[n], :], ACT.Identity, scale=scale).then_inc(bulk_act, 1)

            def tpg_out(j, half):
                act.wait_ge(tpg_mm, j * 2 + half + 1)
                act.activation(tpgT[0:3 * F, half * 512:half * 512 + 512], PS[0:3 * F, 6 + half, :], ACT.Identity,
                               bias=bias_col[0:3 * F, :]).then_inc(tpg_ready, 1)

            def parts(j, half):
                cols = slice(half * 512, half * 512 + 512)
                act.wait_ge(uppers_ready, j * 2 + half + 1)
                act.copy(theta_parts[0:F, cols], uppers[0:F, cols])
                act.copy(theta_parts[F:2 * F, cols], uppers[0:F, cols])
                act.copy(phi_parts[0:F, cols], uppers[F:2 * F, cols])
                act.copy(phi_parts[2 * F:3 * F, cols], uppers[F:2 * F, cols]).then_inc(parts_act, 1)

            bulk(-3, x0T[:, 1, 0:512])
            bulk(-1, x0T[:, 1, 512:1024])
            for half in range(2):
                tpg_out(0, half)
            for half in range(2):
                parts(0, half)

            with act.Fori(0, B) as i:
                def exponentials(u):
                    act.wait_ge(s_max, i * UNITS + u + 1)
                    if u >= 2:
                        act.wait_ge(t_mm, i * UNITS + u - 1)
                    src = PS[:, s_banks(u):s_banks(u) + 2, :].rearrange("p b n -> p (b n)")
                    if u < 2 * NT:
                        if u == NT:
                            act.wait_ge(pr_used, i * UNITS + NT)
                        act.activation(Pm[:, u % 2, :], src, ACT.Exp, bias=neg_max[:, u % 2, 0:1],
                                       accum_out=row_sum[:, u % NT:u % NT + 1]).then_inc(s_exp, 1)
                    else:
                        for h in range(HEADS):
                            o = h * M
                            ins = act.activation(Pm[:, u % 2, o:o + M], src[:, o:o + M], ACT.Exp, bias=neg_max[:, u % 2, h:h + 1],
                                                 accum_out=head_sum[:, u % 2, h:h + 1])
                        ins.then_inc(s_exp, 1)

                def turned(u):
                    act.wait_ge(t_mm, i * UNITS + u + 1)
                    if u >= 2:
                        act.wait_ge(pv_mm, i * UNITS + u - 1)
                    if u < 2 * NT:
                        act.copy(PT[:, u % 2, :], PS[:, 2:4, :].rearrange("p b n -> p (b n)")).then_inc(t_act, 1)
                    else:
                        act.copy(PT[:, u % 2, 0:512], PS[:, 2, :]).then_inc(t_act, 1)

                exponentials(0)
                for s in range(NT):
                    if s + 1 < NT:
                        exponentials(s + 1)
                    turned(s)
                bulk(1, xT[:, 1, 0:512])
                bulk(3, qT[:, 1, 0:512], scale=HD ** -0.5)
                bulk(5, kT[:, 1, 0:512])
                bulk(7, xT[:, 1, 512:1024])
                bulk(9, qT[:, 1, 512:1024], scale=HD ** -0.5)
                bulk(11, kT[:, 1, 512:1024])
                for g in range(NG):
                    act.wait_ge(pinv_in, i * NG + g + 1)
                    act.activation(RX[:, g, :, 1, :], RX[:, g, :, 1, :], ACT.Exp).then_inc(pinv_exp, 1)
                bulk(13, v[:, 2:4, :].rearrange("p t d -> p (t d)"))
                exponentials(NT)
                bulk(15, v[:, 6:8, :].rearrange("p t d -> p (t d)"))
                for s in range(NT):
                    turned(NT + s)
                    exponentials(NT + s + 1)
                for s in range(NT):
                    if s + 1 < NT:
                        exponentials(2 * NT + s + 1)
                    turned(2 * NT + s)
                    if s == NT - 1:
                        bulk(17, x0T[:, 1, 0:512])
                bulk(19, xT[:, 1, 0:512])
                bulk(21, x0T[:, 1, 512:1024])
                for half in range(2):
                    tpg_out(i + 1, half)
                parts(i + 1, 0)
                act.wait_ge(gate_mm, 3 * i + 1)
                act.activation(gateT[0:E, 0:512], PS[0:E, 2, :], ACT.Identity).then_inc(gate_ready, 1)
                bulk(23, xT[:, 1, 512:1024])
                parts(i + 1, 1)

            act.wait_ge(probs_in, 1)
            act.activation(probs, probs, ACT.Exp)
            act.activation(gates[:], gates[:], ACT.Exp).then_inc(probs_exp, 1)

            def scale_rows(s, b, again):
                act.wait_ge(hi_ready, s + 1)
                if again:
                    act.wait_ge(sel_used, s - 1)
                for k in range(2):
                    ins = act.activation(hot_val[:, b, 0, k::2, :], hot_hi[:, b, k::2, :], ACT.Copy, scale=row_no[:, k:k + 1])
                ins.then_inc(rows_scaled, 1)

            for b in range(2):
                scale_rows(b, b, False)
            with act.Fori(1, TT // ST // 2) as i:
                for b in range(2):
                    scale_rows(2 * i + b, b, True)
            act.wait_ge(h_mm, 1)
            act.activation(hb[:, 0, :], PS[:, 2, :], ACT.Gelu).then_inc(gelu_done, 1)

            def next_gelu(i, u):
                if ahead(i, u, 1):
                    n = i * 4 + u
                    act.wait_ge(h_mm, n + 2)
                    act.wait_ge(ht_mm, n + 1)
                    act.activation(hb[:, 1 - u % 2, :], PS[:, 3 - u % 2, :], ACT.Gelu).then_inc(gelu_done, 1)

            with act.Fori(0, ROUNDS) as i:
                for u in range(4):
                    next_gelu(i, u)
            for u in range(len(LAST)):
                next_gelu(ROUNDS, u)

        @block.vector
        def _(dve):
            dve_chain0.link(dve, dve.memset(arena[:, 27648:29696], 0.0))
            dve.memset(small[:, 0:1], 0.0).then_inc(padded, 1)
            dve.wait_ge(consts_ready, 2)
            dve.tensor_copy(iota_e[:], iota_i[:, 0:E])
            dve.tensor_scalar(iota_blk[:], iota_i[:, 0:BW], float(P), None, ALU.mult)
            dve.tensor_copy(iota_lo[:], iota_i[:, 0:P])
            dve.tensor_copy(iota_hi[:], iota_i[:, 0:COLS])
            dve.tensor_copy(tile_no[:], iota_i[:, 0:TT].unsqueeze(2).broadcast_to([P, TT, 2]))
            for k in range(2):
                dve.tensor_scalar(row_no[:, k:k + 1], iota_i[:, 255:256], 2.0, float(k + 1), ALU.mult, ALU.add)
            dve.memset(zero_col[:], 0.0)
            dve.tensor_copy(lower_h[:], lower[:])
            dve_chain0.link(dve, dve.tensor_copy(ones_h[:], ones[:]))

            i = 0

            def bulk(n, dst, scale=None):
                dve.wait_ge(bulk_mm, mm_count(i, n))
                src = PS[:, UNIT_BANK[n], :]
                if scale is not None:
                    cp = dve.tensor_scalar(dst, src, scale, None, ALU.mult)
                else:
                    cp = dve.tensor_copy(dst, src)
                cp.then_inc(bulk_dve, 1)

            def maxima(u, pass_no=None):
                dve.wait_ge(s_mm, (i if pass_no is None else pass_no) * UNITS + u + 1)
                if u >= 2:
                    dve.wait_ge(s_exp, i * UNITS + u - 1)
                src = PS[:, s_banks(u):s_banks(u) + 2, :].rearrange("p b n -> p (b n)")
                dst = neg_max[:, u % 2, 0:1]
                if u >= 2 * NT:
                    src, dst = src.rearrange("p (h m) -> p h m", m=M), neg_max[:, u % 2, :]
                dve.tensor_reduce(dst, src, AX.X, ALU.max, negate=True).then_inc(s_max, 1)

            def parts(j, half):
                cols = slice(half * 512, half * 512 + 512)
                dve.wait_ge(tpg_ready, j * 2 + half + 1)
                dve.tensor_scalar(uppers[0:2 * F, cols].bitcast(I32), tpgT[0:2 * F, cols].bitcast(I32), HIGH_BITS, None,
                                  ALU.bitwise_and).then_inc(uppers_ready, 1)
                dve.wait_ge(uppers_ready, j * 2 + half + 1)
                for dst, quarters, rows in ((theta_parts, (2, 3), slice(0, F)), (phi_parts, (1, 3), slice(F, 2 * F))):
                    for q in quarters:
                        ins = dve.tensor_tensor(dst[F * q:F * q + F, cols], tpgT[rows, cols], uppers[rows, cols], ALU.subtract)
                ins.then_inc(parts_dve, 1)

            def g_out(j):
                dve.wait_ge(gt_mm, j + 1)
                dve.tensor_copy(misc[:, 0, :], PS[:, 0, 0:NT * F]).then_inc(g_ready, 1)

            bulk(-4, x0T[:, 0, 0:512])
            bulk(-2, x0T[:, 0, 512:1024])
            for half in range(2):
                parts(0, half)
            maxima(0)
            for n in range(4):
                dve.wait_ge(prep_mm, n + 1)
                for r in (2 * n, 2 * n + 1):
                    src = PS[:, n, (r % 2) * D:(r % 2 + 1) * D].rearrange("p (c m) -> p c m", c=KC)
                    dst = wT_qkv[:, :, r * P:(r + 1) * P] if r < 6 else wT_out1[:, :, (r - 6) * P:(r - 5) * P]
                    cp = dve.tensor_copy(dst, src)
                cp.then_inc(prep_copied, 1)
            g_out(0)
            with dve.Fori(0, B) as i:
                link = lambda ins: dve_steps.link(dve, ins, i)

                def inverses(t):
                    u = 2 * NT + t
                    dve.wait_ge(s_exp, i * UNITS + u + 1)
                    if t >= 2:
                        dve.wait_ge(inv_mm, i * NT + t - 1)
                    dve.reciprocal(head_inv[:, t % 2, :], head_sum[:, u % 2, :]).then_inc(inv_ready, 1)

                def turned(t):
                    u = 2 * NT + t
                    dve.wait_ge(t_mm, i * UNITS + u + 1)
                    dve.wait_ge(pv_mm, i * UNITS + u - 1)
                    dve.tensor_copy(PT[:, u % 2, 512:1024], PS[:, 3, :]).then_inc(t_dve, 1)

                def out_t(u):
                    dve.wait_ge(pv_mm, i * UNITS + u + 1)
                    if u >= 2:
                        dve.wait_ge(pr_mm, i * UNITS + u - 1)
                    if u < 2 * NT:
                        dve.tensor_copy(OT[:, u % 2, 0:P], PS[:, 0, 0:P]).then_inc(ot_ready, 1)
                    else:
                        dve.wait_ge(inv_copied, i * NT + u - 2 * NT + 1)
                        dve.tensor_tensor(OT[:, u % 2, :], PS[:, 0, 256:512], inv_T[:, u % 2, :], ALU.mult).then_inc(ot_ready, 1)

                def moments(row, t, done):
                    link(dve.bn_stats(stats[:, 0:6], row))
                    apart(dve, "dve")
                    dve.bn_aggr(aggr[:, t, 0:2], stats[:, 0:6]).then_inc(done, 1)

                def norm(row, t):
                    return dve.tensor_scalar(xn[:, t, :], row, aggr[:, t, 0:1], aggr[:, t, 3:4], ALU.subtract, ALU.mult)

                def t2_row(t):
                    return t2[:, t, :]

                def norm0(t):
                    dve.wait_ge(dev_ready, i * NT + t + 1)
                    norm(x1[:, t, :], t).then_inc(xn_ready, 1)

                def norm1(t):
                    dve.wait_ge(dev2_ready, i * NT + t + 1)
                    norm(t2_row(t), t).then_inc(xn2_ready, 1)

                def rows0(t):
                    u = t
                    link(dve.reciprocal(row_inv[:, t:t + 1], row_sum[:, t:t + 1]))
                    dve.wait_ge(pr_mm, i * UNITS + u + 1)
                    dve.scalar_tensor_tensor(x1[:, t, :], PS[:, 1, 0:D], row_inv[:, t:t + 1], xb[:, t, :],
                                             ALU.mult, ALU.add).then_inc(pr_used, 1)
                    dve.wait_ge(pr_used, i * UNITS + u + 1)
                    moments(x1[:, t, :], t, x1_done)

                def rows1(t):
                    u = 2 * NT + t
                    dve.wait_ge(pr_mm, i * UNITS + u + 1)
                    dve.wait_ge(x1b_ready, i * NT + t + 1)
                    dve.tensor_tensor(t2_row(t), PS[:, 1, 0:D], x1[:, t, :], ALU.add).then_inc(pr_used, 1)
                    dve.wait_ge(pr_used, i * UNITS + u + 1)
                    apart(dve, "dve")
                    moments(t2_row(t), t, x2_done)

                maxima(1)
                dve.wait_ge(xb_ready, i + 1)
                for s in range(NT + 2):
                    if s + 2 < NT:
                        maxima(s + 2)
                    if 1 <= s <= NT:
                        out_t(s - 1)
                    if s >= 2:
                        rows0(s - 2)
                        if s == 3:
                            dve.wait_ge(xn_free, i + 1)
                        if s >= 3:
                            norm0(s - 3)
                    if s == NT - 1:
                        bulk(0, xT[:, 0, 0:512])
                    if s == NT:
                        bulk(2, qT[:, 0, 0:512], scale=HD ** -0.5)
                bulk(4, kT[:, 0, 0:512])
                norm0(NT - 1)

                bulk(6, xT[:, 0, 512:1024])
                dve.wait_ge(bulk_act, act_count(i, 7))
                dve.wait_ge(bulk_dve, dve_count(i, 6))
                for c in range(KC):
                    ins = dve.tensor_reduce(xm[:, c, :], xT[:, c, :].rearrange("p (m r) -> p m r", r=RUN), AX.X, ALU.add)
                ins.then_inc(xm_ready, 1)
                bulk(8, qT[:, 0, 512:1024], scale=HD ** -0.5)
                bulk(10, kT[:, 0, 512:1024])
                dve.wait_ge(lm_mm, i + 1)
                for j in range(GH):
                    rows = slice(HD * j, HD * j + HD)
                    sums = PS[rows, 6, :].rearrange("p (a g m) -> p a g m", a=2, g=NG)
                    dve.tensor_scalar(ql_bd[rows, :, j * M:(j + 1) * M], sums[:, 0], HD ** -0.5 / RUN, None, ALU.mult)
                    dve.tensor_scalar(kl_bd[rows, :, j * M:(j + 1) * M], sums[:, 1], 1.0 / RUN, None, ALU.mult)
                dve.tensor_scalar(q_lm.rearrange("p g m -> p (g m)"), PS[:, 6, 0:NG * M], HD ** -0.5 / RUN, None, ALU.mult).then_inc(lm_ready, 1)
                scale_c = small[:, 8:16]
                heads = lambda ap: ap.rearrange("p (h m) -> p h m", m=M)
                spread = lambda ap: ap.unsqueeze(2).broadcast_to([P, GH, M])

                for g in range(NG):
                    bank = heads(PS[:, PIECE_BANK[g + 1], :])
                    dve.wait_ge(pinv_mm, i * n_pieces + g + 1)
                    link(dve.tensor_reduce(small[:, 16 + 4 * g:20 + 4 * g], bank, AX.X, ALU.max, negate=True))
                    dve.tensor_tensor(RX[:, g, :, 1, :], bank, spread(small[:, 16 + 4 * g:20 + 4 * g]), ALU.add).then_inc(pinv_in, 1)
                bulk(12, v[:, 0:2, :].rearrange("p t d -> p (t d)"))
                maxima(NT)
                for g in range(NG):
                    dve.wait_ge(pinv_exp, i * NG + g + 1)
                    link(dve.tensor_reduce(small[:, 56 + 4 * g:60 + 4 * g], RX[:, g, :, 1, :], AX.X, ALU.add))
                    link(dve.reciprocal(small[:, 24:28], small[:, 56 + 4 * g:60 + 4 * g]))
                    dve.tensor_tensor(RX[:, g, :, 1, :], RX[:, g, :, 1, :], spread(small[:, 24:28]), ALU.mult).then_inc(pinv_ev, 1)
                    if g == 0:
                        bulk(14, v[:, 4:6, :].rearrange("p t d -> p (t d)"))

                def inverse_piece(p, g, pair):
                    k = piece_no[(p, g, pair)]
                    dve.wait_ge(pinv_mm, i * n_pieces + k)
                    done = lambda ins: ins.then_inc(pinv_ev, 1)
                    A, bank = RX[:, g, :, 1, :], PS[:, PIECE_BANK[k], :]
                    if p == "transpose":
                        done(dve.tensor_copy(AT[:, g, :], bank))
                    elif p == "norm 1":
                        done(dve.tensor_reduce(small[:, 28 + 4 * g:32 + 4 * g], heads(bank), AX.X, ALU.max))
                    elif p == "norm inf":
                        link(dve.tensor_reduce(small[:, 36:40], heads(bank), AX.X, ALU.max))
                        link(dve.tensor_tensor(small[:, 40:44], small[:, 28 + 4 * g:32 + 4 * g], small[:, 36:40], ALU.mult))
                        link(dve.reciprocal(scale_c[:, g * GH:(g + 1) * GH], small[:, 40:44]))
                        done(dve.tensor_scalar(small[:, 48 + 4 * g:52 + 4 * g], scale_c[:, g * GH:(g + 1) * GH], -1.0, None, ALU.mult))
                    elif p == "start":
                        for h in range(GH):
                            ins = dve.scalar_tensor_tensor(RX[:, g, h, 0, :], bank[:, h * M:(h + 1) * M],
                                                           small[:, 48 + 4 * g + h:49 + 4 * g + h], ident[:], ALU.mult, ALU.add)
                        done(ins)
                    elif p < PINV_ITERS - 1:
                        src = bank.rearrange("p (h r m) -> p h r m", r=2, m=M)
                        mine = RX[:, g, 2 * pair:2 * pair + 2]
                        dve.tensor_copy(mine[:, :, 0, :], src[:, :, 0, :])
                        done(dve.tensor_tensor(mine[:, :, 1, :], src[:, :, 1, :], mine[:, :, 1, :], ALU.add))
                    else:
                        done(dve.tensor_tensor(A, heads(bank), A, ALU.add))

                for s in range(NT + 2):
                    if s == NT + 1:
                        inverses(0)
                        maxima(2 * NT + 1)
                    if s >= 2:
                        h = s - 2
                        link(dve.reciprocal(row_inv[:, h:h + 1], row_sum[:, h:h + 1]))
                        dve.wait_ge(pr_mm, i * UNITS + NT + h + 1)
                        dve.tensor_scalar(W_sb[:, h, :], PS[:, 0, 256:256 + HD], row_inv[:, h:h + 1], None, ALU.mult).then_inc(pr_used, 1)
                    mine = slot_pieces.get(s, [])
                    for piece in mine[0:1]:
                        inverse_piece(*piece)
                    if s < NT:
                        maxima(NT + s + 1)
                    for piece in mine[1:2]:
                        inverse_piece(*piece)
                    if 1 <= s <= NT:
                        out_t(NT + s - 1)
                    for piece in mine[2:]:
                        inverse_piece(*piece)
                for s in range(NT + 2):
                    if s < NT:
                        dve.wait_ge(inv_mm, i * NT + s + 1)
                        dve.tensor_copy(inv_T[:, s % 2, :], PS[:, 0, 0:D]).then_inc(inv_copied, 1)
                        turned(s)
                    if s == 0:
                        dve.wait_ge(y_head_mm, i + 1)
                        dve.tensor_tensor(Y_sb, PS[:, 1, 0:D].rearrange("p (h d) -> p h d", d=HD),
                                          scale_c.unsqueeze(2).broadcast_to([P, HEADS, HD]), ALU.mult).then_inc(y_head_ready, 1)
                    if s + 1 < NT:
                        inverses(s + 1)
                    if s == NT - 1:
                        bulk(16, x0T[:, 0, 0:512])
                    if s == NT:
                        bulk(18, xT[:, 0, 0:512])
                        bulk(20, x0T[:, 0, 512:1024])
                    if 1 <= s <= NT:
                        out_t(2 * NT + s - 1)
                    if s + 2 < NT:
                        maxima(2 * NT + s + 2)
                    if s >= 2:
                        rows1(s - 2)
                        if s >= 3:
                            norm1(s - 3)
                norm1(NT - 1)
                parts(i + 1, 0)
                bulk(22, xT[:, 0, 512:1024])
                parts(i + 1, 1)
                g_out(i + 1)
                dve.wait_ge(gate_mm, 3 * i + 2)
                dve.tensor_copy(gateT[0:E, 512:1024], PS[0:E, 3, :]).then_inc(gate_ready, 1)
                maxima(0, i + 1)
                dve.wait_ge(gate_mm, 3 * i + 3)
                link(dve.tensor_copy(logits[:, bass.ds(i * NT, NT), :].rearrange("p t e -> p (t e)"), PS[:, 1, 0:NT * E]))
                dve.memset(small[:, 4:5], 0.0).then_inc(sample_done, 1)
                dve_steps.close()

            link = lambda ins: dve_chain2.link(dve, ins)
            spread = lambda ap, n: ap.unsqueeze(2).broadcast_to([ap.shape[0], ap.shape[1], n])
            for t in range(TT):
                ins = dve.max(out=top[:, t, :], in_=logits[:, t, :])
            link(ins)
            dve.tensor_tensor(gates[:], top[:, :, 0:2], spread(top[:, :, 0], 2), ALU.subtract)
            dve.tensor_tensor(probs, logits[:], spread(top[:, :, 0], E), ALU.subtract).then_inc(probs_in, 1)
            for t in range(TT):
                ins = dve.max_index(out=top_i[:, t, :], in_max=top[:, t, :], in_values=logits[:, t, :])
            link(ins)
            link(dve.tensor_copy(pick[:], top_i[:, :, 0:2]))
            link(dve.tensor_tensor(oh.rearrange("p t k e -> p (t k) e"), iota_e[:].unsqueeze(1).broadcast_to([P, 2 * TT, E]),
                                   spread(pick[:].rearrange("p t k -> p (t k)"), E), ALU.is_equal))
            by_t = lambda ap: ap.rearrange("p (t e) -> p t e", e=E)
            dve.tensor_tensor(by_t(both), oh[:, :, 0, :], oh[:, :, 1, :], ALU.add).then_inc(hot_ready, 1)
            dve.wait_ge(probs_exp, 1)
            link(dve.tensor_reduce(prob_sum[:, 0, :], probs, AX.X, ALU.add))
            link(dve.reciprocal(prob_sum[:, 1, :], prob_sum[:, 0, :]))
            dve.tensor_tensor(gates[:], gates[:], spread(prob_sum[:, 1, :], 2), ALU.mult).then_inc(gates_made, 1)
            dve.wait_ge(rank_mm, 1)
            by_e = lambda ap: ap.rearrange("p (e t) -> p e t", e=E)
            counts = PS[:, 1, :].rearrange("p (t e) -> p e t", e=E)
            link(dve.tensor_copy(by_e(total), counts))
            link(dve.tensor_tensor_scan(run, total, zero_col[:].broadcast_to([P, TT * E]), 0.0, ALU.add, ALU.add))
            link(dve.tensor_tensor(total, run, total, ALU.subtract))
            first, last = by_e(total)[:, :, 0], by_e(run)[:, :, TT - 1]
            link(dve.tensor_tensor(col_e[:, 0, :], last, first, ALU.subtract))
            link(dve.tensor_scalar(col_ei[:], col_e[:, 0, :], float(P - 1), None, ALU.add))
            link(dve.tensor_scalar(col_ei[:], col_ei[:], 7, 7, ALU.logical_shift_right, ALU.logical_shift_left))
            link(dve.tensor_copy(col_e[:, 1, :], col_ei[:]))
            link(dve.tensor_tensor_scan(col_e[:, 2, :], col_e[:, 1, :], zero_col[:].broadcast_to([P, E]), 0.0, ALU.add, ALU.add))
            link(dve.tensor_tensor(col_e[:, 3, :], col_e[:, 2, :], col_e[:, 1, :], ALU.subtract))
            link(dve.tensor_tensor(col_e[:, 4, :], col_e[:, 3, :], first, ALU.subtract))
            link(dve.tensor_tensor(by_e(total), by_e(total), spread(col_e[:, 4, :], TT), ALU.add))
            link(dve.tensor_tensor(by_t(run), by_t(PS[:, 0, :]), by_e(total).rearrange("p e t -> p t e"), ALU.add))
            link(dve.tensor_tensor(weighed, oh, by_t(run).unsqueeze(2).broadcast_to([P, TT, 2, E]), ALU.mult))
            link(dve.tensor_reduce(pos[:], weighed.rearrange("p t k e -> p (t k) e"), AX.X, ALU.add))
            link(dve.tensor_copy(pos_i[:, 0], pos[:]))
            dve.tensor_scalar(pos_i[:, 1], pos_i[:, 0], P - 1, None, ALU.bitwise_and)
            link(dve.tensor_scalar(pos_i[:, 2], pos_i[:, 0], 7, None, ALU.logical_shift_right))
            dve.tensor_copy(pos_lo[:], pos_i[:, 1])
            link(dve.tensor_copy(pos_hi[:], pos_i[:, 2]))

            def select(s, b, again):
                mine = bass.ds(s * (2 * ST), 2 * ST)
                row_of_all = lambda ap, n: ap[:].unsqueeze(1).broadcast_to([P, 2 * ST, n])
                if again:
                    dve.wait_ge(rows_scaled, s - 1)
                    dve.wait_ge(tiles_scaled, s - 1)
                    dve.wait_ge(sel_used, s - 1)
                dve.tensor_tensor(hot_hi[:, b], row_of_all(iota_hi, COLS), spread(pos_hi[:, mine], COLS),
                                  ALU.is_equal).then_inc(hi_ready, 1)
                dve.tensor_tensor(hot_lo[:, b], row_of_all(iota_lo, P), spread(pos_lo[:, mine], P), ALU.is_equal).then_inc(sel_ready, 1)

            for b in range(2):
                select(b, b, False)
            with dve.Fori(1, TT // ST // 2) as i:
                for b in range(2):
                    select(2 * i + b, b, True)
            link(dve.tensor_tensor(ended, spread(iota_blk[:], E), col_e[:, 2, :].unsqueeze(1).broadcast_to([P, BW, E]), ALU.is_ge))
            dve.memset(slot[:, 0, :], 0.0)
            link(dve.tensor_reduce(slot[:, 2, :], ended, AX.X, ALU.add))
            dve.tensor_scalar(expert_of[:], slot[:, 2, :], float(E - 1), None, ALU.min)
            dve.wait_ge(sel_used, TT // ST)
            link(dve.tensor_copy(slot[:, 1, 0:COLS], PS[:, 2, 0:COLS]))
            link(dve.scalar_tensor_tensor(slot[:, 0, 0:COLS], PS[:, 2, COLS:2 * COLS], 256.0, slot[:, 1, 0:COLS], ALU.mult, ALU.add))
            dve.tensor_scalar(slot_i[:], slot[:, 0, :], -1.0, 0.0, ALU.add, ALU.max)
            link(dve.tensor_scalar(slot[:, 1, :], slot[:, 0, :], 0.0, float(NO_ROW), ALU.is_equal, ALU.mult))
            dve.tensor_scalar(token_of[:], slot_i[:], 1, None, ALU.logical_shift_right).then_inc(tokens_ready, 1)
            link(dve.tensor_scalar(pick_i[:], slot_i[:], 1, None, ALU.bitwise_and))
            link(dve.tensor_copy(slot[:, 3, :], token_of[:]))
            dve.tensor_tensor(row_of[:], slot[:, 3, :], slot[:, 1, :], ALU.add)
            link(dve.tensor_copy(pick_of[:, :, 1], pick_i[:]))
            link(dve.tensor_scalar(pick_of[:, :, 0], pick_of[:, :, 1], -1.0, 1.0, ALU.mult, ALU.add))
            for u in range(2):
                dve.memset(small[:, 44 + u:45 + u], 0.0).then_inc(y_copied, 1)
            dve.memset(small[:, 46:47], 0.0).then_inc(tables_ready, 1)

            def rows_turned(n, p, u, chain):
                dve.wait_ge(xt_mm, n + 1)
                chain(dve.tensor_tensor(gate_parts[:, u, :], xg[:, u, D:D + 2],
                                        pick_of[:, bass.ds(n, 1), :].rearrange("p o k -> p (o k)"), ALU.mult))
                chain(dve.tensor_tensor(slot_gate[:, u:u + 1], gate_parts[:, u, 0:1], gate_parts[:, u, 1:2], ALU.add))
                dve.tensor_copy(xgT[:, p].rearrange("p c n -> p (c n)"), PS[:, p, 0:D]).then_inc(xgT_ready, 1)
            rows_turned(0, 0, 0, link)
            rows_turned(1, 1, 1, link)

            def expert_copies(i, u, again):
                n, p = i * 4 + u, u % 2
                dve.wait_ge(ht_mm, n + 2)
                dve.tensor_copy(hT[:, p].rearrange("p c n -> p (c n)"), PS[:, 4 + p, :]).then_inc(hT_ready, 1)
                dve.wait_ge(h_mm, n + 1)
                if ahead(i, u, 2):
                    rows_turned(n + 2, p, (u + 2) % 4, lambda ins: gate_chain.link(dve, ins, i))
                dve.wait_ge(y_mm, n + 1)
                if again:
                    dve.wait_ge(y_stored[u], i * 16)
                dve.tensor_scalar(y_sb[:, u, :], PS[:, 6 + p, 0:D], slot_gate[:, u:u + 1], None, ALU.mult).then_inc(y_copied, 1)

            for u in range(4):
                expert_copies(0, u, False)
            gate_chain.close()
            with dve.Fori(1, ROUNDS) as i:
                for u in range(4):
                    expert_copies(i, u, True)
                gate_chain.close()
            for u in range(len(LAST)):
                expert_copies(ROUNDS, u, True)


_INS = ['x', 'L0_conv_W_theta', 'L0_conv_b_theta', 'L0_conv_W_phi', 'L0_conv_b_phi', 'L0_conv_W_g', 'L0_conv_b_g',
        'L0_conv_W_out', 'L0_conv_b_out', 'L1_attn_w_qkv', 'L1_attn_w_out', 'L1_attn_b_out', 'L1_ffn_W_gate',
        'L1_ffn_W1', 'L1_ffn_W2']
_OUTS = [((4, 32, 32, 256), 'float32')]


def kernel(**inputs):
    import numpy as _np
    import concourse.bacc as _bacc
    from concourse import mybir as _mybir
    from concourse.bass_utils import run_bass_kernel_spmd as _run

    nc = _bacc.Bacc("TRN2", target_bir_lowering=False, num_devices=1)
    arrays, args = {}, []
    for name in _INS:
        a = _np.ascontiguousarray(inputs[name])
        arrays[f"in_{name}_dram"] = a
        args.append(nc.dram_tensor(f"in_{name}_dram", a.shape, _mybir.dt.from_np(a.dtype), kind="ExternalInput").ap())
    for i, (shape, dtype) in enumerate(_OUTS):
        dt = _mybir.dt.from_np(_np.dtype(dtype))
        args.append(nc.dram_tensor(f"out_{i}_dram", shape, dt, kind="ExternalOutput").ap())
    conv_attn_nystrom_moe_kernel(nc, *args)
    r = _run(nc, [arrays], core_ids=[0])
    return r.results[0]["out_0_dram"]
```
